# Optimizing a Trainium2 kernel written in Bass

```python
import numpy as np
import jax
import jax.numpy as jnp

def _softmax(x, axis=-1):
    return jax.nn.softmax(x, axis=axis)

def _gelu(x):
    return jax.nn.gelu(x, approximate=True)

def _silu(x):
    return jax.nn.silu(x)

def _sigmoid(x):
    return jax.nn.sigmoid(x)

def _layernorm(x, axis=-1, eps=1e-05):
    m = jnp.mean(x, axis=axis, keepdims=True)
    v = jnp.var(x, axis=axis, keepdims=True)
    return (x - m) / jnp.sqrt(v + eps)

def _scatter_add(tgt, idx, src, axis=0):
    return tgt.at[idx].add(src)

def _segment_sum(src, seg, n):
    return jax.ops.segment_sum(src, seg, n)
kernel_name = 'mk_vit_tower_d2_tok_img768_r4_edeafa'

def setup_inputs(seed: int=0):
    np.random.seed(seed)
    _w = jnp.asarray

    def _rec_inputs():
        import jax
        import jax.numpy as jnp
        _rk = jax.random.key(seed)
        x = -0.00016672 + 0.999947 * jax.random.normal(jax.random.fold_in(_rk, 1), (32, 96, 96, 3), jnp.float32)
        return x
    x = _rec_inputs()

    def _L0_tok_setup():
        import jax, jax.numpy as jnp
        import numpy as np
        PATCH = 16
        HIDDEN = 192

        def extract_patches(x, p):
            B, H, W, C = x.shape
            Hp, Wp = (H // p, W // p)
            x = x.reshape(B, Hp, p, Wp, p, C)
            x = x.transpose(0, 1, 3, 2, 4, 5)
            return x.reshape(B, Hp * Wp, p * p * C)
        key = jax.random.key(seed)
        k1, k2, k3, k4, k5 = jax.random.split(key, 5)
        B, H, W, C = (64, 96, 96, 3)
        num_patches = (H // PATCH) ** 2
        patch_dim = PATCH * PATCH * C
        contactMap = jax.random.normal(k1, (B, H, W, C), dtype=jnp.float32)
        W_proj = jax.random.normal(k2, (patch_dim, HIDDEN), dtype=jnp.float32) * (1.0 / np.sqrt(patch_dim))
        b_proj = jnp.zeros((HIDDEN,), dtype=jnp.float32)
        cls_token = jax.random.normal(k3, (1, 1, HIDDEN), dtype=jnp.float32) * 0.05
        pos_embedding = jax.random.normal(k4, (num_patches + 1, HIDDEN), dtype=jnp.float32) * 0.05
        return {'contactMap': contactMap, 'W_proj': W_proj, 'b_proj': b_proj, 'cls_token': cls_token, 'pos_embedding': pos_embedding}
    _L0_tok_all = _L0_tok_setup()
    _L0_tok_in = {k: v for k, v in _L0_tok_all.items() if k in ('W_proj', 'b_proj', 'cls_token', 'pos_embedding')}
    del _L0_tok_all

    def _L0_attn_setup():
        import jax, jax.numpy as jnp
        import numpy as np
        B, N, C = (32, 256, 192)
        H = 12
        E = C // H
        SCALE = E ** (-0.5)
        EPS = 1e-06
        key = jax.random.key(seed)
        k1, k2, k3 = jax.random.split(key, 3)
        x = jax.random.normal(k1, (B, N, C), dtype=jnp.float32)
        qkv_w = jax.random.normal(k2, (3 * C, C), dtype=jnp.float32) * C ** (-0.5)
        proj_w = jax.random.normal(k3, (C, C), dtype=jnp.float32) * C ** (-0.5)
        proj_b = jnp.zeros((C,), dtype=jnp.float32)
        return {'x': x, 'qkv_w': qkv_w, 'proj_w': proj_w, 'proj_b': proj_b}
    _L0_attn_all = _L0_attn_setup()
    _L0_attn_in = {k: v for k, v in _L0_attn_all.items() if k in ('qkv_w', 'proj_w', 'proj_b')}
    del _L0_attn_all

    def _L0_ffn_setup():
        import jax, jax.numpy as jnp
        import numpy as np
        D = 192
        I = 768
        E = 8
        K = 2
        LIMIT = 10.0
        VOCAB = 8192

        def _expert(xf, W1, W2, W3):
            gate = jnp.minimum(xf @ W1, LIMIT)
            up = jnp.clip(xf @ W3, -LIMIT, LIMIT)
            return jax.nn.silu(gate) * up @ W2
        key = jax.random.key(seed)
        ks = jax.random.split(key, 10)
        s = 0.02
        return {'x': jax.random.normal(ks[0], (1, 512, D), dtype=jnp.float32), 'input_ids': jax.random.randint(ks[1], (1, 512), 0, VOCAB, dtype=jnp.int64), 'gate_w': jax.random.normal(ks[2], (D, E), dtype=jnp.float32) * s, 'gate_bias': jnp.zeros((E,), dtype=jnp.float32), 'w1': jax.random.normal(ks[3], (E, D, I), dtype=jnp.float32) * s, 'w2': jax.random.normal(ks[4], (E, I, D), dtype=jnp.float32) * s, 'w3': jax.random.normal(ks[5], (E, D, I), dtype=jnp.float32) * s, 'w1s': jax.random.normal(ks[6], (D, I), dtype=jnp.float32) * s, 'w2s': jax.random.normal(ks[7], (I, D), dtype=jnp.float32) * s, 'w3s': jax.random.normal(ks[8], (D, I), dtype=jnp.float32) * s}
    _L0_ffn_all = _L0_ffn_setup()
    _L0_ffn_in = {k: v for k, v in _L0_ffn_all.items() if k in ('input_ids', 'gate_w', 'gate_bias', 'w1', 'w2', 'w3', 'w1s', 'w2s', 'w3s')}
    del _L0_ffn_all

    def _L1_attn_setup():
        import jax, jax.numpy as jnp
        import numpy as np
        B, S, D = (2, 512, 192)
        H, STRIDE = (12, 8)
        HD = D // H

        def _stride_mask(S, stride, causal):
            i = jnp.arange(S)[:, None]
            j = jnp.arange(S)[None, :]
            strided = j % stride == 0
            if causal:
                strided = strided & (j <= i)
            return strided | (j == i) | (j == i - 1)
        key = jax.random.key(seed)
        k0, k1, k2 = jax.random.split(key, 3)
        x = jax.random.normal(k0, (B, S, D), dtype=jnp.float32)
        qkv_w = jax.random.normal(k1, (3 * D, D), dtype=jnp.float32) * 0.02
        qkv_b = jnp.zeros((3 * D,), dtype=jnp.float32)
        out_w = jax.random.normal(k2, (D, D), dtype=jnp.float32) * 0.02
        out_b = jnp.zeros((D,), dtype=jnp.float32)
        return {'x': x, 'qkv_w': qkv_w, 'qkv_b': qkv_b, 'out_w': out_w, 'out_b': out_b}
    _L1_attn_all = _L1_attn_setup()
    _L1_attn_in = {k: v for k, v in _L1_attn_all.items() if k in ('qkv_w', 'qkv_b', 'out_w', 'out_b')}
    del _L1_attn_all

    def _L1_ffn_setup():
        import jax, jax.numpy as jnp
        import numpy as np
        DIM = 192
        NUM_EXPERTS = 4
        NUM_HEADS = 12
        HEAD_DIM = DIM // NUM_HEADS
        MLP_HID = 4 * DIM
        FC1_OUT = MLP_HID + 3 * DIM
        FC2_IN = MLP_HID + DIM
        FC2_OUT = 2 * DIM
        CAP_FACTOR = 0.5
        LN_EPS = 1e-06
        key = jax.random.key(seed)
        ks = jax.random.split(key, 4)
        B, N = (8, 256)
        return {'x': jax.random.normal(ks[0], (B, N, DIM), jnp.float32), 'w_router': jax.random.normal(ks[1], (NUM_EXPERTS, DIM), jnp.float32) * 0.02, 'gamma1': jnp.ones((DIM,), jnp.float32), 'beta1': jnp.zeros((DIM,), jnp.float32), 'w1': jax.random.normal(ks[2], (FC1_OUT, DIM), jnp.float32) * 0.02, 'b1': jnp.zeros((FC1_OUT,), jnp.float32), 'w2': jax.random.normal(ks[3], (FC2_OUT, FC2_IN), jnp.float32) * 0.02, 'b2': jnp.zeros((FC2_OUT,), jnp.float32)}
    _L1_ffn_all = _L1_ffn_setup()
    _L1_ffn_in = {k: v for k, v in _L1_ffn_all.items() if k in ('w_router', 'gamma1', 'beta1', 'w1', 'b1', 'w2', 'b2')}
    del _L1_ffn_all
    return {'x': x, 'L0_tok_W_proj': _L0_tok_in['W_proj'], 'L0_tok_b_proj': _L0_tok_in['b_proj'], 'L0_tok_cls_token': _L0_tok_in['cls_token'], 'L0_tok_pos_embedding': _L0_tok_in['pos_embedding'], 'L0_attn_qkv_w': _L0_attn_in['qkv_w'], 'L0_attn_proj_w': _L0_attn_in['proj_w'], 'L0_attn_proj_b': _L0_attn_in['proj_b'], 'L0_ffn_input_ids': _L0_ffn_in['input_ids'], 'L0_ffn_gate_w': _L0_ffn_in['gate_w'], 'L0_ffn_gate_bias': _L0_ffn_in['gate_bias'], 'L0_ffn_w1': _L0_ffn_in['w1'], 'L0_ffn_w2': _L0_ffn_in['w2'], 'L0_ffn_w3': _L0_ffn_in['w3'], 'L0_ffn_w1s': _L0_ffn_in['w1s'], 'L0_ffn_w2s': _L0_ffn_in['w2s'], 'L0_ffn_w3s': _L0_ffn_in['w3s'], 'L1_attn_qkv_w': _L1_attn_in['qkv_w'], 'L1_attn_qkv_b': _L1_attn_in['qkv_b'], 'L1_attn_out_w': _L1_attn_in['out_w'], 'L1_attn_out_b': _L1_attn_in['out_b'], 'L1_ffn_w_router': _L1_ffn_in['w_router'], 'L1_ffn_gamma1': _L1_ffn_in['gamma1'], 'L1_ffn_beta1': _L1_ffn_in['beta1'], 'L1_ffn_w1': _L1_ffn_in['w1'], 'L1_ffn_b1': _L1_ffn_in['b1'], 'L1_ffn_w2': _L1_ffn_in['w2'], 'L1_ffn_b2': _L1_ffn_in['b2']}

def reference(x, L0_tok_W_proj, L0_tok_b_proj, L0_tok_cls_token, L0_tok_pos_embedding, L0_attn_qkv_w, L0_attn_proj_w, L0_attn_proj_b, L0_ffn_input_ids, L0_ffn_gate_w, L0_ffn_gate_bias, L0_ffn_w1, L0_ffn_w2, L0_ffn_w3, L0_ffn_w1s, L0_ffn_w2s, L0_ffn_w3s, L1_attn_qkv_w, L1_attn_qkv_b, L1_attn_out_w, L1_attn_out_b, L1_ffn_w_router, L1_ffn_gamma1, L1_ffn_beta1, L1_ffn_w1, L1_ffn_b1, L1_ffn_w2, L1_ffn_b2):
    import jax
    import jax.numpy as jnp

    def _L0_tok_ref(contactMap, W_proj, b_proj, cls_token, pos_embedding):
        import jax, jax.numpy as jnp
        import numpy as np
        PATCH = 16
        HIDDEN = 192

        def extract_patches(x, p):
            B, H, W, C = x.shape
            Hp, Wp = (H // p, W // p)
            x = x.reshape(B, Hp, p, Wp, p, C)
            x = x.transpose(0, 1, 3, 2, 4, 5)
            return x.reshape(B, Hp * Wp, p * p * C)
        B = contactMap.shape[0]
        patches = extract_patches(contactMap, PATCH)
        enc = jnp.einsum('bnd,dh->bnh', patches, W_proj) + b_proj
        cls = jnp.broadcast_to(cls_token.astype(contactMap.dtype), (B, 1, enc.shape[-1]))
        enc = jnp.concatenate([cls, enc], axis=1)
        return enc + pos_embedding

    def _L0_attn_ref(x, qkv_w, proj_w, proj_b):
        import jax, jax.numpy as jnp
        import numpy as np
        B, N, C = (32, 256, 192)
        H = 12
        E = C // H
        SCALE = E ** (-0.5)
        EPS = 1e-06
        b, n, c = x.shape
        qkv = jnp.einsum('bnc,dc->bnd', x, qkv_w).reshape(b, n, 3, H, E)
        q = qkv[:, :, 0]
        k = qkv[:, :, 1]
        v = qkv[:, :, 2]
        q_ = jax.nn.relu(q) + SCALE
        k_ = jax.nn.relu(k) + SCALE
        kv = jnp.einsum('bnhe,bnhd->bhed', k_, v)
        k_sum = jnp.sum(k_, axis=1)
        z = 1.0 / (jnp.einsum('bnhe,bhe->bnh', q_, k_sum) + EPS)
        out = jnp.einsum('bnhe,bhed->bnhd', q_, kv) * z[..., None]
        out = out.reshape(b, n, c)
        return jnp.einsum('bnc,dc->bnd', out, proj_w) + proj_b

    def _L0_ffn_ref(x, input_ids, gate_w, gate_bias, w1, w2, w3, w1s, w2s, w3s):
        import jax, jax.numpy as jnp
        import numpy as np
        D = 192
        I = 768
        E = 8
        K = 2
        LIMIT = 10.0
        VOCAB = 8192

        def _expert(xf, W1, W2, W3):
            gate = jnp.minimum(xf @ W1, LIMIT)
            up = jnp.clip(xf @ W3, -LIMIT, LIMIT)
            return jax.nn.silu(gate) * up @ W2
        B, T, _ = x.shape
        flat = x.reshape(-1, D)
        N = flat.shape[0]
        scores = jnp.sqrt(jax.nn.softplus(flat @ gate_w))
        routed_scores = scores + gate_bias
        _, indices = jax.lax.top_k(routed_scores, K)
        weights = jnp.take_along_axis(scores, indices, axis=1)
        weights = weights / jnp.clip(weights.sum(axis=-1, keepdims=True), 1e-06)
        combine = jnp.zeros((N, E), dtype=weights.dtype)
        combine = combine.at[jnp.arange(N)[:, None], indices].add(weights)
        y = _expert(flat, w1s, w2s, w3s)
        gate_h = jnp.minimum(jnp.einsum('td,edi->eti', flat, w1), LIMIT)
        up_h = jnp.clip(jnp.einsum('td,edi->eti', flat, w3), -LIMIT, LIMIT)
        h = jax.nn.silu(gate_h) * up_h
        out_e = jnp.einsum('eti,eid->etd', h, w2)
        routed = jnp.einsum('etd,te->td', out_e, combine)
        return (y + routed).reshape(B, T, D)

    def _L1_attn_ref(x, qkv_w, qkv_b, out_w, out_b):
        import jax, jax.numpy as jnp
        import numpy as np
        B, S, D = (2, 512, 192)
        H, STRIDE = (12, 8)
        HD = D // H

        def _stride_mask(S, stride, causal):
            i = jnp.arange(S)[:, None]
            j = jnp.arange(S)[None, :]
            strided = j % stride == 0
            if causal:
                strided = strided & (j <= i)
            return strided | (j == i) | (j == i - 1)
        Bx, Sx, Dx = x.shape
        qkv = x @ qkv_w.T + qkv_b
        qkv = qkv.reshape(Bx, Sx, 3, H, HD)
        q, k, v = jnp.transpose(qkv, (2, 0, 3, 1, 4))
        scale = HD ** (-0.5)
        attn = jnp.einsum('bhid,bhjd->bhij', q, k) * scale
        mask = _stride_mask(Sx, STRIDE, True)
        attn = jnp.where(mask[None, None], attn, -jnp.inf)
        a = jax.nn.softmax(attn, axis=-1)
        a = jnp.nan_to_num(a, nan=0.0)
        out = jnp.einsum('bhij,bhjd->bhid', a, v)
        out = jnp.transpose(out, (0, 2, 1, 3)).reshape(Bx, Sx, Dx)
        return out @ out_w.T + out_b

    def _L1_ffn_ref(x, w_router, gamma1, beta1, w1, b1, w2, b2):
        import jax, jax.numpy as jnp
        import numpy as np
        DIM = 192
        NUM_EXPERTS = 4
        NUM_HEADS = 12
        HEAD_DIM = DIM // NUM_HEADS
        MLP_HID = 4 * DIM
        FC1_OUT = MLP_HID + 3 * DIM
        FC2_IN = MLP_HID + DIM
        FC2_OUT = 2 * DIM
        CAP_FACTOR = 0.5
        LN_EPS = 1e-06
        B, N, C = x.shape
        E = NUM_EXPERTS
        cap = int(CAP_FACTOR * N)
        m = np.array([C // 2 ** (E - 1 - e) for e in range(E)])
        in_mask = (np.arange(C)[None, :] < m[:, None]).astype(np.float32)
        in_mask = jnp.asarray(in_mask)
        out_mask = jnp.concatenate([in_mask, in_mask], axis=-1)
        logits = jnp.einsum('bnc,ec->bne', x, w_router)
        probs = jax.nn.softmax(logits, axis=-1)
        gate, idx = jax.lax.top_k(jnp.swapaxes(probs, 1, 2), cap)
        dispatch = jax.nn.one_hot(idx, N, dtype=x.dtype)
        combine = dispatch * gate[..., None]
        mu = jnp.mean(x, -1, keepdims=True)
        var = jnp.var(x, -1, keepdims=True)
        y = (x - mu) * jax.lax.rsqrt(var + LN_EPS) * gamma1 + beta1
        xg = jnp.einsum('becn,bnd->becd', dispatch, y)
        xg = xg * in_mask[None, :, None, :]
        h = jnp.einsum('becd,fd->becf', xg, w1) + b1
        h = jnp.einsum('becn,becf->bnf', dispatch, h)
        x_mlp, x_qkv = (h[..., :MLP_HID], h[..., MLP_HID:])
        qkv = x_qkv.reshape(B, N, 3, NUM_HEADS, HEAD_DIM).transpose(2, 0, 3, 1, 4)
        q, k, v = (qkv[0], qkv[1], qkv[2])
        scale = HEAD_DIM ** (-0.5)
        attn = jax.nn.softmax(jnp.einsum('bhqd,bhkd->bhqk', q, k) * scale, axis=-1)
        x_attn = jnp.einsum('bhqk,bhkd->bhqd', attn, v)
        x_attn = x_attn.transpose(0, 2, 1, 3).reshape(B, N, C)
        x_mlp = jax.nn.gelu(x_mlp, approximate=False)
        y2 = jnp.concatenate([x_mlp, x_attn], axis=-1)
        yg = jnp.einsum('becn,bnf->becf', dispatch, y2)
        o = jnp.einsum('becf,of->beco', yg, w2) + b2
        o = o * out_mask[None, :, None, :]
        z = jnp.einsum('becn,beco->bno', combine, o)
        x_mlp2, x_attn2 = (z[..., :C], z[..., C:])
        return x + x_mlp2 + x_attn2
    h = _L0_tok_ref(x, L0_tok_W_proj, L0_tok_b_proj, L0_tok_cls_token, L0_tok_pos_embedding)
    h = h + _L0_attn_ref(_layernorm(h, axis=-1), L0_attn_qkv_w, L0_attn_proj_w, L0_attn_proj_b)
    h = h + _L0_ffn_ref(_layernorm(h, axis=-1), L0_ffn_input_ids, L0_ffn_gate_w, L0_ffn_gate_bias, L0_ffn_w1, L0_ffn_w2, L0_ffn_w3, L0_ffn_w1s, L0_ffn_w2s, L0_ffn_w3s)
    h = h + _L1_attn_ref(_layernorm(h, axis=-1), L1_attn_qkv_w, L1_attn_qkv_b, L1_attn_out_w, L1_attn_out_b)
    h = h + _L1_ffn_ref(_layernorm(h, axis=-1), L1_ffn_w_router, L1_ffn_gamma1, L1_ffn_beta1, L1_ffn_w1, L1_ffn_b1, L1_ffn_w2, L1_ffn_b2)
    return h

_drawn_inputs = setup_inputs


def setup_inputs(seed=0):
    import zlib

    import numpy as np

    out = dict(_drawn_inputs(seed))
    spreads = {'L0_tok_b_proj': (0.0, 0.1),
     'L0_attn_proj_b': (0.0, 0.1),
     'L0_ffn_gate_bias': (0.0, 0.481),
     'L1_attn_qkv_b': (0.0, 0.289),
     'L1_attn_out_b': (0.0, 0.1),
     'L1_ffn_gamma1': (1.0, 0.6),
     'L1_ffn_beta1': (0.0, 2.0),
     'L1_ffn_b1': (0.0, 0.369),
     'L1_ffn_b2': (0.0, 0.308)}
    factors = {'L0_ffn_gate_w': 4.93,
     'L0_ffn_w1': 3.452,
     'L0_ffn_w2': 3.406,
     'L0_ffn_w3': 3.382,
     'L0_ffn_w1s': 2.712,
     'L0_ffn_w3s': 2.803}
    for name, (base, spread) in spreads.items():
        noise = np.random.default_rng([zlib.crc32(name.encode()), seed]).standard_normal(out[name].shape)
        drawn = base * np.exp(spread * noise) if base else spread * noise
        out[name] = jnp.asarray(drawn.astype(out[name].dtype))
    for name, factor in factors.items():
        out[name] = (out[name] * factor).astype(out[name].dtype)
    return out
```

```python
import numpy as np
import concourse.bass as bass
from concourse import mybir
from contextlib import ExitStack

F32 = mybir.dt.float32
ALU = mybir.AluOpType
ACT = mybir.ActivationFunctionType
AX = mybir.AxisListType

P = 128
SLOT = 64
NIMG, NTOK, D, NH, HD = 32, 37, 192, 12, 16
TILES = NIMG // 2
DUOS = TILES // 2
LN_EPS = 1e-5
EPS2 = 1e-6
QKV17 = 2 * D + NH * 17
MLP = 768
FFN = 768
LIMIT = 10.0
SILU_LIMIT = LIMIT / (1 + float(np.exp(-LIMIT)))
CAP = NTOK // 2
RNG = ((0, 24), (24, 48), (48, 96), (96, 192))


def vit(nc, x_patches, tok_w, tok_pos, tok_onehot, tok_addrows, l0_qkv, l0_proj, ident_in, hmask17, moe_w1, moe_w3, moe_w2, gate_w, gate_bias, before8,
        l1_w, l1_out, l1_mask, kmask, vmask, ffn_w1, ffn_w2, ffn_router, ffn_gb, ffn_ranges, slot_eye, same_image, earlier, out):
    with ExitStack() as ctx:
        def sb(name, shape, dt=F32, ctx=ctx):
            return ctx.enter_context(nc.sbuf_tensor(name, shape, dt))[tuple(slice(None) for _ in shape)]

        def sem(name):
            return ctx.enter_context(nc.semaphore(name))

        banks = ctx.enter_context(nc.psum_tensor("banks", [P, 8, 512], F32))[:, :, :]
        ident = sb("ident", [P, P])
        w_tok = sb("w_tok", [P, 6, D])
        pos_bias = sb("pos_bias", [P, D])
        onehot = sb("onehot", [2, P])
        addrows = sb("addrows", [2, D])
        w_qkv0 = sb("w_qkv0", [P, 2, 3 * D])
        w_proj0 = sb("w_proj0", [P, 2, D])
        mask17 = sb("mask17", [P, 204])
        neghalf = sb("neghalf", [P, 2])
        h = sb("h", [P, TILES, D])
        xn = [sb(f"xn{j}", [P, 2, 256]) for j in range(2)]
        xt = [sb(f"xt{j}", [P, 2, 2, P]) for j in range(2)]
        ao = [sb(f"ao{j}", [P, 2, 256]) for j in range(2)]
        den = [sb(f"den{j}", [P, 2, NH]) for j in range(2)]
        st = [sb(f"st{j}", [P, 2, 6]) for j in range(2)]
        mv = [sb(f"mv{j}", [P, 2, 2]) for j in range(2)]
        ve = [sb(f"ve{j}", [P, 2]) for j in range(2)]
        rs = [sb(f"rs{j}", [P, 2]) for j in range(2)]

        w_g = sb("w_g", [P, 2, 8])
        gbias = sb("gbias", [P, 8])
        tri8 = sb("tri8", [P, 8, 8])
        xt_all = sb("xt_all", [P, 2, TILES * P])
        glog = sb("glog", [P, TILES, 8])
        gs = [sb(f"gs{k}", [P, TILES, 8]) for k in range(4)]
        gpair = [sb(f"gpair{k}", [P, TILES, 8, 8]) for k in range(2)]
        gsum = sb("gsum", [P, TILES])
        comb = sb("comb", [P, TILES, 9])
        sil = [sb(f"sil{k}", [P, 296]) for k in range(2)]
        upc = [sb(f"upc{k}", [P, 296]) for k in range(2)]
        eh = [sb(f"eh{k}", [P, 6, 8, SLOT]) for k in range(2)]
        w_l1 = sb("w_l1", [P, 2, QKV17])
        w_l1o = sb("w_l1o", [P, 2, D])
        m_causal = sb("m_causal", [P, NTOK])
        m_k = sb("m_k", [P, 12])
        m_v = sb("m_v", [3 * NTOK, 51])
        w_f1 = sb("w_f1", [P, 2, MLP + QKV17])
        w_f2 = sb("w_f2", [P, 8, 2, D])
        w_f2s = sb("w_f2s", [P, 8, D])
        w_r = sb("w_r", [P, 2, 4])
        gb = sb("gb", [P, 2, 2])
        ranges = sb("ranges", [P, 2, 4])
        beta4 = sb("beta4", [P, 2, 4])
        eye37 = sb("eye37", [P, NTOK])
        samei = sb("samei", [P, P])
        tri = sb("tri", [P, NTOK])
        xc = [sb(f"xc{j}", [P, 2, 4 * SLOT]) for j in range(2)]
        qp = [sb(f"qp{j}", [P, 2, 4, SLOT]) for j in range(2)]
        mx = [sb(f"mx{j}", [P, 2, 12]) for j in range(2)]
        yn = [sb(f"yn{j}", [P, 2, 256]) for j in range(2)]
        hid = [sb(f"hid{j}", [P, 6, 4, SLOT]) for j in range(2)]
        lg = [sb(f"lg{j}", [P, 2, 4]) for j in range(2)]
        pr = [sb(f"pr{j}", [P, 2, 4]) for j in range(2)]
        l1s = [sb(f"l1s{j}", [P, 2]) for j in range(2)]
        rank = [sb(f"rank{j}", [P, 2, 4]) for j in range(2)]
        sg = [sb(f"sg{j}", [P, 2, 2, 4]) for j in range(2)]
        rsr = [sb(f"rsr{j}", [P, 2, 4]) for j in range(2)]

        with ExitStack() as during:
            patches = [sb(f"patches{j}", [P, 6, 2 * P], ctx=during) for j in range(2)]
            kpos = [sb(f"kpos{j}", [P, 2, D], ctx=during) for j in range(2)]
            v17 = [sb(f"v17{j}", [P, 2, NH, 17], ctx=during) for j in range(2)]
            qt = [sb(f"qt{j}", [P, 2, 2, P], ctx=during) for j in range(2)]
            kvm = [sb(f"kvm{j}", [P, 4, 204], ctx=during) for j in range(2)]
        with ExitStack() as during:
            ew1 = [sb(f"ew1{r}", [P, 2, FFN], ctx=during) for r in range(3)]
            ew3 = [sb(f"ew3{r}", [P, 2, FFN], ctx=during) for r in range(3)]
            ew2 = [sb(f"ew2{r}", [P, 6, D], ctx=during) for r in range(3)]
        xr = [sb(f"xr{j}", [P, 2, 4, 3 * NTOK]) for j in range(2)]
        kc = [sb(f"kc{j}", [P, 2, 4, NTOK]) for j in range(2)]
        kx = [sb(f"kx{j}", [P, 4, 12 * NTOK]) for j in range(2)]
        sc = [sb(f"sc{j}", [P, 2, 12, NTOK]) for j in range(2)]
        pt = [sb(f"pt{j}", [3 * NTOK, 2, 4, P]) for j in range(2)]
        vx = [sb(f"vx{j}", [3 * NTOK, 4, 204]) for j in range(2)]
        dg = [sb(f"dg{j}", [P, 2, 4, NTOK]) for j in range(2)]
        gt = [sb(f"gt{j}", [P, 2, 4, NTOK]) for j in range(2)]
        eq = [sb(f"eq{j}", [P, 2, 4, NTOK]) for j in range(2)]
        zz = [xn[j][:, :, 0:D] for j in range(2)]

        w_in = sem("w_in")
        patches_in = [sem("patches_in0"), sem("patches_in1")]
        consts_set = sem("consts_set")
        posb_mm = sem("posb_mm")
        posb_set = sem("posb_set")
        tok_mm = sem("tok_mm")
        h_tok = sem("h_tok")
        st1 = sem("st1"); mv1 = sem("mv1"); ve1 = sem("ve1"); rs1 = sem("rs1"); xn1 = sem("xn1")
        xt1_mm = sem("xt1_mm"); xt1 = sem("xt1")
        kv_mm = sem("kv_mm"); kset = sem("kset"); vset = sem("vset")
        q_mm = sem("q_mm"); qset = sem("qset")
        kvi_mm = sem("kvi_mm"); kvm_set = sem("kvm_set")
        o_mm = sem("o_mm"); den_e = sem("den_e"); den_set = sem("den_set"); ao_set = sem("ao_set")
        at_mm = sem("at_mm"); at_set = sem("at_set")
        pr_mm = sem("pr_mm"); h_attn = sem("h_attn")
        out_done = sem("out_done")
        y_free = sem("y_free")
        sil_free = sem("sil_free")
        upc_set = sem("upc_set")
        NAMES = "xr st ve rs xn xt_mm xt q_mm k_mm q k kx v_mm vx s_mm sm mx sub e pt_mm pt o_mm den rden ao at_mm at pr_mm h".split()
        A1 = {n: sem("l1_" + n) for n in NAMES}
        A2 = {n: sem("f_" + n) for n in NAMES + "lg_mm lgmx lgsub lgexp lgsum lgrec p dg bc_mm cmp cmp2 rank sel s2 s3 s4 st2 ve2 rs2 rsr yn yt_mm yt mlp_mm gelu fc_mm zz hx".split()}
        A0 = {n: sem("g_" + n) for n in "ve rs xn xt_mm xt xall lg_mm lg abs exp ln sp sq comb".split()}
        ew_in = [sem(f"ew_in{r}") for r in range(3)]
        g_mm = sem("g_mm"); u_mm = sem("u_mm"); silu_set = sem("silu_set"); up_read = sem("up_read"); eh_set = sem("eh_set"); y_mm = sem("y_mm"); y_added = sem("y_added")
        beta4_set = sem("beta4_set"); bw_mm = sem("bw_mm"); bw_set = sem("bw_set"); w2_set = sem("w2_set")

        block = ctx.enter_context(nc.Block())
        NW = 24

        def bank(j, n, k=1):
            return banks[:, 4 * j + n] if k == 1 else banks[:, 4 * j + n:4 * j + n + k, :]

        @block.sync
        def _(sp):
            for dst, src in ((ident, ident_in), (onehot, tok_onehot), (addrows, tok_addrows), (pos_bias, tok_pos),
                             (w_tok, tok_w), (mask17, hmask17), (w_qkv0, l0_qkv), (w_proj0, l0_proj), (w_g, gate_w), (gbias, gate_bias), (tri8, before8),
                             (w_l1, l1_w), (w_l1o, l1_out), (m_causal, l1_mask), (m_k, kmask), (m_v, vmask), (w_f1, ffn_w1), (w_f2, ffn_w2), (w_r, ffn_router), (gb, ffn_gb), (ranges, ffn_ranges), (eye37, slot_eye), (samei, same_image), (tri, earlier)):
                sp.dma_start(dst[:], src).then_inc(w_in, 16)
            for j in range(2):
                sp.dma_start(patches[j], x_patches[j]).then_inc(patches_in[j], 16)
            with sp.Fori(0, DUOS // 2 - 1) as it:
                for j in range(2):
                    sp.wait_ge(tok_mm, 2 * it + j + 1)
                    sp.dma_start(patches[j], x_patches[bass.ds(2 * it + j + 2, 1)].rearrange("o p c n -> (o p) c n")).then_inc(patches_in[j], 16)
            sp.wait_ge(h_attn, DUOS)
            for r in range(3):
                for dst, src in ((ew1, moe_w1), (ew3, moe_w3), (ew2, moe_w2)):
                    sp.dma_start(dst[r], src[r]).then_inc(ew_in[r], 16)
            with sp.Fori(0, 2) as ie:
                for r in range(3):
                    sp.wait_ge(y_mm, 24 * ie + 8 * r + 8)
                    for dst, src in ((ew1, moe_w1), (ew3, moe_w3), (ew2, moe_w2)):
                        sp.dma_start(dst[r], src[bass.ds(3 * ie + r + 3, 1)].rearrange("o p c n -> (o p) c n")).then_inc(ew_in[r], 16)
            sp.wait_ge(A2["h"], DUOS)
            for im in range(2):
                o = out.rearrange("(t i) n d -> i n t d", i=2)[im]
                sp.dma_start(o, h[SLOT * im:SLOT * im + NTOK, :, :]).then_inc(out_done, 16)
            sp.wait_ge(out_done, 32)

        @block.gpsimd
        def _(pool):
            pool.memset(neghalf[:], -0.5)
            pool.memset(comb, 1.0)
            pool.wait_ge(w_in, 16 * NW)
            for j in range(2):
                pool.memset(xn[j][:, :, 192:193], 1.0)
                pool.memset(xn[j][:, :, 193:256], 0.0)
                pool.memset(ao[j][:, :, 192:193], 1.0)
                pool.memset(ao[j][:, :, 193:256], 0.0)
                ins = pool.memset(v17[j][:, :, :, 16:17], 1.0)
                pool.memset(qp[j], 0.0)
                pool.memset(eh[j], 0.0)
                pool.memset(hid[j], 0.0)
                pool.memset(yn[j][:, :, 196:197], 1.0)
                ins = pool.memset(yn[j][:, :, 197:256], 0.0)
            ins.then_inc(consts_set, 1)
            pool.wait_ge(consts_set, 1)
            for c in range(2):
                ins = pool.tensor_tensor(beta4[:, c], ranges[:, c], gb[:, c, 1:2].to_broadcast([P, 4]), ALU.mult)
            ins.then_inc(beta4_set, 1)
            pool.tensor_tensor(w_f2s, w_f2[:, :, 0, :], w_f2[:, :, 1, :], ALU.add).then_inc(w2_set, 1)
            with pool.Fori(0, DUOS // 2) as it:
                for j in range(2):
                    pool.wait_ge(ve1, 2 * it + j + 1)
                    pool.tensor_tensor(rs[j][:], ve[j][:], neghalf[:], ALU.pow).then_inc(rs1, 1)
                for j in range(2):
                    pool.wait_ge(A0["ve"], 2 * it + j + 1)
                    pool.tensor_tensor(rs[j][:], ve[j][:], neghalf[:], ALU.pow).then_inc(A0["rs"], 1)
                for j in range(2):
                    pool.wait_ge(A0["xt"], 2 * it + j + 1)
                    pool.tensor_copy(xt_all[:, :, bass.ds(512 * it + 256 * j, 256)], xc[j]).then_inc(A0["xall"], 1)

            def kexp(a, it):
                for j in range(2):
                    pool.wait_ge(a["k"], 2 * it + j + 1)
                    for c, (h0, nh) in enumerate(((0, 8), (8, 4))):
                        for im in range(4):
                            ins = pool.tensor_tensor(kx[j][:, im, NTOK * h0:NTOK * (h0 + nh)].rearrange("p (h n) -> p h n", h=nh),
                                           kc[j][:, c, im].unsqueeze(1).to_broadcast([P, nh, NTOK]),
                                           m_k[:, h0:h0 + nh].unsqueeze(2).to_broadcast([P, nh, NTOK]), ALU.mult)
                    ins.then_inc(a["kx"], 1)

            with pool.Fori(0, DUOS // 2) as it:
                for j in range(2):
                    pool.wait_ge(A1["ve"], 2 * it + j + 1)
                    pool.tensor_tensor(rs[j][:], ve[j][:], neghalf[:], ALU.pow).then_inc(A1["rs"], 1)
                kexp(A1, it)
            with pool.Fori(0, DUOS // 2) as it:
                for j in range(2):
                    pool.wait_ge(A2["ve"], 2 * it + j + 1)
                    pool.tensor_tensor(rs[j][:], ve[j][:], neghalf[:], ALU.pow).then_inc(A2["rs"], 1)
                for j in range(2):
                    pool.wait_ge(A2["ve2"], 2 * it + j + 1)
                    pool.tensor_tensor(rs[j][:], ve[j][:], neghalf[:], ALU.pow).then_inc(A2["rs2"], 1)
                kexp(A2, it)

        @block.tensor
        def _(pe):
            def transposes(src, dst, ready, done, n):
                for j in range(2):
                    pe.wait_ge(ready, n[j])
                    for c in range(2):
                        for t in range(2):
                            mm = pe.transpose(bank(j, dst)[:, (2 * c + t) * P:(2 * c + t + 1) * P],
                                              src[j][:, t, c * P:(c + 1) * P], ident)
                    mm.then_inc(done, 1)

            pe.wait_ge(w_in, 16 * NW)
            pe.matmul(bank(0, 0)[:, 0:D], onehot[:], addrows[:], start=True, stop=True).then_inc(posb_mm, 1)
            pe.wait_ge(posb_set, 1)
            with pe.Fori(0, DUOS // 2) as it:
                n = [2 * it + 1, 2 * it + 2]
                for j in range(2):
                    pe.wait_ge(patches_in[j], 16 * (it + 1))
                    for t in range(2):
                        for c in range(6):
                            mm = pe.matmul(bank(j, 0)[:, t * D:(t + 1) * D], patches[j][:, c, t * P:(t + 1) * P],
                                           w_tok[:, c, :], start=(c == 0), stop=(c == 5))
                    mm.then_inc(tok_mm, 1)
                for j in range(2):
                    pe.wait_ge(xn1, n[j])
                    for t in range(2):
                        for c in range(2):
                            mm = pe.transpose(bank(j, 1)[:, (2 * t + c) * P:(2 * t + c + 1) * P],
                                              xn[j][:, t, c * P:(c + 1) * P], ident[:])
                    mm.then_inc(xt1_mm, 1)
                for j in range(2):
                    pe.wait_ge(xt1, n[j])
                    for b, f in ((2, slice(D, 2 * D)), (3, slice(2 * D, 3 * D))):
                        for t in range(2):
                            o = bank(j, b)[:, t * D:(t + 1) * D]
                            pe.matmul(o, xt[j][:, t, 0, :], w_qkv0[:, 0, f], start=True, stop=False)
                            mm = pe.matmul(o, xt[j][0:64, t, 1, :], w_qkv0[0:64, 1, f], start=False, stop=True)
                    mm.then_inc(kv_mm, 1)
                    for c in range(2):
                        f = slice(64 * c, 64 * c + P)
                        o = bank(j, 0).rearrange("p (t c n) -> p t c n", t=2, c=2)[:, :, c, :]
                        pe.matmul(o, w_qkv0[:, 0, f], xt[j][:, :, 0, :], start=True, stop=False)
                        mm = pe.matmul(o, w_qkv0[0:64, 1, f], xt[j][0:64, :, 1, :], start=False, stop=True)
                    mm.then_inc(q_mm, 1)
                for j in range(2):
                    pe.wait_ge(kset, n[j])
                    pe.wait_ge(vset, n[j])
                    for t in range(2):
                        for im in range(2):
                            r = slice(SLOT * im, SLOT * im + NTOK)
                            o = bank(j, 2 + im)[:, 204 * t:204 * t + 204]
                            vr = v17[j][r, t].rearrange("p h e -> p (h e)")
                            pe.matmul(o[:, 0:136], kpos[j][r, t, 0:P], vr[:, 0:136], start=True, stop=True)
                            mm = pe.matmul(o[:, 136:204], kpos[j][r, t, 64:192], vr[:, 136:204], start=True, stop=True)
                    mm.then_inc(kvi_mm, 1)
                for j in range(2):
                    pe.wait_ge(qset, n[j])
                    pe.wait_ge(kvm_set, n[j])
                    for t in range(2):
                        for im in range(2):
                            r = slice(SLOT * im, SLOT * im + SLOT)
                            o = bank(j, 1)[r, 204 * t:204 * t + 204]
                            pe.matmul(o[:, 0:136], qt[j][:, t, 0, r], kvm[j][:, 2 * im + t, 0:136], start=True, stop=True)
                            mm = pe.matmul(o[:, 136:204], qt[j][:, t, 1, r], kvm[j][:, 2 * im + t, 136:204], start=True, stop=True)
                    mm.then_inc(o_mm, 1)
                for j in range(2):
                    pe.wait_ge(ao_set, n[j])
                    for t in range(2):
                        for c in range(2):
                            mm = pe.transpose(bank(j, 0)[:, (2 * t + c) * P:(2 * t + c + 1) * P],
                                              ao[j][:, t, c * P:(c + 1) * P], ident[:])
                    mm.then_inc(at_mm, 1)
                for j in range(2):
                    pe.wait_ge(at_set, n[j])
                    for t in range(2):
                        pe.matmul(bank(j, 2)[:, t * D:(t + 1) * D], xt[j][:, t, 0, :], w_proj0[:, 0, :], start=True, stop=False)
                        mm = pe.matmul(bank(j, 2)[:, t * D:(t + 1) * D], xt[j][0:65, t, 1, :], w_proj0[0:65, 1, :], start=False, stop=True)
                    mm.then_inc(pr_mm, 1)
                transposes(xn, 3, A0["xn"], A0["xt_mm"], n)
                for j in range(2):
                    pe.wait_ge(A0["xt"], n[j])
                    for t in range(2):
                        o = bank(j, 1)[:, 8 * t:8 * t + 8]
                        pe.matmul(o, xc[j][:, 0, P * t:P * t + P], w_g[:, 0, :], start=True, stop=False)
                        mm = pe.matmul(o, xc[j][0:64, 1, P * t:P * t + P], w_g[0:64, 1, :], start=False, stop=True)
                    mm.then_inc(A0["lg_mm"], 1)

            pe.wait_ge(A0["lg"], DUOS)
            pe.wait_ge(A0["xall"], DUOS)
            with pe.Fori(0, 3) as ie:
                for r in range(3):
                    pe.wait_ge(ew_in[r], 48 * ie + 48)
                    for c in range(4):
                        k = 12 * ie + 4 * r + c
                        xm = [xt_all[0:pk, i, 512 * c:512 * c + 512].rearrange("p (i s) -> p i s", s=SLOT)[:, :, 0:NTOK] for i, pk in ((0, P), (1, 64))]
                        for f in range(6):
                            m = slice(P * f, P * f + P)
                            for w, b0, done, free in ((ew1, 0, g_mm, silu_set), (ew3, 2, u_mm, up_read)):
                                pe.wait_ge(free, 6 * k + f + 1)
                                o = banks[:, b0 + f % 2, 0:296].rearrange("p (i n) -> p i n", n=NTOK)
                                pe.matmul(o, w[r][:, 0, m], xm[0], start=True, stop=False)
                                pe.matmul(o, w[r][0:64, 1, m], xm[1], start=False, stop=True).then_inc(done, 1)
                        pe.wait_ge(eh_set, 6 * k + 6)
                        for t2 in range(2):
                            pe.wait_ge(y_added, 2 * k + t2 + 1)
                            for t in range(2):
                                o = banks[:, 4 + 2 * (c % 2) + t2, t * D:(t + 1) * D]
                                for f in range(6):
                                    mm = pe.matmul(o, eh[c % 2][:, f, 4 * t2 + 2 * t:4 * t2 + 2 * t + 2, :].rearrange("p i s -> p (i s)"), ew2[r][:, f, :], start=(f == 0), stop=(f == 5))
                            mm.then_inc(y_mm, 1)
            pe.wait_ge(y_added, 72 + 4)
            pe.wait_ge(beta4_set, 1)
            pe.wait_ge(h_attn, DUOS)
            for n0 in range(3):
                f = slice(452 * n0, 452 * n0 + 452)
                o = banks[64:68, 4 + n0, 0:452]
                pe.matmul(o, beta4[:, 0, :], w_f1[:, 0, f], start=True, stop=False)
                mm = pe.matmul(o, beta4[0:64, 1, :], w_f1[0:64, 1, f], start=False, stop=True)
            mm.then_inc(bw_mm, 1)

            def toks(buf, j, k, c):
                return buf[j][0:k, c].rearrange("p (i s) -> p i s", s=SLOT)[:, :, 0:NTOK]

            def attention_in(a, w, f0, k1, n, x_set):
                for j in range(2):
                    pe.wait_ge(x_set, n[j])
                    for b, g, done in ((1, f0, a["q_mm"]), (2, f0 + D, a["k_mm"])):
                        for c in range(2):
                            f = slice(g + 64 * c, g + 64 * c + P)
                            o = bank(j, b)[:, 148 * c:148 * c + 148].rearrange("p (i n) -> p i n", n=NTOK)
                            pe.matmul(o, w[:, 0, f], toks(xc, j, P, 0), start=True, stop=False)
                            mm = pe.matmul(o, w[0:k1, 1, f], toks(xc, j, k1, 1), start=False, stop=True)
                        mm.then_inc(done, 1)
                    pe.wait_ge(a["xr"], n[j])
                    for im in range(2):
                        for t in range(2):
                            f = slice(f0 + 2 * D, f0 + QKV17)
                            o = bank(j, 3 - 3 * im)[0:3 * NTOK, 204 * t:204 * t + 204]
                            pe.matmul(o, xr[j][:, 0, 2 * t + im], w[:, 0, f], start=True, stop=False)
                            mm = pe.matmul(o, xr[j][0:k1, 1, 2 * t + im], w[0:k1, 1, f], start=False, stop=True)
                    mm.then_inc(a["v_mm"], 1)

            def attention_core(a, n):
                for j in range(2):
                    pe.wait_ge(a["q"], n[j])
                    pe.wait_ge(a["kx"], n[j])
                    for t in range(2):
                        for im in range(2):
                            o = bank(j, 1 + t)[SLOT * im:SLOT * im + SLOT, 0:444]
                            i = 2 * t + im
                            pe.matmul(o[:, 0:296], qp[j][:, 0, i, :], kx[j][:, i, 0:296], start=True, stop=True)
                            mm = pe.matmul(o[:, 296:444], qp[j][:, 1, i, :], kx[j][:, i, 296:444], start=True, stop=True)
                    mm.then_inc(a["s_mm"], 1)
                for j in range(2):
                    pe.wait_ge(a["e"], n[j])
                    pe.wait_ge(a["vx"], n[j])
                    for t in range(2):
                        for g in range(4):
                            mm = pe.transpose(bank(j, 3 - 3 * t)[0:111, P * g:P * g + P],
                                              sc[j][:, t, 3 * g:3 * g + 3, :].rearrange("p h n -> p (h n)"), ident)
                    mm.then_inc(a["pt_mm"], 1)
                for j in range(2):
                    pe.wait_ge(a["pt"], n[j])
                    for t in range(2):
                        for im in range(2):
                            for g in range(4):
                                o = bank(j, 1)[SLOT * im:SLOT * im + SLOT, 204 * t + 51 * g:204 * t + 51 * g + 51]
                                mm = pe.matmul(o, pt[j][:, t, g, SLOT * im:SLOT * im + SLOT], vx[j][:, 2 * im + t, 51 * g:51 * g + 51], start=True, stop=True)
                    mm.then_inc(a["o_mm"], 1)

            pe.wait_ge(bw_set, 1)
            pe.wait_ge(w2_set, 1)
            with pe.Fori(0, DUOS // 2) as it:
                n = [2 * it + 1, 2 * it + 2]
                transposes(xn, 0, A1["xn"], A1["xt_mm"], n)
                attention_in(A1, w_l1, 0, 65, n, A1["xt"])
                attention_core(A1, n)
                transposes(ao, 2, A1["ao"], A1["at_mm"], n)
                for j in range(2):
                    pe.wait_ge(A1["at"], n[j])
                    for t in range(2):
                        o = bank(j, 3)[:, t * D:(t + 1) * D]
                        pe.matmul(o, xc[j][:, 0, P * t:P * t + P], w_l1o[:, 0, :], start=True, stop=False)
                        mm = pe.matmul(o, xc[j][0:65, 1, P * t:P * t + P], w_l1o[0:65, 1, :], start=False, stop=True)
                    mm.then_inc(A1["pr_mm"], 1)

            with pe.Fori(0, DUOS // 2) as it:
                n = [2 * it + 1, 2 * it + 2]
                transposes(xn, 0, A2["xn"], A2["xt_mm"], n)
                for j in range(2):
                    pe.wait_ge(A2["xt"], n[j])
                    for t in range(2):
                        o = bank(j, 1)[:, 4 * t:4 * t + 4]
                        pe.matmul(o, xc[j][:, 0, P * t:P * t + P], w_r[:, 0, :], start=True, stop=False)
                        mm = pe.matmul(o, xc[j][0:64, 1, P * t:P * t + P], w_r[0:64, 1, :], start=False, stop=True)
                    mm.then_inc(A2["lg_mm"], 1)
                for j in range(2):
                    pe.wait_ge(A2["dg"], n[j])
                    pe.matmul(bank(j, 2)[:, 0:296], samei, dg[j].rearrange("p t e n -> p (t e n)"), start=True, stop=True).then_inc(A2["bc_mm"], 1)
                transposes(yn, 0, A2["yn"], A2["yt_mm"], n)
                attention_in(A2, w_f1, MLP, 69, n, A2["yt"])
                attention_core(A2, n)
                for j in range(2):
                    pe.wait_ge(A2["ao"], n[j])
                    for b in range(2):
                        for i in range(3):
                            f = slice(P * (3 * b + i), P * (3 * b + i + 1))
                            o = bank(j, b)[:, 148 * i:148 * i + 148].rearrange("p (i n) -> p i n", n=NTOK)
                            pe.matmul(o, w_f1[:, 0, f], toks(xc, j, P, 0), start=True, stop=False)
                            mm = pe.matmul(o, w_f1[0:69, 1, f], toks(xc, j, 69, 1), start=False, stop=True)
                    mm.then_inc(A2["mlp_mm"], 1)
                transposes(ao, 2, A2["ao"], A2["at_mm"], n)
                for j in range(2):
                    pe.wait_ge(A2["at"], n[j])
                    pe.wait_ge(A2["gelu"], n[j])
                    for t in range(2):
                        o = bank(j, 3)[:, t * D:(t + 1) * D]
                        for c in range(6):
                            pe.matmul(o, hid[j][:, c, 2 * t:2 * t + 2, :].rearrange("p i s -> p (i s)"), w_f2s[:, c, :], start=(c == 0), stop=False)
                        pe.matmul(o, xc[j][:, 0, P * t:P * t + P], w_f2s[:, 6, :], start=False, stop=False)
                        mm = pe.matmul(o, xc[j][0:65, 1, P * t:P * t + P], w_f2s[0:65, 7, :], start=False, stop=True)
                    mm.then_inc(A2["fc_mm"], 1)

        @block.scalar
        def _(act):
            def columns(b, ready, done, n):
                for j in range(2):
                    act.wait_ge(ready, n[j])
                    act.copy(xc[j].rearrange("p c n -> p (c n)"), bank(j, b)).then_inc(done, 1)

            with act.Fori(0, DUOS // 2) as it:
                n = [2 * it + 1, 2 * it + 2]
                for j in range(2):
                    act.wait_ge(xt1_mm, n[j])
                    act.copy(xt[j].rearrange("p t c n -> p (t c n)"), bank(j, 1)).then_inc(xt1, 1)
                for j in range(2):
                    act.wait_ge(kv_mm, n[j])
                    act.copy(v17[j][:, :, :, 0:16], bank(j, 3)[:, 0:2 * D].rearrange("p (t h e) -> p t h e", t=2, h=NH)).then_inc(vset, 1)
                for j in range(2):
                    act.wait_ge(at_mm, n[j])
                    act.copy(xt[j].rearrange("p t c n -> p (t c n)"), bank(j, 0)).then_inc(at_set, 1)
                columns(3, A0["xt_mm"], A0["xt"], n)
            act.wait_ge(A0["lg"], DUOS)
            act.activation(gs[0], glog, ACT.Abs).then_inc(A0["abs"], 1)
            act.wait_ge(A0["abs"], 1)
            act.activation(gs[0], gs[0], ACT.Exp, scale=-1.0).then_inc(A0["exp"], 1)
            act.wait_ge(A0["exp"], 1)
            act.activation(gs[1], gs[0], ACT.Ln, bias=1.0).then_inc(A0["ln"], 1)
            act.wait_ge(A0["sp"], 1)
            act.activation(gs[2], gs[3], ACT.Sqrt).then_inc(A0["sq"], 1)
            act.sem_inc(silu_set, 2)
            with act.Fori(0, 3) as ie:
                for c in range(12):
                    for f in range(6):
                        q = 72 * ie + 6 * c + f
                        act.wait_ge(g_mm, q + 1)
                        act.wait_ge(sil_free, q + 1)
                        act.activation(sil[f % 2], banks[:, f % 2, 0:296], ACT.Silu).then_inc(silu_set, 1)

            def attention(a, n):
                for j in range(2):
                    for c in range(2):
                        ins = act.copy(xr[j][:, c].rearrange("p i (r n) -> p i r n", r=3), xc[j][:, c].rearrange("p (i s) -> p i s", s=SLOT)[:, :, 0:NTOK].unsqueeze(2).to_broadcast([P, 4, 3, NTOK]))
                    ins.then_inc(a["xr"], 1)
                for j in range(2):
                    act.wait_ge(a["q_mm"], n[j])
                    act.copy(qp[j][:, :, :, 0:NTOK], bank(j, 1)[:, 0:296].rearrange("p (c i n) -> p c i n", c=2, n=NTOK)).then_inc(a["q"], 1)
                    act.wait_ge(a["k_mm"], n[j])
                    act.copy(kc[j].rearrange("p c i n -> p (c i n)"), bank(j, 2)[:, 0:296]).then_inc(a["k"], 1)
                for j in range(2):
                    act.wait_ge(a["sub"], n[j])
                    act.activation(sc[j], sc[j], ACT.Exp, scale=HD ** -0.5).then_inc(a["e"], 1)
                for j in range(2):
                    act.wait_ge(a["pt_mm"], n[j])
                    for t in range(2):
                        ins = act.copy(pt[j][:, t].rearrange("p g n -> p (g n)"), bank(j, 3 - 3 * t)[0:111, :])
                    ins.then_inc(a["pt"], 1)

            with act.Fori(0, DUOS // 2) as it:
                n = [2 * it + 1, 2 * it + 2]
                columns(0, A1["xt_mm"], A1["xt"], n)
                act.wait_ge(A1["xt"], n[1])
                attention(A1, n)
                columns(2, A1["at_mm"], A1["at"], n)
            with act.Fori(0, DUOS // 2) as it:
                n = [2 * it + 1, 2 * it + 2]
                columns(0, A2["xt_mm"], A2["xt"], n)
                for j in range(2):
                    act.wait_ge(A2["lgsub"], n[j])
                    act.activation(pr[j], lg[j], ACT.Exp).then_inc(A2["lgexp"], 1)
                columns(0, A2["yt_mm"], A2["yt"], n)
                act.wait_ge(A2["yt"], n[1])
                attention(A2, n)
                for j in range(2):
                    act.wait_ge(A2["mlp_mm"], n[j])
                    for b in range(2):
                        for i in range(3):
                            ins = act.activation(hid[j][:, 3 * b + i, :, 0:NTOK],
                                       bank(j, b)[:, 148 * i:148 * i + 148].rearrange("p (i n) -> p i n", n=NTOK), ACT.Gelu)
                    ins.then_inc(A2["gelu"], 1)
                columns(2, A2["at_mm"], A2["at"], n)

        @block.vector
        def _(dve):
            def stats(a, src, j, n, eps, ve_sem):
                for t in range(2):
                    dve.bn_stats(st[j][:, t, :], src[t])
                dve.drain()
                for t in range(2):
                    ins = dve.bn_aggr(mv[j][:, t, :], st[j][:, t, :])
                dve.drain()
                dve.tensor_scalar_add(ve[j], mv[j][:, :, 1], eps).then_inc(ve_sem, 1)

            def h_tiles(it):
                return ([h[:, bass.ds(4 * it + 2 * j, 2), :] for j in range(2)],
                        [[h[:, bass.ds(4 * it + 2 * j + t, 1), :].rearrange("p o d -> p (o d)") for t in range(2)] for j in range(2)])

            def normalised(a, h1, n):
                for j in range(2):
                    stats(a, h1[j], j, n, LN_EPS, a["ve"])
                for j in range(2):
                    dve.wait_ge(a["rs"], n[j])
                    for t in range(2):
                        ins = dve.tensor_scalar(xn[j][:, t, 0:D], h1[j][t], mv[j][:, t, 0:1], rs[j][:, t:t + 1], ALU.subtract, ALU.mult)
                    ins.then_inc(a["xn"], 1)

            dve.wait_ge(w_in, 16 * NW)
            dve.wait_ge(posb_mm, 1)
            dve.tensor_tensor(pos_bias[:], pos_bias[:], bank(0, 0)[:, 0:D], ALU.add).then_inc(posb_set, 1)
            dve.wait_ge(posb_set, 1)
            dve.wait_ge(consts_set, 1)
            with dve.Fori(0, DUOS // 2) as it:
                n = [2 * it + 1, 2 * it + 2]
                ht = [h[:, bass.ds(4 * it + 2 * j, 2), :] for j in range(2)]
                h1 = [[h[:, bass.ds(4 * it + 2 * j + t, 1), :].rearrange("p o d -> p (o d)") for t in range(2)] for j in range(2)]
                for j in range(2):
                    dve.wait_ge(tok_mm, n[j])
                    dve.tensor_tensor(ht[j], bank(j, 0)[:, 0:2 * D].rearrange("p (t d) -> p t d", t=2),
                                      pos_bias.unsqueeze(1).to_broadcast([P, 2, D]), ALU.add)
                    dve.drain()
                    for t in range(2):
                        ins = dve.bn_stats(st[j][:, t, :], h1[j][t])
                    dve.drain()
                    for t in range(2):
                        ins = dve.bn_aggr(mv[j][:, t, :], st[j][:, t, :])
                    ins.then_inc(mv1, 1)
                    dve.wait_ge(mv1, n[j])
                    dve.tensor_scalar_add(ve[j][:], mv[j][:, :, 1], LN_EPS).then_inc(ve1, 1)
                for j in range(2):
                    dve.wait_ge(rs1, n[j])
                    for t in range(2):
                        ins = dve.tensor_scalar(xn[j][:, t, 0:D], h1[j][t], mv[j][:, t, 0:1], rs[j][:, t:t + 1], ALU.subtract, ALU.mult)
                    ins.then_inc(xn1, 1)
                for j in range(2):
                    dve.wait_ge(kv_mm, n[j])
                    dve.tensor_scalar(kpos[j].rearrange("p t d -> p (t d)"), bank(j, 2)[:, 0:2 * D], 0.0, HD ** -0.5, ALU.max, ALU.add).then_inc(kset, 1)
                    dve.wait_ge(q_mm, n[j])
                    dve.tensor_scalar(qt[j].rearrange("p t c n -> p (t c n)"), bank(j, 0), 0.0, HD ** -0.5, ALU.max, ALU.add).then_inc(qset, 1)
                for j in range(2):
                    dve.wait_ge(kvi_mm, n[j])
                    for im in range(2):
                        ins = dve.tensor_tensor(kvm[j][:, 2 * im:2 * im + 2, :], bank(j, 2 + im)[:, 0:408].rearrange("p (i n) -> p i n", i=2),
                                      mask17.unsqueeze(1).to_broadcast([P, 2, 204]), ALU.mult)
                    ins.then_inc(kvm_set, 1)
                for j in range(2):
                    dve.wait_ge(o_mm, n[j])
                    o4 = bank(j, 1)[:, 0:408].rearrange("p (t h e) -> p t h e", t=2, h=NH)
                    dve.tensor_scalar_add(den[j][:], o4[:, :, :, 16], 1e-6).then_inc(den_e, 1)
                    dve.wait_ge(den_e, n[j])
                    dve.reciprocal(den[j][:], den[j][:]).then_inc(den_set, 1)
                    dve.wait_ge(den_set, n[j])
                    for t in range(2):
                        ins = dve.tensor_tensor(ao[j][:, t, 0:D].rearrange("p (h e) -> p h e", h=NH), o4[:, t, :, 0:16],
                                      den[j][:, t].unsqueeze(2).to_broadcast([P, NH, HD]), ALU.mult)
                    ins.then_inc(ao_set, 1)
                for j in range(2):
                    dve.wait_ge(pr_mm, n[j])
                    dve.tensor_tensor(ht[j], ht[j], bank(j, 2)[:, 0:2 * D].rearrange("p (t d) -> p t d", t=2), ALU.add).then_inc(h_attn, 1)
                dve.drain()
                normalised(A0, h1, n)
                for j in range(2):
                    dve.wait_ge(A0["lg_mm"], n[j])
                    dve.tensor_copy(glog[:, bass.ds(4 * it + 2 * j, 2), :], bank(j, 1)[:, 0:16].rearrange("p (t e) -> p t e", t=2)).then_inc(A0["lg"], 1)
            gv = "p t e -> p t e"
            dve.wait_ge(A0["lg"], DUOS)
            dve.tensor_scalar(gs[2], glog, 0.0, None, ALU.max)
            dve.drain()
            dve.wait_ge(A0["ln"], 1)
            dve.tensor_tensor(gs[3], gs[2], gs[1], ALU.add).then_inc(A0["sp"], 1)
            dve.wait_ge(A0["sq"], 1)
            dve.tensor_tensor(gs[0], gs[2], gbias.unsqueeze(1).to_broadcast([P, TILES, 8]), ALU.add)
            dve.drain()
            for t in range(TILES):
                other = gs[0][:, t].unsqueeze(1).to_broadcast([P, 8, 8])
                own = gs[0][:, t].unsqueeze(2).to_broadcast([P, 8, 8])
                dve.tensor_tensor(gpair[0][:, t], other, own, ALU.is_gt)
                dve.tensor_tensor(gpair[1][:, t], other, own, ALU.is_equal)
            dve.drain()
            dve.tensor_tensor(gpair[1].rearrange("p t a b -> p t (a b)"), gpair[1].rearrange("p t a b -> p t (a b)"), tri8.rearrange("p a b -> p (a b)").unsqueeze(1).to_broadcast([P, TILES, 64]), ALU.mult)
            dve.drain()
            dve.tensor_tensor(gpair[0], gpair[0], gpair[1], ALU.add)
            dve.drain()
            dve.tensor_reduce(gs[1], gpair[0], AX.X, ALU.add)
            dve.drain()
            dve.tensor_scalar(gs[1], gs[1], 1.5, None, ALU.is_lt)
            dve.drain()
            dve.tensor_tensor(gs[1], gs[1], gs[2], ALU.mult)
            dve.drain()
            dve.tensor_reduce(gsum, gs[1], AX.X, ALU.add)
            dve.drain()
            dve.tensor_scalar(gsum, gsum, 1e-6, None, ALU.max)
            dve.drain()
            dve.reciprocal(gsum, gsum)
            dve.drain()
            dve.tensor_tensor(comb[:, :, 0:8], gs[1], gsum.unsqueeze(2).to_broadcast([P, TILES, 8]), ALU.mult)
            dve.drain()
            dve.sem_inc(up_read, 2)
            dve.sem_inc(sil_free, 2)
            dve.sem_inc(y_added, 4)
            with dve.Fori(0, 3) as ie:
                for c in range(12):
                    for f in range(6):
                        q = 72 * ie + 6 * c + f
                        dve.wait_ge(u_mm, q + 1)
                        dve.tensor_scalar(upc[f % 2], banks[:, 2 + f % 2, 0:296], LIMIT, -LIMIT, ALU.min, ALU.max).then_inc(up_read, 1)
                        dve.wait_ge(up_read, q + 3)
                        dve.wait_ge(silu_set, q + 3)
                        dve.scalar_tensor_tensor(eh[c % 2][:, f, :, 0:NTOK], sil[f % 2].rearrange("p (i n) -> p i n", n=NTOK), SILU_LIMIT,
                                                 upc[f % 2].rearrange("p (i n) -> p i n", n=NTOK), ALU.min, ALU.mult).then_inc(eh_set, 1)
                        dve.wait_ge(eh_set, q + 1)
                        dve.sem_inc(sil_free, 1)
                    for t2 in range(2):
                        dve.wait_ge(y_mm, 24 * ie + 2 * c + t2 + 1)
                        for t in range(2):
                            tile = 4 * (c % 4) + 2 * t2 + t
                            hh = h[:, tile, :]
                            e = 3 * ie + c // 4
                            ins = dve.scalar_tensor_tensor(hh, banks[:, 4 + 2 * (c % 2) + t2, t * D:(t + 1) * D], comb[:, tile, bass.ds(e, 1)], hh, ALU.mult, ALU.add)
                        ins.then_inc(y_added, 1)
            dve.drain()

            dve.wait_ge(bw_mm, 1)
            for n0 in range(3):
                f = slice(452 * n0, 452 * n0 + 452)
                dve.tensor_tensor(w_f1[64:68, 1, f], w_f1[64:68, 1, f], banks[64:68, 4 + n0, 0:452], ALU.add)
            dve.tensor_scalar(w_f1[:, 0, :], w_f1[:, 0, :], gb[:, 0, 0:1], None, ALU.mult)
            dve.tensor_scalar(w_f1[0:64, 1, :], w_f1[0:64, 1, :], gb[0:64, 1, 0:1], None, ALU.mult).then_inc(bw_set, 1)

            def attention(a, n, masked):
                for j in range(2):
                    dve.wait_ge(a["v_mm"], n[j])
                    for im in range(2):
                        ins = dve.tensor_tensor(vx[j][:, 2 * im:2 * im + 2, :].rearrange("p t (g e) -> p (t g) e", g=4),
                                      bank(j, 3 - 3 * im)[0:111, 0:408].rearrange("p (g e) -> p g e", e=51),
                                      m_v.unsqueeze(1).to_broadcast([111, 8, 51]), ALU.mult)
                    ins.then_inc(a["vx"], 1)
                for j in range(2):
                    dve.wait_ge(a["s_mm"], n[j])
                    s2 = banks[:, 4 * j + 1:4 * j + 3, 0:444].rearrange("p t (h n) -> p t h n", h=12)
                    if masked:
                        for t in range(2):
                            dve.tensor_tensor(sc[j][:, t], s2[:, t], m_causal.unsqueeze(1).to_broadcast([P, 12, NTOK]), ALU.add)
                        dve.drain()
                        s2 = sc[j]
                    dve.tensor_reduce(mx[j], s2, AX.X, ALU.max).then_inc(a["mx"], 1)
                    dve.wait_ge(a["mx"], n[j])
                    for t in range(2):
                        ins = dve.tensor_tensor(sc[j][:, t], s2[:, t], mx[j][:, t].unsqueeze(2).to_broadcast([P, 12, NTOK]), ALU.subtract)
                    ins.then_inc(a["sub"], 1)
                for j in range(2):
                    dve.wait_ge(a["o_mm"], n[j])
                    o4 = bank(j, 1)[:, 0:408].rearrange("p (t h e) -> p t h e", t=2, h=NH)
                    dve.reciprocal(den[j], o4[:, :, :, 16]).then_inc(a["rden"], 1)
                    dve.wait_ge(a["rden"], n[j])
                    for t in range(2):
                        ins = dve.tensor_tensor(ao[j][:, t, 0:D].rearrange("p (h e) -> p h e", h=NH), o4[:, t, :, 0:16],
                                      den[j][:, t].unsqueeze(2).to_broadcast([P, NH, HD]), ALU.mult)
                    ins.then_inc(a["ao"], 1)

            dve.drain()
            with dve.Fori(0, DUOS // 2) as it:
                n = [2 * it + 1, 2 * it + 2]
                ht, h1 = h_tiles(it)
                normalised(A1, h1, n)
                attention(A1, n, True)
                for j in range(2):
                    dve.wait_ge(A1["pr_mm"], n[j])
                    dve.tensor_tensor(ht[j], ht[j], bank(j, 3)[:, 0:2 * D].rearrange("p (t d) -> p t d", t=2), ALU.add).then_inc(A1["h"], 1)

            dve.drain()
            with dve.Fori(0, DUOS // 2) as it:
                n = [2 * it + 1, 2 * it + 2]
                ht, h1 = h_tiles(it)
                normalised(A2, h1, n)
                for j in range(2):
                    dve.wait_ge(A2["xn"], n[j])
                    for t in range(2):
                        dve.bn_stats(st[j][:, t, :], xn[j][:, t, 0:D])
                    dve.drain()
                    for t in range(2):
                        dve.bn_aggr(mv[j][:, t, :], st[j][:, t, :])
                    dve.drain()
                    dve.tensor_scalar_add(ve[j], mv[j][:, :, 1], EPS2).then_inc(A2["ve2"], 1)
                    dve.tensor_tensor(ht[j], ht[j], xn[j][:, :, 0:D], ALU.add).then_inc(A2["hx"], 1)
                for j in range(2):
                    dve.wait_ge(A2["lg_mm"], n[j])
                    l2 = bank(j, 1)[:, 0:8].rearrange("p (t e) -> p t e", t=2)
                    dve.tensor_reduce(l1s[j], l2, AX.X, ALU.max).then_inc(A2["lgmx"], 1)
                    dve.wait_ge(A2["lgmx"], n[j])
                    dve.tensor_tensor(lg[j], l2, l1s[j].unsqueeze(2).to_broadcast([P, 2, 4]), ALU.subtract).then_inc(A2["lgsub"], 1)
                for j in range(2):
                    dve.wait_ge(A2["lgexp"], n[j])
                    dve.tensor_reduce(l1s[j], pr[j], AX.X, ALU.add).then_inc(A2["lgsum"], 1)
                    dve.wait_ge(A2["lgsum"], n[j])
                    dve.reciprocal(l1s[j], l1s[j]).then_inc(A2["lgrec"], 1)
                    dve.wait_ge(A2["lgrec"], n[j])
                    dve.tensor_tensor(pr[j], pr[j], l1s[j].unsqueeze(2).to_broadcast([P, 2, 4]), ALU.mult).then_inc(A2["p"], 1)
                    dve.wait_ge(A2["p"], n[j])
                    dve.tensor_tensor(dg[j].rearrange("p t e n -> p (t e) n"), eye37.unsqueeze(1).to_broadcast([P, 8, NTOK]),
                                      pr[j].rearrange("p t e -> p (t e)").unsqueeze(2).to_broadcast([P, 8, NTOK]), ALU.mult).then_inc(A2["dg"], 1)
                for j in range(2):
                    dve.wait_ge(A2["bc_mm"], n[j])
                    others = bank(j, 2)[:, 0:296].rearrange("p (e n) -> p e n", n=NTOK)
                    own = pr[j].rearrange("p t e -> p (t e)").unsqueeze(2).to_broadcast([P, 8, NTOK])
                    g3 = gt[j].rearrange("p t e n -> p (t e) n")
                    e3 = eq[j].rearrange("p t e n -> p (t e) n")
                    dve.tensor_tensor(g3, others, own, ALU.is_gt)
                    dve.tensor_tensor(e3, others, own, ALU.is_equal).then_inc(A2["cmp"], 1)
                    dve.wait_ge(A2["cmp"], n[j])
                    dve.tensor_tensor(e3, e3, tri.unsqueeze(1).to_broadcast([P, 8, NTOK]), ALU.mult)
                    dve.drain()
                    dve.tensor_tensor(g3, g3, e3, ALU.add).then_inc(A2["cmp2"], 1)
                    dve.wait_ge(A2["cmp2"], n[j])
                    dve.tensor_reduce(rank[j].rearrange("p t e -> p (t e)"), g3, AX.X, ALU.add).then_inc(A2["rank"], 1)
                    dve.wait_ge(A2["rank"], n[j])
                    dve.tensor_scalar(sg[j][:, 0], rank[j], CAP - 0.5, None, ALU.is_lt)
                    dve.drain()
                    dve.tensor_tensor(sg[j][:, 1], sg[j][:, 0], pr[j], ALU.mult)
                    dve.drain()
                    for e in (2, 1, 0):
                        dve.tensor_tensor(sg[j][:, :, :, e], sg[j][:, :, :, e], sg[j][:, :, :, e + 1], ALU.add)
                        dve.drain()
                    dve.wait_ge(A2["rs2"], n[j])
                    dve.tensor_tensor(rsr[j], sg[j][:, 0], rs[j].unsqueeze(2).to_broadcast([P, 2, 4]), ALU.mult).then_inc(A2["rsr"], 1)
                    dve.wait_ge(A2["rsr"], n[j])
                    for t in range(2):
                        for r, (a0, a1) in enumerate(RNG):
                            dve.tensor_scalar(yn[j][:, t, a0:a1], xn[j][:, t, a0:a1], mv[j][:, t, 0:1], rsr[j][:, t, r:r + 1], ALU.subtract, ALU.mult)
                    dve.tensor_copy(yn[j][:, :, 192:196], sg[j][:, 0]).then_inc(A2["yn"], 1)
                attention(A2, n, False)
                for j in range(2):
                    dve.wait_ge(A2["fc_mm"], n[j])
                    for r, (a0, a1) in enumerate(RNG):
                        dve.tensor_tensor(zz[j][:, :, a0:a1], bank(j, 3)[:, 0:2 * D].rearrange("p (t d) -> p t d", t=2)[:, :, a0:a1],
                                          sg[j][:, 1, :, r:r + 1].to_broadcast([P, 2, a1 - a0]), ALU.mult)
                    dve.drain()
                    dve.tensor_tensor(ht[j], ht[j], zz[j], ALU.add).then_inc(A2["h"], 1)


def two_chunks(w):
    a = np.zeros((256, w.shape[1]), w.dtype)
    a[:w.shape[0]] = w
    return np.ascontiguousarray(a.reshape(2, 128, -1).transpose(1, 0, 2))


def qkv17(w, rows, ones_row):
    a = two_chunks(w.T)
    for r, v in rows.items():
        a[r, 1] = v
    v17 = np.zeros((P, 2, NH, 17), w.dtype)
    v17[..., :16] = a[:, :, 2 * D:].reshape(P, 2, NH, HD)
    v17[ones_row, 1, :, 16] = 1
    return np.concatenate([a[:, :, :2 * D], v17.reshape(P, 2, -1)], 2)


def kernel(**inputs):
    import concourse.bacc as _bacc
    from concourse.bass_utils import run_bass_kernel_spmd as _run
    x = np.asarray(inputs["x"])
    g = {k: np.asarray(v) for k, v in inputs.items()}
    pt = x.reshape(NIMG, 6, 16, 6, 16, 3).transpose(0, 1, 3, 2, 4, 5).reshape(NIMG, 36, 6, 128)
    xp = np.zeros((NIMG, SLOT, 6, 128), x.dtype)
    xp[:, 1:37] = pt
    xp = np.ascontiguousarray(xp.reshape(DUOS, 4 * SLOT, 6, 128).transpose(0, 3, 2, 1))
    pos = np.zeros((2, SLOT, D), x.dtype)
    pos[:, :NTOK] = g["L0_tok_pos_embedding"]
    oh = np.zeros((2, 2, SLOT), np.float32)
    oh[0, :, 0] = 1
    oh[1, :, 1:NTOK] = 1
    addrows = np.stack([g["L0_tok_cls_token"].reshape(D), g["L0_tok_b_proj"]])
    m17 = np.zeros((P, NH, 17), np.float32)
    for e in range(P):
        m17[e, :8][np.arange(8) == e // 16] = 1
        if e >= 64:
            m17[e, 8:][np.arange(8, 12) == (e + 64) // 16] = 1
    def experts(name):
        w = np.concatenate([g[f"L0_ffn_{name}"], g[f"L0_ffn_{name}s"][None]])
        return np.stack([two_chunks(a) for a in w])

    i, jj = np.arange(NTOK)[:, None], np.arange(NTOK)[None, :]
    mask = np.where(((jj % 8 == 0) & (jj <= i)) | (jj == i) | (jj == i - 1), 0, -1e30).astype(np.float32)
    pad = np.zeros((SLOT - NTOK, NTOK), np.float32)
    kmask = m17[:, :, 0]
    vmask = np.zeros((3, NTOK, 3, 17), np.float32)
    for k in range(3):
        vmask[k, :, k] = 1
    rng = np.zeros((D, 4), np.float32)
    for k, (a0, a1) in enumerate(RNG):
        rng[a0:a1, k] = 1
    same = np.zeros((2, SLOT, 2, SLOT), np.float32)
    for k in range(2):
        same[k, :, k] = 1
    same = same.reshape(P, P)
    ffn_w1 = np.concatenate([two_chunks(g["L1_ffn_w1"][:MLP].T), qkv17(g["L1_ffn_w1"][MLP:], {64: g["L1_ffn_b1"][MLP:]}, 68)], 2)
    ffn_w1[64, 1, :MLP] = g["L1_ffn_b1"][:MLP]
    w2 = np.zeros((1024, 2 * D), np.float32)
    w2[:960] = g["L1_ffn_w2"].T
    w2[960] = g["L1_ffn_b2"]
    arrays = {
        "x_patches": xp, "tok_w": g["L0_tok_W_proj"].reshape(6, 128, D).transpose(1, 0, 2), "tok_pos": pos.reshape(P, D),
        "tok_onehot": oh.reshape(2, P), "tok_addrows": addrows, "l0_qkv": two_chunks(g["L0_attn_qkv_w"].T),
        "l0_proj": two_chunks(np.concatenate([g["L0_attn_proj_w"].T, g["L0_attn_proj_b"][None]])),
        "l1_w": qkv17(g["L1_attn_qkv_w"], {64: g["L1_attn_qkv_b"]}, 64),
        "l1_out": two_chunks(np.concatenate([g["L1_attn_out_w"].T, g["L1_attn_out_b"][None]])),
        "l1_mask": np.concatenate([mask, pad] * 2), "kmask": kmask, "vmask": vmask.reshape(3 * NTOK, 51),
        "ffn_w1": ffn_w1, "ffn_w2": w2.reshape(8, P, 2, D).transpose(1, 0, 2, 3), "ffn_router": two_chunks(g["L1_ffn_w_router"].T),
        "ffn_gb": two_chunks(np.stack([g["L1_ffn_gamma1"], g["L1_ffn_beta1"]], 1)), "ffn_ranges": two_chunks(rng),
        "slot_eye": np.concatenate([np.eye(NTOK, dtype=np.float32), pad] * 2), "same_image": same,
        "earlier": np.concatenate([np.tril(np.ones((NTOK, NTOK), np.float32), -1), pad] * 2),
        "moe_w1": experts("w1"), "moe_w3": experts("w3"), "gate_w": two_chunks(g["L0_ffn_gate_w"]),
        "moe_w2": np.concatenate([g["L0_ffn_w2"], g["L0_ffn_w2s"][None]]).reshape(9, 6, P, D).transpose(0, 2, 1, 3),
        "gate_bias": np.tile(g["L0_ffn_gate_bias"], (P, 1)), "before8": np.tile(np.tril(np.ones((8, 8), np.float32), -1), (P, 1, 1)),
        "ident_in": np.eye(P, dtype=np.float32), "hmask17": m17.reshape(P, 204),
    }
    arrays = {k: np.ascontiguousarray(v) for k, v in arrays.items()}
    nc = _bacc.Bacc("TRN2", target_bir_lowering=False, num_devices=1)
    args = {k: nc.dram_tensor(k + "_dram", v.shape, mybir.dt.from_np(v.dtype), kind="ExternalInput").ap() for k, v in arrays.items()}
    out = nc.dram_tensor("out_dram", (NIMG, NTOK, D), F32, kind="ExternalOutput").ap()
    vit(nc, out=out, **args)
    r = _run(nc, [{k + "_dram": v for k, v in arrays.items()}], core_ids=[0])
    return r.results[0]["out_dram"]
```

```python
import numpy as np
import concourse.bass as bass
from concourse import mybir
from contextlib import ExitStack

F32 = mybir.dt.float32
F16 = mybir.dt.float16
I32 = mybir.dt.int32
ALU = mybir.AluOpType
ACT = mybir.ActivationFunctionType
AX = mybir.AxisListType

P = 128
SLOT = 64
NIMG, NTOK, D, NH, HD = 32, 37, 192, 12, 16
TILES = NIMG // 2
DUOS = TILES // 2
LN_EPS = 1e-5
EPS2 = 1e-6
QKV17 = 2 * D + NH * 17
MLP = 768
FFN = 768
LIMIT = 10.0
SILU_LIMIT = LIMIT / (1 + float(np.exp(-LIMIT)))
CAP = NTOK // 2
EXPERTS, TOPK = 8, 2
SHARED_TILES = -(-NIMG * NTOK // P)
ROUTED_TILES = (NIMG * NTOK * TOPK - EXPERTS) // P + EXPERTS
MTILES = SHARED_TILES + ROUTED_TILES
SPARE_ROWS = MTILES * P
XSCALE, WSCALE = 16.0, 16.0
UNITS = 6
RNG = ((0, 24), (24, 48), (48, 96), (96, 192))


class Place:

    def __init__(self, nc, start):
        self.nc, self.at = nc, start

    def take(self, name, shape, dt=F32):
        size = {F32: 4, I32: 4, F16: 2}[dt]
        for n in shape[1:]:
            size *= n
        t = self.nc.alloc_sbuf_tensor_at(name, shape, dt, offset=self.at)[tuple(slice(None) for _ in shape)]
        self.at += -(-size // 32) * 32
        return t


def vit(nc, x_patches, tok_w, tok_pos, tok_onehot, tok_addrows, l0_qkv, l0_proj, ident_in, hmask17,
        moe_13, moe_2, gate_w, gate_bias, before8, route_c, lt_in, ones_in,
        l1_w, l1_out, l1_mask, kmask, vmask, ffn_w1, ffn_w2, ffn_router, ffn_gb, ffn_ranges, slot_eye, same_image, earlier, out):
    xs = nc.dram_tensor("moe_rows_in", [SPARE_ROWS + TOPK * TILES * P, 2 * D], F16).ap()
    ys = nc.dram_tensor("moe_rows_out", [MTILES * P, D], F32).ap()
    with ExitStack() as ctx:
        def sem(name):
            return ctx.enter_context(nc.semaphore(name))

        banks = ctx.enter_context(nc.psum_tensor("banks", [P, 8, 512], F32))[:, :, :]
        keep = Place(nc, -(-nc.sbuf_base // 32) * 32)
        ident = keep.take("ident", [P, P])
        ident16 = keep.take("ident16", [P, P], F16)
        pos_bias = keep.take("pos_bias", [P, D])
        onehot = keep.take("onehot", [2, P])
        addrows = keep.take("addrows", [2, D])
        mask17 = keep.take("mask17", [P, 204])
        neghalf = keep.take("neghalf", [P, 2])
        m_causal = keep.take("m_causal", [P, NTOK])
        m_k = keep.take("m_k", [P, 12])
        m_v = keep.take("m_v", [3 * NTOK, 51])
        w_g = keep.take("w_g", [P, 2, 8])
        h = keep.take("h", [P, TILES, D])
        rows16 = keep.take("rows16", [P, TILES, 2 * D], F16)
        shared_y = rows16.bitcast(F32)
        xn = [keep.take(f"xn{j}", [P, 2, 256]) for j in range(2)]
        xc = [keep.take(f"xc{j}", [P, 2, 4 * SLOT]) for j in range(2)]
        ao = [keep.take(f"ao{j}", [P, 2, 256]) for j in range(2)]
        den = [keep.take(f"den{j}", [P, 2, NH]) for j in range(2)]
        st = [keep.take(f"st{j}", [P, 2, 6]) for j in range(2)]
        mv = [keep.take(f"mv{j}", [P, 2, 2]) for j in range(2)]
        ve = [keep.take(f"ve{j}", [P, 2]) for j in range(2)]
        rs = [keep.take(f"rs{j}", [P, 2]) for j in range(2)]
        glog = keep.take("glog", [P, TILES, EXPERTS])
        wk = keep.take("wk", [P, TOPK, TILES])
        gather_at = keep.take("gather_at", [P, TOPK, TILES], I32)
        scatter_at = keep.take("scatter_at", [P, TOPK, TILES], I32)
        tile_expert = keep.take("tile_expert", [1, MTILES], I32)

        ex = Place(nc, keep.at)
        w13 = ex.take("w13", [P, 9, 2, 3, FFN], F16)
        w2r = ex.take("w2r", [P, 9, 6, 2, D], F16)
        la = Place(nc, keep.at)
        got = la.take("got", [P, TOPK, TILES, D])
        w_f1 = la.take("w_f1", [P, 2, MLP + QKV17])
        w_f2 = la.take("w_f2", [P, 8, 2, D])
        w_f2s = la.take("w_f2s", [P, 8, D])
        w_r = la.take("w_r", [P, 2, 4])
        gb = la.take("gb", [P, 2, 2])
        ranges = la.take("ranges", [P, 2, 4])
        beta4 = la.take("beta4", [P, 2, 4])
        eye37 = la.take("eye37", [P, NTOK])
        samei = la.take("samei", [P, P])
        tri = la.take("tri", [P, NTOK])
        xr = [la.take(f"xr{j}", [P, 2, 4, 3 * NTOK]) for j in range(2)]
        kc = [la.take(f"kc{j}", [P, 2, 4, NTOK]) for j in range(2)]
        kx = [la.take(f"kx{j}", [P, 4, 12 * NTOK]) for j in range(2)]
        sc = [la.take(f"sc{j}", [P, 2, 12, NTOK]) for j in range(2)]
        vx = [la.take(f"vx{j}", [3 * NTOK, 4, 204]) for j in range(2)]
        mx = [la.take(f"mx{j}", [P, 2, 12]) for j in range(2)]
        lg = [la.take(f"lg{j}", [P, 2, 4]) for j in range(2)]
        pr = [la.take(f"pr{j}", [P, 2, 4]) for j in range(2)]
        l1s = [la.take(f"l1s{j}", [P, 2]) for j in range(2)]
        rank = [la.take(f"rank{j}", [P, 2, 4]) for j in range(2)]
        sg = [la.take(f"sg{j}", [P, 2, 2, 4]) for j in range(2)]
        rsr = [la.take(f"rsr{j}", [P, 2, 4]) for j in range(2)]
        dg = [la.take(f"dg{j}", [P, 2, 4, NTOK]) for j in range(2)]
        gt = [la.take(f"gt{j}", [P, 2, 4, NTOK]) for j in range(2)]
        eq = [la.take(f"eq{j}", [P, 2, 4, NTOK]) for j in range(2)]
        qp = [la.take(f"qp{j}", [P, 2, 4, SLOT]) for j in range(2)]
        assert la.at <= ex.at

        sp1 = Place(nc, ex.at)
        stage = [sp1.take(f"stage{r}", [P, FFN]) for r in range(3)]
        sp2 = Place(nc, ex.at)
        w_l1 = sp2.take("w_l1", [P, 2, QKV17])
        w_l1o = sp2.take("w_l1o", [P, 2, D])
        assert sp2.at <= sp1.at

        p1 = Place(nc, sp1.at)
        w_tok = p1.take("w_tok", [P, 6, D])
        w_qkv0 = p1.take("w_qkv0", [P, 2, 3 * D])
        w_proj0 = p1.take("w_proj0", [P, 2, D])
        patches = [p1.take(f"patches{t}", [P, 6, P]) for t in range(2)]
        kpos = [p1.take(f"kpos{j}", [P, 2, D]) for j in range(2)]
        v17 = [p1.take(f"v17{j}", [P, 2, NH, 17]) for j in range(2)]
        qt = [p1.take(f"qt{j}", [P, 2, 2 * P]) for j in range(2)]
        kvm = [p1.take(f"kvm{j}", [P, 4, 204]) for j in range(2)]
        p2 = Place(nc, sp1.at)
        gbias = p2.take("gbias", [P, 8])
        tri8 = p2.take("tri8", [P, 8, 8])
        route = p2.take("route", [P, 1 + TOPK * TILES + 10 + ROUTED_TILES])
        lt = p2.take("lt", [P, P])
        ones = p2.take("ones", [P, P])
        gs = [p2.take(f"gs{k}", [P, TILES, 8]) for k in range(3)]
        gr = [p2.take(f"gr{k}", [P, TILES, 8]) for k in range(4)]
        gpair = [p2.take(f"gpair{k}", [P, TILES, 64]) for k in range(2)]
        gsum = p2.take("gsum", [P, TILES])
        sel = p2.take("sel", [P, TILES + 1, 8])
        cnt = p2.take("cnt", [P, 4, 8])
        slotf = p2.take("slotf", [P, TOPK, TILES])
        cmpt = p2.take("cmpt", [P, ROUTED_TILES * 8])
        eidf = p2.take("eidf", [P, ROUTED_TILES])
        xg = [p2.take(f"xg{k}", [P, 2 * D], F16) for k in range(2)]
        xt16 = [p2.take(f"xt16{k}", [P, 4, P], F16) for k in range(2)]
        sil = [p2.take(f"sil{g}", [P, 3 * P]) for g in range(2)]
        upc = [p2.take(f"upc{g}", [P, 3 * P]) for g in range(2)]
        h32 = [p2.take(f"h32{g}", [P, 3 * P]) for g in range(2)]
        eh = [p2.take(f"eh{k}", [P, 2, 6, P], F16) for k in range(2)]
        ysb = [p2.take(f"ysb{k}", [P, D]) for k in range(2)]
        zrow = p2.take("zrow", [P, 2 * D], F16)
        p3 = Place(nc, sp1.at)
        pt = [p3.take(f"pt{j}", [3 * NTOK, 2, 4, P]) for j in range(2)]
        hid = [p3.take(f"hid{j}", [P, 6, 4, SLOT]) for j in range(2)]
        yn = [p3.take(f"yn{j}", [P, 2, 256]) for j in range(2)]
        assert max(p1.at, p2.at, p3.at) <= nc.sbuf_usable_end, (p1.at, p2.at, p3.at, nc.sbuf_usable_end)
        zz = [xn[j][:, :, 0:D] for j in range(2)]

        w_in = sem("w_in"); c1_in = sem("c1_in"); c2_in = sem("c2_in"); r_in = sem("r_in")
        patches_in = [sem("patches_in0"), sem("patches_in1")]
        consts_set = sem("consts_set"); consts2_set = sem("consts2_set"); zrow_set = sem("zrow_set"); zeroed = sem("zeroed")
        posb_mm = sem("posb_mm"); posb_set = sem("posb_set"); tok_mm = sem("tok_mm")
        ve1 = sem("ve1"); rs1 = sem("rs1"); xn1 = sem("xn1")
        xt1_mm = sem("xt1_mm"); xt1 = sem("xt1")
        kv_mm = sem("kv_mm"); kset = sem("kset"); vset = sem("vset")
        q_mm = sem("q_mm"); qset = sem("qset")
        kvi_mm = sem("kvi_mm"); kvm_set = sem("kvm_set")
        o_mm = sem("o_mm"); den_e = sem("den_e"); den_set = sem("den_set"); ao_set = sem("ao_set")
        at_mm = sem("at_mm"); at_set = sem("at_set")
        pr_mm = sem("pr_mm"); h_attn = sem("h_attn")
        stage_in = [sem(f"stage_in{r}") for r in range(3)]
        high_set = sem("high_set"); stage_free = sem("stage_free")
        rows_hi = sem("rows_hi"); rows_set = sem("rows_set"); rows_out = sem("rows_out")
        A0 = {n: sem("g_" + n) for n in "ve rs xn xt_mm xt lg_mm lg abs exp ln sp sq".split()}
        sel_set = sem("sel_set"); count_mm = sem("count_mm"); routed = sem("routed"); scattered = sem("scattered")
        M = {n: sem("m_" + n) for n in "xt_mm xt gate_mm up_mm silu clip h hi lo y_mm y".split()}
        xg_in = [sem("xg_in0"), sem("xg_in1")]
        y_out = [sem("y_out0"), sem("y_out1")]
        sy_zero = sem("sy_zero"); sy_in = sem("sy_in"); h_shared = sem("h_shared")
        gathered = [sem("gathered0"), sem("gathered1")]
        h_moe = sem("h_moe")
        NAMES = "xr ve rs xn xt_mm xt q_mm k_mm q k kx v_mm vx s_mm mx sub e pt_mm pt o_mm rden ao at_mm at pr_mm h".split()
        A1 = {n: sem("l1_" + n) for n in NAMES}
        A2 = {n: sem("f_" + n) for n in NAMES + "lg_mm lgmx lgsub lgexp lgsum lgrec p dg bc_mm cmp cmp2 rank ve2 rs2 rsr yn yt_mm yt mlp_mm gelu fc_mm hx".split()}
        beta4_set = sem("beta4_set"); bw_mm = sem("bw_mm"); bw_set = sem("bw_set"); w2_set = sem("w2_set")
        out_done = sem("out_done")

        block = ctx.enter_context(nc.Block())
        first = ((ident, ident_in), (onehot, tok_onehot), (addrows, tok_addrows), (pos_bias, tok_pos), (w_tok, tok_w), (mask17, hmask17),
                 (w_qkv0, l0_qkv), (w_proj0, l0_proj), (w_g, gate_w), (m_causal, l1_mask), (m_k, kmask), (m_v, vmask))
        second = ((gbias, gate_bias), (tri8, before8), (route, route_c), (lt, lt_in), (ones, ones_in))
        third = ((w_l1, l1_w), (w_l1o, l1_out))
        fourth = ((w_f1, ffn_w1), (w_f2, ffn_w2), (w_r, ffn_router), (gb, ffn_gb), (ranges, ffn_ranges), (eye37, slot_eye), (samei, same_image), (tri, earlier))

        def bank(j, n):
            return banks[:, 4 * j + n]

        def stage_source(e, u):
            return moe_13[e, u] if u < 4 else moe_2[e, u - 4]

        def routed_rows(k):
            return xs[bass.ds(P * k, P), :]

        @block.sync
        def _(sp):
            for dst, src in first:
                sp.dma_start(dst, src).then_inc(w_in, 16)
            def load_stage(e, u):
                if u < 4:
                    src, dst = moe_13.rearrange("e u p f -> (e u) p f")[bass.ds(4 * e + u, 1)].rearrange("o p f -> (o p) f"), stage[u % 3]
                else:
                    src, dst = moe_2.rearrange("e u p f -> (e u) p f")[bass.ds(2 * e + u - 4, 1)].rearrange("o p f -> (o p) f"), stage[u % 3][:, 0:3 * D]
                sp.dma_start(dst, src).then_inc(stage_in[u % 3], 16)

            for u in range(3):
                load_stage(0, u)
            with sp.Fori(0, 4) as it:
                for q in range(12):
                    sp.wait_ge(stage_free, 12 * it + q + 1)
                    load_stage(2 * it + (q + 3) // UNITS, (q + 3) % UNITS)
            for u in range(3, UNITS):
                sp.wait_ge(stage_free, 48 + u - 2)
                load_stage(8, u)
            sp.wait_ge(h_attn, DUOS)
            for dst, src in second:
                sp.dma_start(dst, src).then_inc(r_in, 16)
            sp.wait_ge(zrow_set, 1)
            fill = xs[NIMG * NTOK:SHARED_TILES * P]
            sp.dma_start(fill, zrow[0:SHARED_TILES * P - NIMG * NTOK]).then_inc(zeroed, 16)
            sp.dma_start(xs[SHARED_TILES * P:SPARE_ROWS].rearrange("(n p) f -> p n f", p=P),
                         zrow.unsqueeze(1).to_broadcast([P, ROUTED_TILES, 2 * D])).then_inc(zeroed, 16)
            sp.wait_ge(stage_free, 54)
            for dst, src in third:
                sp.dma_start(dst, src).then_inc(c1_in, 16)

            def load_rows(k, par):
                sp.dma_start(xg[par], routed_rows(k)).then_inc(xg_in[par], 16)

            def store_rows(k, par):
                sp.wait_ge(M["y"], k + 1)
                sp.dma_start(ys[bass.ds(P * k, P), :], ysb[par]).then_inc(y_out[par], 16)

            sp.wait_ge(rows_out, 32 * DUOS)
            sp.wait_ge(zeroed, 32)
            load_rows(0, 0)
            load_rows(1, 1)
            sp.wait_ge(M["xt_mm"], 1)
            load_rows(2, 0)
            sp.wait_ge(M["xt_mm"], 2)
            load_rows(3, 1)
            store_rows(0, 0)
            with sp.Fori(0, 3) as it:
                for par in range(2):
                    sp.wait_ge(M["xt_mm"], 2 * it + par + 3)
                    load_rows(2 * it + par + 4, par)
                    store_rows(2 * it + par + 1, 1 - par)
            sp.wait_ge(scattered, 16 * TOPK * TILES)
            with sp.Fori(0, 13) as it:
                for par in range(2):
                    sp.wait_ge(M["xt_mm"], 2 * it + par + 9)
                    load_rows(2 * it + par + 10, par)
                    store_rows(2 * it + par + 7, 1 - par)
            store_rows(33, 1)
            store_rows(34, 0)
            store_rows(35, 1)
            sp.wait_ge(M["y_mm"], MTILES)
            for dst, src in fourth:
                sp.dma_start(dst, src).then_inc(c2_in, 16)
            sp.wait_ge(A2["h"], DUOS)
            for im in range(2):
                o = out.rearrange("(t i) n d -> i n t d", i=2)[im]
                sp.dma_start(o, h[SLOT * im:SLOT * im + NTOK, :, :]).then_inc(out_done, 16)
            sp.wait_ge(out_done, 32)

        @block.gpsimd
        def _(pool):
            pool.memset(neghalf, -0.5)
            pool.memset(tile_expert, 0)
            for j in range(2):
                pool.memset(xn[j][:, :, 192:193], 1.0)
                pool.memset(xn[j][:, :, 193:256], 0.0)
                pool.memset(ao[j][:, :, 192:193], 1.0)
                pool.memset(ao[j][:, :, 193:256], 0.0)
                ins = pool.memset(v17[j][:, :, :, 16:17], 1.0)
            ins.then_inc(consts_set, 1)
            pool.wait_ge(consts_set, 1)

            def load_patches(tile, t):
                pool.dma_start(patches[t], x_patches[bass.ds(tile, 1)].rearrange("o p c n -> (o p) c n")).then_inc(patches_in[t], 16)

            load_patches(0, 0)
            load_patches(1, 1)

            def phase_a(it, more):
                for j in range(2):
                    for t in range(2):
                        if more or j == 0:
                            pool.wait_ge(tok_mm, 4 * it + 2 * j + t + 1)
                            load_patches(4 * it + 2 * j + t + 2, t)
                    pool.wait_ge(ve1, 2 * it + j + 1)
                    pool.tensor_tensor(rs[j], ve[j], neghalf, ALU.pow).then_inc(rs1, 1)
                for j in range(2):
                    pool.wait_ge(A0["ve"], 2 * it + j + 1)
                    pool.tensor_tensor(rs[j], ve[j], neghalf, ALU.pow).then_inc(A0["rs"], 1)
                for j in range(2):
                    pool.wait_ge(rows_set, 2 * it + j + 1)
                    for im in range(2):
                        pool.dma_start(xs[0:NIMG * NTOK].rearrange("(t i n) f -> i n t f", i=2, n=NTOK)[im][:, bass.ds(4 * it + 2 * j, 2), :],
                                       rows16[SLOT * im:SLOT * im + NTOK, bass.ds(4 * it + 2 * j, 2), :]).then_inc(rows_out, 16)

            with pool.Fori(0, DUOS // 2 - 1) as it:
                phase_a(it, True)
            phase_a(DUOS // 2 - 1, False)
            pool.wait_ge(h_attn, DUOS)
            pool.memset(zrow, 0.0).then_inc(zrow_set, 1)
            pool.wait_ge(routed, 1)
            pool.wait_ge(zeroed, 32)
            for k in range(TOPK):
                for t in range(TILES):
                    pool.indirect_dma_start(out=xs, out_offset=bass.IndirectOffsetOnAxis(ap=scatter_at[:, k, t:t + 1], axis=0),
                                            in_=rows16[:, t, :], in_offset=None).then_inc(scattered, 16)
            pool.wait_ge(scattered, 16 * TOPK * TILES)
            pool.wait_ge(rows_out, 32 * DUOS)
            pool.memset(shared_y, 0.0).then_inc(sy_zero, 1)
            pool.wait_ge(sy_zero, 1)
            for par in range(2):
                pool.wait_ge(y_out[par], 16 * SHARED_TILES // 2)
            for im in range(2):
                pool.dma_start(shared_y[SLOT * im:SLOT * im + NTOK, :, :],
                               ys[0:NIMG * NTOK].rearrange("(t i n) d -> i n t d", i=2, n=NTOK)[im]).then_inc(sy_in, 16)
            for par in range(2):
                pool.wait_ge(y_out[par], 16 * MTILES // 2)
            pool.wait_ge(M["y_mm"], MTILES)
            for t in range(TILES):
                for k in range(TOPK):
                    pool.indirect_dma_start(out=got[:, k, t, :], out_offset=None, in_=ys,
                                            in_offset=bass.IndirectOffsetOnAxis(ap=gather_at[:, k, t:t + 1], axis=0)).then_inc(gathered[t // 8], 16)
            for j in range(2):
                pool.memset(qp[j], 0.0)
                pool.memset(hid[j], 0.0)
                pool.memset(yn[j][:, :, 196:197], 1.0)
                ins = pool.memset(yn[j][:, :, 197:256], 0.0)
            ins.then_inc(consts2_set, 1)
            pool.wait_ge(c2_in, 16 * len(fourth))
            for c in range(2):
                ins = pool.tensor_tensor(beta4[:, c], ranges[:, c], gb[:, c, 1:2].to_broadcast([P, 4]), ALU.mult)
            ins.then_inc(beta4_set, 1)
            pool.tensor_tensor(w_f2s, w_f2[:, :, 0, :], w_f2[:, :, 1, :], ALU.add).then_inc(w2_set, 1)

            def kexp(a, it):
                for j in range(2):
                    pool.wait_ge(a["k"], 2 * it + j + 1)
                    for c, (h0, nh) in enumerate(((0, 8), (8, 4))):
                        for im in range(4):
                            ins = pool.tensor_tensor(kx[j][:, im, NTOK * h0:NTOK * (h0 + nh)].rearrange("p (h n) -> p h n", h=nh),
                                           kc[j][:, c, im].unsqueeze(1).to_broadcast([P, nh, NTOK]),
                                           m_k[:, h0:h0 + nh].unsqueeze(2).to_broadcast([P, nh, NTOK]), ALU.mult)
                    ins.then_inc(a["kx"], 1)

            with pool.Fori(0, DUOS // 2) as it:
                for j in range(2):
                    pool.wait_ge(A1["ve"], 2 * it + j + 1)
                    pool.tensor_tensor(rs[j], ve[j], neghalf, ALU.pow).then_inc(A1["rs"], 1)
                kexp(A1, it)
            with pool.Fori(0, DUOS // 2) as it:
                for j in range(2):
                    pool.wait_ge(A2["ve"], 2 * it + j + 1)
                    pool.tensor_tensor(rs[j], ve[j], neghalf, ALU.pow).then_inc(A2["rs"], 1)
                for j in range(2):
                    pool.wait_ge(A2["ve2"], 2 * it + j + 1)
                    pool.tensor_tensor(rs[j], ve[j], neghalf, ALU.pow).then_inc(A2["rs2"], 1)
                kexp(A2, it)

        @block.tensor
        def _(pe):
            def transposes(src, dst, ready, done, n):
                for j in range(2):
                    pe.wait_ge(ready, n[j])
                    for c in range(2):
                        for t in range(2):
                            mm = pe.transpose(bank(j, dst)[:, (2 * c + t) * P:(2 * c + t + 1) * P],
                                              src[j][:, t, c * P:(c + 1) * P], ident)
                    mm.then_inc(done, 1)

            pe.wait_ge(w_in, 16 * len(first))
            pe.matmul(bank(0, 0)[:, 0:D], onehot, addrows, start=True, stop=True).then_inc(posb_mm, 1)
            pe.wait_ge(posb_set, 1)
            with pe.Fori(0, DUOS // 2) as it:
                n = [2 * it + 1, 2 * it + 2]
                for j in range(2):
                    for t in range(2):
                        pe.wait_ge(patches_in[t], 32 * it + 16 * j + 16)
                        for c in range(6):
                            mm = pe.matmul(bank(j, 0)[:, t * D:(t + 1) * D], patches[t][:, c, :], w_tok[:, c, :], start=(c == 0), stop=(c == 5))
                        mm.then_inc(tok_mm, 1)
                transposes(xn, 1, xn1, xt1_mm, n)
                for j in range(2):
                    pe.wait_ge(xt1, n[j])
                    for b, f in ((2, slice(D, 2 * D)), (3, slice(2 * D, 3 * D))):
                        for t in range(2):
                            o = bank(j, b)[:, t * D:(t + 1) * D]
                            pe.matmul(o, xc[j][:, 0, P * t:P * t + P], w_qkv0[:, 0, f], start=True, stop=False)
                            mm = pe.matmul(o, xc[j][0:64, 1, P * t:P * t + P], w_qkv0[0:64, 1, f], start=False, stop=True)
                    mm.then_inc(kv_mm, 1)
                    for c in range(2):
                        f = slice(64 * c, 64 * c + P)
                        o = bank(j, 0)[:, 256 * c:256 * c + 256]
                        pe.matmul(o, w_qkv0[:, 0, f], xc[j][:, 0, :], start=True, stop=False)
                        mm = pe.matmul(o, w_qkv0[0:64, 1, f], xc[j][0:64, 1, :], start=False, stop=True)
                    mm.then_inc(q_mm, 1)
                for j in range(2):
                    pe.wait_ge(kset, n[j])
                    pe.wait_ge(vset, n[j])
                    for t in range(2):
                        for im in range(2):
                            r = slice(SLOT * im, SLOT * im + NTOK)
                            o = bank(j, 2 + im)[:, 204 * t:204 * t + 204]
                            vr = v17[j][r, t].rearrange("p h e -> p (h e)")
                            pe.matmul(o[:, 0:136], kpos[j][r, t, 0:P], vr[:, 0:136], start=True, stop=True)
                            mm = pe.matmul(o[:, 136:204], kpos[j][r, t, 64:192], vr[:, 136:204], start=True, stop=True)
                    mm.then_inc(kvi_mm, 1)
                for j in range(2):
                    pe.wait_ge(qset, n[j])
                    pe.wait_ge(kvm_set, n[j])
                    for t in range(2):
                        for im in range(2):
                            o = bank(j, 1)[SLOT * im:SLOT * im + SLOT, 204 * t:204 * t + 204]
                            q0 = P * t + SLOT * im
                            pe.matmul(o[:, 0:136], qt[j][:, 0, q0:q0 + SLOT], kvm[j][:, 2 * im + t, 0:136], start=True, stop=True)
                            mm = pe.matmul(o[:, 136:204], qt[j][:, 1, q0:q0 + SLOT], kvm[j][:, 2 * im + t, 136:204], start=True, stop=True)
                    mm.then_inc(o_mm, 1)
                transposes(ao, 0, ao_set, at_mm, n)
                for j in range(2):
                    pe.wait_ge(at_set, n[j])
                    for t in range(2):
                        o = bank(j, 2)[:, t * D:(t + 1) * D]
                        pe.matmul(o, xc[j][:, 0, P * t:P * t + P], w_proj0[:, 0, :], start=True, stop=False)
                        mm = pe.matmul(o, xc[j][0:65, 1, P * t:P * t + P], w_proj0[0:65, 1, :], start=False, stop=True)
                    mm.then_inc(pr_mm, 1)
                transposes(xn, 3, A0["xn"], A0["xt_mm"], n)
                for j in range(2):
                    pe.wait_ge(A0["xt"], n[j])
                    for t in range(2):
                        o = bank(j, 1)[:, 8 * t:8 * t + 8]
                        pe.matmul(o, xc[j][:, 0, P * t:P * t + P], w_g[:, 0, :], start=True, stop=False)
                        mm = pe.matmul(o, xc[j][0:64, 1, P * t:P * t + P], w_g[0:64, 1, :], start=False, stop=True)
                    mm.then_inc(A0["lg_mm"], 1)

            pe.wait_ge(sel_set, 1)
            places = banks[:, 7][:, 0:8 * (TILES + 1)]
            pe.matmul(places, lt, sel.rearrange("p t e -> p (t e)"), start=True, stop=False)
            for t in range(TILES):
                mm = pe.matmul(places.rearrange("p (t e) -> p t e", e=8)[:, t + 1:, :], ones,
                               sel[:, t:t + 1, :].to_broadcast([P, TILES - t, 8]), start=False, stop=(t == TILES - 1))
            mm.then_inc(count_mm, 1)

            def turn_rows(k, par):
                pe.wait_ge(xg_in[par], 16 * (k // 2 + 1) if isinstance(k, int) else 8 * (k - (k_par[0])) + 16)
                o = banks[:, 0].bitcast(F16)
                pe.transpose(o[:, 0:P], xg[par][:, 0:P], ident16)
                for i, c0 in ((1, P), (3, D + P)):
                    for half in range(2):
                        mm = pe.transpose(o[64 * half:64 * half + 64, P * i:P * i + P], xg[par][:, c0:c0 + 64], ident16)
                pe.transpose(o[:, 2 * P:3 * P], xg[par][:, D:D + P], ident16).then_inc(M["xt_mm"], 1)

            k_par = [0]

            def gate_up(k, par, e):
                pe.wait_ge(M["xt"], k + 1)
                for g in range(2):
                    for m, b, free, done in ((0, 1, "silu", "gate_mm"), (1, 3, "clip", "up_mm")):
                        if not (isinstance(k, int) and k == 0):
                            pe.wait_ge(M[free], 2 * k + g - 1)
                        for f in range(3):
                            o = banks[:, b + g, P * f:P * f + P]
                            c0 = P * (3 * g + f)
                            for i, (part, x) in enumerate(((0, 0), (0, 2), (1, 0), (2, 1), (2, 3))):
                                w = w13[:, bass.ds(e, 1), m, part, c0:c0 + P].rearrange("p o f -> p (o f)")
                                mm = pe.matmul(o, w, xt16[par][:, x, :], start=(i == 0), stop=(i == 4))
                        mm.then_inc(M[done], 1)

            def down(k, par, e):
                pe.wait_ge(M["lo"], 2 * k + 2)
                o = banks[:, 5 + par, 0:D]
                for f in range(6):
                    for i, (hx, wx) in enumerate(((0, 0), (1, 0), (0, 1))):
                        w = w2r[:, bass.ds(e, 1), f, wx, :].rearrange("p o d -> p (o d)")
                        mm = pe.matmul(o, eh[par][:, hx, f, :], w, start=(f == 0 and i == 0), stop=(f == 5 and i == 2))
                mm.then_inc(M["y_mm"], 1)

            pe.wait_ge(stage_free, 54)
            pe.wait_ge(high_set, 54)
            pe.wait_ge(A0["lg"], DUOS)
            turn_rows(0, 0)
            pe.wait_ge(M["xt"], 1)
            turn_rows(1, 1)
            gate_up(0, 0, 0)
            with pe.Fori(0, 4) as it:
                for par in range(2):
                    k = 2 * it + 1 + par
                    k_par[0] = par
                    pe.wait_ge(M["xt"], k + 1)
                    turn_rows(k + 1, par)
                    gate_up(k, 1 - par, 0)
                    down(k - 1, par, 0)
            pe.wait_ge(routed, 1)
            with pe.Fori(0, 13) as it:
                for par in range(2):
                    k = 2 * it + 9 + par
                    k_par[0] = par
                    pe.wait_ge(M["xt"], k + 1)
                    turn_rows(k + 1, par)
                    e = pe.value_load(tile_expert[0:1, bass.ds(k, 1)], min_val=0, max_val=8)
                    gate_up(k, 1 - par, e)
                    e1 = pe.value_load(tile_expert[0:1, bass.ds(k - 1, 1)], min_val=0, max_val=8)
                    down(k - 1, par, e1)
            e = pe.value_load(tile_expert[0:1, 35:36], min_val=0, max_val=8)
            gate_up(35, 1, e)
            e1 = pe.value_load(tile_expert[0:1, 34:35], min_val=0, max_val=8)
            down(34, 0, e1)
            e = pe.value_load(tile_expert[0:1, 35:36], min_val=0, max_val=8)
            down(35, 1, e)

            def toks(buf, j, k, c):
                return buf[j][0:k, c].rearrange("p (i s) -> p i s", s=SLOT)[:, :, 0:NTOK]

            def attention_in(a, w, f0, k1, n, x_set):
                for j in range(2):
                    pe.wait_ge(x_set, n[j])
                    for b, g, done in ((1, f0, a["q_mm"]), (2, f0 + D, a["k_mm"])):
                        for c in range(2):
                            f = slice(g + 64 * c, g + 64 * c + P)
                            o = bank(j, b)[:, 148 * c:148 * c + 148].rearrange("p (i n) -> p i n", n=NTOK)
                            pe.matmul(o, w[:, 0, f], toks(xc, j, P, 0), start=True, stop=False)
                            mm = pe.matmul(o, w[0:k1, 1, f], toks(xc, j, k1, 1), start=False, stop=True)
                        mm.then_inc(done, 1)
                    pe.wait_ge(a["xr"], n[j])
                    for im in range(2):
                        for t in range(2):
                            f = slice(f0 + 2 * D, f0 + QKV17)
                            o = bank(j, 3 - 3 * im)[0:3 * NTOK, 204 * t:204 * t + 204]
                            pe.matmul(o, xr[j][:, 0, 2 * t + im], w[:, 0, f], start=True, stop=False)
                            mm = pe.matmul(o, xr[j][0:k1, 1, 2 * t + im], w[0:k1, 1, f], start=False, stop=True)
                    mm.then_inc(a["v_mm"], 1)

            def attention_core(a, n):
                for j in range(2):
                    pe.wait_ge(a["q"], n[j])
                    pe.wait_ge(a["kx"], n[j])
                    for t in range(2):
                        for im in range(2):
                            o = bank(j, 1 + t)[SLOT * im:SLOT * im + SLOT, 0:444]
                            i = 2 * t + im
                            pe.matmul(o[:, 0:296], qp[j][:, 0, i, :], kx[j][:, i, 0:296], start=True, stop=True)
                            mm = pe.matmul(o[:, 296:444], qp[j][:, 1, i, :], kx[j][:, i, 296:444], start=True, stop=True)
                    mm.then_inc(a["s_mm"], 1)
                for j in range(2):
                    pe.wait_ge(a["e"], n[j])
                    pe.wait_ge(a["vx"], n[j])
                    for t in range(2):
                        for g in range(4):
                            mm = pe.transpose(bank(j, 3 - 3 * t)[0:111, P * g:P * g + P],
                                              sc[j][:, t, 3 * g:3 * g + 3, :].rearrange("p h n -> p (h n)"), ident)
                    mm.then_inc(a["pt_mm"], 1)
                for j in range(2):
                    pe.wait_ge(a["pt"], n[j])
                    for t in range(2):
                        for im in range(2):
                            for g in range(4):
                                o = bank(j, 1)[SLOT * im:SLOT * im + SLOT, 204 * t + 51 * g:204 * t + 51 * g + 51]
                                mm = pe.matmul(o, pt[j][:, t, g, SLOT * im:SLOT * im + SLOT], vx[j][:, 2 * im + t, 51 * g:51 * g + 51], start=True, stop=True)
                    mm.then_inc(a["o_mm"], 1)

            pe.wait_ge(c1_in, 16 * len(third))
            pe.wait_ge(consts2_set, 1)
            with pe.Fori(0, DUOS // 2) as it:
                n = [2 * it + 1, 2 * it + 2]
                transposes(xn, 0, A1["xn"], A1["xt_mm"], n)
                attention_in(A1, w_l1, 0, 65, n, A1["xt"])
                attention_core(A1, n)
                transposes(ao, 2, A1["ao"], A1["at_mm"], n)
                for j in range(2):
                    pe.wait_ge(A1["at"], n[j])
                    for t in range(2):
                        o = bank(j, 3)[:, t * D:(t + 1) * D]
                        pe.matmul(o, xc[j][:, 0, P * t:P * t + P], w_l1o[:, 0, :], start=True, stop=False)
                        mm = pe.matmul(o, xc[j][0:65, 1, P * t:P * t + P], w_l1o[0:65, 1, :], start=False, stop=True)
                    mm.then_inc(A1["pr_mm"], 1)

            pe.wait_ge(beta4_set, 1)
            pe.wait_ge(A1["h"], DUOS)
            for n0 in range(3):
                f = slice(452 * n0, 452 * n0 + 452)
                o = banks[64:68, 1 + n0, 0:452]
                pe.matmul(o, beta4[:, 0, :], w_f1[:, 0, f], start=True, stop=False)
                mm = pe.matmul(o, beta4[0:64, 1, :], w_f1[0:64, 1, f], start=False, stop=True)
            mm.then_inc(bw_mm, 1)
            pe.wait_ge(bw_set, 1)
            pe.wait_ge(w2_set, 1)
            with pe.Fori(0, DUOS // 2) as it:
                n = [2 * it + 1, 2 * it + 2]
                transposes(xn, 0, A2["xn"], A2["xt_mm"], n)
                for j in range(2):
                    pe.wait_ge(A2["xt"], n[j])
                    for t in range(2):
                        o = bank(j, 1)[:, 4 * t:4 * t + 4]
                        pe.matmul(o, xc[j][:, 0, P * t:P * t + P], w_r[:, 0, :], start=True, stop=False)
                        mm = pe.matmul(o, xc[j][0:64, 1, P * t:P * t + P], w_r[0:64, 1, :], start=False, stop=True)
                    mm.then_inc(A2["lg_mm"], 1)
                for j in range(2):
                    pe.wait_ge(A2["dg"], n[j])
                    pe.matmul(bank(j, 2)[:, 0:296], samei, dg[j].rearrange("p t e n -> p (t e n)"), start=True, stop=True).then_inc(A2["bc_mm"], 1)
                transposes(yn, 0, A2["yn"], A2["yt_mm"], n)
                attention_in(A2, w_f1, MLP, 69, n, A2["yt"])
                attention_core(A2, n)
                for j in range(2):
                    pe.wait_ge(A2["ao"], n[j])
                    for b in range(2):
                        for i in range(3):
                            f = slice(P * (3 * b + i), P * (3 * b + i + 1))
                            o = bank(j, b)[:, 148 * i:148 * i + 148].rearrange("p (i n) -> p i n", n=NTOK)
                            pe.matmul(o, w_f1[:, 0, f], toks(xc, j, P, 0), start=True, stop=False)
                            mm = pe.matmul(o, w_f1[0:69, 1, f], toks(xc, j, 69, 1), start=False, stop=True)
                    mm.then_inc(A2["mlp_mm"], 1)
                transposes(ao, 2, A2["ao"], A2["at_mm"], n)
                for j in range(2):
                    pe.wait_ge(A2["at"], n[j])
                    pe.wait_ge(A2["gelu"], n[j])
                    for t in range(2):
                        o = bank(j, 3)[:, t * D:(t + 1) * D]
                        for c in range(6):
                            pe.matmul(o, hid[j][:, c, 2 * t:2 * t + 2, :].rearrange("p i s -> p (i s)"), w_f2s[:, c, :], start=(c == 0), stop=False)
                        pe.matmul(o, xc[j][:, 0, P * t:P * t + P], w_f2s[:, 6, :], start=False, stop=False)
                        mm = pe.matmul(o, xc[j][0:65, 1, P * t:P * t + P], w_f2s[0:65, 7, :], start=False, stop=True)
                    mm.then_inc(A2["fc_mm"], 1)

        @block.scalar
        def _(act):
            def columns(b, ready, done, n):
                for j in range(2):
                    act.wait_ge(ready, n[j])
                    act.copy(xc[j].rearrange("p c n -> p (c n)"), bank(j, b)).then_inc(done, 1)

            def high(e, u, wait):
                act.wait_ge(stage_in[u % 3], wait)
                if u < 4:
                    dst = w13[:, bass.ds(e, 1), u // 2, 2 * (u % 2), :].rearrange("p o f -> p (o f)")
                    src = stage[u % 3]
                else:
                    dst = w2r[:, bass.ds(e, 1), 3 * (u - 4):3 * (u - 4) + 3, 0, :].rearrange("p o c d -> p (o c) d")
                    src = stage[u % 3][:, 0:3 * D].rearrange("p (c d) -> p c d", c=3)
                act.activation(dst, src, ACT.Copy, scale=WSCALE).then_inc(high_set, 1)

            act.wait_ge(w_in, 16 * len(first))
            act.copy(ident16, ident)
            with act.Fori(0, DUOS // 2) as it:
                n = [2 * it + 1, 2 * it + 2]
                def units(a, b):
                    for q in range(a, b):
                        high(2 * it + q // UNITS, q % UNITS, 64 * it + 16 * (q // 3) + 16)
                columns(1, xt1_mm, xt1, n)
                units(0, 3)
                for j in range(2):
                    act.wait_ge(kv_mm, n[j])
                    act.copy(v17[j][:, :, :, 0:16], bank(j, 3)[:, 0:2 * D].rearrange("p (t h e) -> p t h e", t=2, h=NH)).then_inc(vset, 1)
                units(3, 6)
                columns(0, at_mm, at_set, n)
                units(6, 9)
                for j in range(2):
                    act.wait_ge(A0["xn"], n[j])
                    act.activation(rows16[:, bass.ds(4 * it + 2 * j, 2), 0:D], xn[j][:, :, 0:D], ACT.Copy, scale=XSCALE).then_inc(rows_hi, 1)
                columns(3, A0["xt_mm"], A0["xt"], n)
                units(9, 12)
            for u in range(UNITS):
                high(8, u, 256 + 16 * (u // 3) + 16)
            act.wait_ge(A0["lg"], DUOS)
            act.activation(gs[0], glog, ACT.Abs).then_inc(A0["abs"], 1)
            act.wait_ge(A0["abs"], 1)
            act.activation(gs[0], gs[0], ACT.Exp, scale=-1.0).then_inc(A0["exp"], 1)
            act.wait_ge(A0["exp"], 1)
            act.activation(gs[1], gs[0], ACT.Ln, bias=1.0).then_inc(A0["ln"], 1)
            act.wait_ge(A0["sp"], 1)
            act.activation(gs[2], gr[0], ACT.Sqrt).then_inc(A0["sq"], 1)

            def turned(k, par):
                act.wait_ge(M["xt_mm"], k + 1)
                act.copy(xt16[par].rearrange("p c n -> p (c n)"), banks[:, 0].bitcast(F16)[:, 0:4 * P]).then_inc(M["xt"], 1)

            def hidden(k, par):
                for g in range(2):
                    act.wait_ge(M["gate_mm"], 2 * k + g + 1)
                    if not (isinstance(k, int) and k == 0):
                        act.wait_ge(M["h"], 2 * k + g - 1)
                    act.activation(sil[g], banks[:, 1 + g, 0:3 * P], ACT.Silu, scale=1 / (XSCALE * WSCALE)).then_inc(M["silu"], 1)
                for g in range(2):
                    act.wait_ge(M["h"], 2 * k + g + 1)
                    act.copy(eh[par][:, 0, 3 * g:3 * g + 3, :].rearrange("p f n -> p (f n)"), h32[g]).then_inc(M["hi"], 1)

            def result(k, par):
                act.wait_ge(M["y_mm"], k + 1)
                if not (isinstance(k, int) and k < 2):
                    act.wait_ge(y_out[par], 8 * (k - par))
                act.activation(ysb[par], banks[:, 5 + par, 0:D], ACT.Copy, scale=1 / (XSCALE * WSCALE * WSCALE)).then_inc(M["y"], 1)

            turned(0, 0)
            turned(1, 1)
            hidden(0, 0)
            turned(2, 0)
            hidden(1, 1)
            result(0, 0)
            turned(3, 1)
            hidden(2, 0)
            result(1, 1)
            with act.Fori(0, 16) as it:
                for par in range(2):
                    k = 2 * it + 3 + par
                    turned(k + 1, par)
                    hidden(k, 1 - par)
                    result(k - 1, par)
            hidden(35, 1)
            result(34, 0)
            result(35, 1)

            def attention(a, n):
                for j in range(2):
                    for c in range(2):
                        ins = act.copy(xr[j][:, c].rearrange("p i (r n) -> p i r n", r=3), xc[j][:, c].rearrange("p (i s) -> p i s", s=SLOT)[:, :, 0:NTOK].unsqueeze(2).to_broadcast([P, 4, 3, NTOK]))
                    ins.then_inc(a["xr"], 1)
                for j in range(2):
                    act.wait_ge(a["q_mm"], n[j])
                    act.copy(qp[j][:, :, :, 0:NTOK], bank(j, 1)[:, 0:296].rearrange("p (c i n) -> p c i n", c=2, n=NTOK)).then_inc(a["q"], 1)
                    act.wait_ge(a["k_mm"], n[j])
                    act.copy(kc[j].rearrange("p c i n -> p (c i n)"), bank(j, 2)[:, 0:296]).then_inc(a["k"], 1)
                for j in range(2):
                    act.wait_ge(a["sub"], n[j])
                    act.activation(sc[j], sc[j], ACT.Exp, scale=HD ** -0.5).then_inc(a["e"], 1)
                for j in range(2):
                    act.wait_ge(a["pt_mm"], n[j])
                    for t in range(2):
                        ins = act.copy(pt[j][:, t].rearrange("p g n -> p (g n)"), bank(j, 3 - 3 * t)[0:111, :])
                    ins.then_inc(a["pt"], 1)

            with act.Fori(0, DUOS // 2) as it:
                n = [2 * it + 1, 2 * it + 2]
                columns(0, A1["xt_mm"], A1["xt"], n)
                act.wait_ge(A1["xt"], n[1])
                attention(A1, n)
                columns(2, A1["at_mm"], A1["at"], n)
            with act.Fori(0, DUOS // 2) as it:
                n = [2 * it + 1, 2 * it + 2]
                columns(0, A2["xt_mm"], A2["xt"], n)
                for j in range(2):
                    act.wait_ge(A2["lgsub"], n[j])
                    act.activation(pr[j], lg[j], ACT.Exp).then_inc(A2["lgexp"], 1)
                columns(0, A2["yt_mm"], A2["yt"], n)
                act.wait_ge(A2["yt"], n[1])
                attention(A2, n)
                for j in range(2):
                    act.wait_ge(A2["mlp_mm"], n[j])
                    for b in range(2):
                        for i in range(3):
                            ins = act.activation(hid[j][:, 3 * b + i, :, 0:NTOK],
                                       bank(j, b)[:, 148 * i:148 * i + 148].rearrange("p (i n) -> p i n", n=NTOK), ACT.Gelu)
                    ins.then_inc(A2["gelu"], 1)
                columns(2, A2["at_mm"], A2["at"], n)

        @block.vector
        def _(dve):
            def stats(a, src, j, n, eps, ve_sem):
                for t in range(2):
                    dve.bn_stats(st[j][:, t, :], src[t])
                dve.drain()
                for t in range(2):
                    ins = dve.bn_aggr(mv[j][:, t, :], st[j][:, t, :])
                dve.drain()
                dve.tensor_scalar_add(ve[j], mv[j][:, :, 1], eps).then_inc(ve_sem, 1)

            def h_tiles(it):
                return ([h[:, bass.ds(4 * it + 2 * j, 2), :] for j in range(2)],
                        [[h[:, bass.ds(4 * it + 2 * j + t, 1), :].rearrange("p o d -> p (o d)") for t in range(2)] for j in range(2)])

            def normalised(a, h1, n):
                for j in range(2):
                    stats(a, h1[j], j, n, LN_EPS, a["ve"])
                for j in range(2):
                    dve.wait_ge(a["rs"], n[j])
                    for t in range(2):
                        ins = dve.tensor_scalar(xn[j][:, t, 0:D], h1[j][t], mv[j][:, t, 0:1], rs[j][:, t:t + 1], ALU.subtract, ALU.mult)
                    ins.then_inc(a["xn"], 1)

            def low(e, u, n):
                dve.wait_ge(high_set, n)
                if u < 4:
                    rows = slice(64 * (u % 2), P)
                    hi = w13[rows, bass.ds(e, 1), u // 2, 2 * (u % 2), :].rearrange("p o f -> p (o f)")
                    lo = w13[rows, bass.ds(e, 1), u // 2, 1 + u % 2, :].rearrange("p o f -> p (o f)")
                    src = stage[u % 3][rows]
                else:
                    rows = slice(3 * (u - 4), 3 * (u - 4) + 3)
                    hi = w2r[:, bass.ds(e, 1), rows, 0, :].rearrange("p o c d -> p (o c) d")
                    lo = w2r[:, bass.ds(e, 1), rows, 1, :].rearrange("p o c d -> p (o c) d")
                    src = stage[u % 3][:, 0:3 * D].rearrange("p (c d) -> p c d", c=3)
                dve.scalar_tensor_tensor(lo, src, WSCALE, hi, ALU.mult, ALU.subtract).then_inc(stage_free, 1)

            dve.wait_ge(w_in, 16 * len(first))
            dve.wait_ge(posb_mm, 1)
            dve.tensor_tensor(pos_bias, pos_bias, bank(0, 0)[:, 0:D], ALU.add).then_inc(posb_set, 1)
            dve.wait_ge(posb_set, 1)
            dve.wait_ge(consts_set, 1)
            with dve.Fori(0, DUOS // 2) as it:
                n = [2 * it + 1, 2 * it + 2]
                ht, h1 = h_tiles(it)
                def units(a, b):
                    for q in range(a, b):
                        low(2 * it + q // UNITS, q % UNITS, 12 * it + q + 1)
                for j in range(2):
                    dve.wait_ge(tok_mm, 4 * it + 2 * j + 2)
                    dve.tensor_tensor(ht[j], bank(j, 0)[:, 0:2 * D].rearrange("p (t d) -> p t d", t=2),
                                      pos_bias.unsqueeze(1).to_broadcast([P, 2, D]), ALU.add)
                    dve.drain()
                    stats(None, h1[j], j, n, LN_EPS, ve1)
                for j in range(2):
                    dve.wait_ge(rs1, n[j])
                    for t in range(2):
                        ins = dve.tensor_scalar(xn[j][:, t, 0:D], h1[j][t], mv[j][:, t, 0:1], rs[j][:, t:t + 1], ALU.subtract, ALU.mult)
                    ins.then_inc(xn1, 1)
                units(0, 2)
                for j in range(2):
                    dve.wait_ge(kv_mm, n[j])
                    dve.tensor_scalar(kpos[j].rearrange("p t d -> p (t d)"), bank(j, 2)[:, 0:2 * D], 0.0, HD ** -0.5, ALU.max, ALU.add).then_inc(kset, 1)
                    dve.wait_ge(q_mm, n[j])
                    dve.tensor_scalar(qt[j].rearrange("p c n -> p (c n)"), bank(j, 0), 0.0, HD ** -0.5, ALU.max, ALU.add).then_inc(qset, 1)
                units(2, 4)
                for j in range(2):
                    dve.wait_ge(kvi_mm, n[j])
                    for im in range(2):
                        ins = dve.tensor_tensor(kvm[j][:, 2 * im:2 * im + 2, :], bank(j, 2 + im)[:, 0:408].rearrange("p (i n) -> p i n", i=2),
                                      mask17.unsqueeze(1).to_broadcast([P, 2, 204]), ALU.mult)
                    ins.then_inc(kvm_set, 1)
                units(4, 6)
                for j in range(2):
                    dve.wait_ge(o_mm, n[j])
                    o4 = bank(j, 1)[:, 0:408].rearrange("p (t h e) -> p t h e", t=2, h=NH)
                    dve.tensor_scalar_add(den[j], o4[:, :, :, 16], 1e-6).then_inc(den_e, 1)
                    dve.wait_ge(den_e, n[j])
                    dve.reciprocal(den[j], den[j]).then_inc(den_set, 1)
                    dve.wait_ge(den_set, n[j])
                    for t in range(2):
                        ins = dve.tensor_tensor(ao[j][:, t, 0:D].rearrange("p (h e) -> p h e", h=NH), o4[:, t, :, 0:16],
                                      den[j][:, t].unsqueeze(2).to_broadcast([P, NH, HD]), ALU.mult)
                    ins.then_inc(ao_set, 1)
                units(6, 8)
                for j in range(2):
                    dve.wait_ge(pr_mm, n[j])
                    dve.tensor_tensor(ht[j], ht[j], bank(j, 2)[:, 0:2 * D].rearrange("p (t d) -> p t d", t=2), ALU.add).then_inc(h_attn, 1)
                dve.drain()
                normalised(A0, h1, n)
                for j in range(2):
                    dve.wait_ge(rows_hi, n[j])
                    dve.scalar_tensor_tensor(rows16[:, bass.ds(4 * it + 2 * j, 2), D:2 * D], xn[j][:, :, 0:D], XSCALE,
                                             rows16[:, bass.ds(4 * it + 2 * j, 2), 0:D], ALU.mult, ALU.subtract).then_inc(rows_set, 1)
                units(8, 10)
                for j in range(2):
                    dve.wait_ge(A0["lg_mm"], n[j])
                    dve.tensor_copy(glog[:, bass.ds(4 * it + 2 * j, 2), :], bank(j, 1)[:, 0:16].rearrange("p (t e) -> p t e", t=2)).then_inc(A0["lg"], 1)
                units(10, 12)

            for u in range(UNITS):
                low(8, u, 48 + u + 1)

            valid = route[:, 0:1]
            spare = route[:, 1:1 + TOPK * TILES].rearrange("p (k t) -> p k t", k=TOPK)
            whole = route[:, 33:43]
            numbers = route[:, 43:43 + ROUTED_TILES]
            dve.wait_ge(r_in, 16 * len(second))
            dve.wait_ge(A0["lg"], DUOS)
            dve.tensor_scalar(gr[1], glog, 0.0, None, ALU.max)
            dve.drain()
            dve.wait_ge(A0["ln"], 1)
            dve.tensor_tensor(gr[0], gr[1], gs[1], ALU.add).then_inc(A0["sp"], 1)
            dve.wait_ge(A0["sq"], 1)
            dve.tensor_tensor(gr[1], gs[2], gbias.unsqueeze(1).to_broadcast([P, TILES, 8]), ALU.add)
            dve.drain()
            pair = [g.rearrange("p t (a b) -> p t a b", a=8) for g in gpair]
            for t in range(TILES):
                other = gr[1][:, t].unsqueeze(1).to_broadcast([P, 8, 8])
                own = gr[1][:, t].unsqueeze(2).to_broadcast([P, 8, 8])
                dve.tensor_tensor(pair[0][:, t], other, own, ALU.is_gt)
                dve.tensor_tensor(pair[1][:, t], other, own, ALU.is_equal)
            dve.drain()
            dve.tensor_tensor(gpair[1], gpair[1], tri8.rearrange("p a b -> p (a b)").unsqueeze(1).to_broadcast([P, TILES, 64]), ALU.mult)
            dve.drain()
            dve.tensor_tensor(gpair[0], gpair[0], gpair[1], ALU.add)
            dve.drain()
            dve.tensor_reduce(gr[0], pair[0], AX.X, ALU.add)
            dve.drain()
            for k in range(TOPK):
                dve.tensor_scalar(gr[1 + k], gr[0], float(k), valid, ALU.is_equal, ALU.mult)
            dve.memset(sel[:, TILES, :], 0.0)
            dve.drain()
            dve.tensor_tensor(sel[:, 0:TILES, :], gr[1], gr[2], ALU.add).then_inc(sel_set, 1)
            for k in range(TOPK):
                dve.tensor_tensor(gr[3], gr[1 + k], gs[2], ALU.mult)
                dve.drain()
                dve.tensor_reduce(wk[:, k], gr[3], AX.X, ALU.add)
                dve.drain()
            dve.tensor_tensor(gsum, wk[:, 0], wk[:, 1], ALU.add)
            dve.drain()
            dve.tensor_scalar(gsum, gsum, 1e-6, None, ALU.max)
            dve.drain()
            dve.reciprocal(gsum, gsum)
            dve.drain()
            dve.tensor_tensor(wk, wk, gsum.unsqueeze(1).to_broadcast([P, TOPK, TILES]), ALU.mult)
            dve.wait_ge(count_mm, 1)
            places = banks[:, 7][:, 0:8 * (TILES + 1)].rearrange("p (t e) -> p t e", e=8)
            dve.tensor_copy(cnt[:, 0], places[:, TILES, :])
            dve.drain()
            full = cmpt[:, 0:80].rearrange("p (e q) -> p e q", e=8)
            dve.tensor_tensor(full, cnt[:, 0].unsqueeze(2).to_broadcast([P, 8, 10]), whole.unsqueeze(1).to_broadcast([P, 8, 10]), ALU.is_gt)
            dve.drain()
            dve.tensor_reduce(cnt[:, 1], full, AX.X, ALU.add)
            dve.drain()
            before = cmpt[:, 0:64].rearrange("p (a b) -> p a b", a=8)
            dve.tensor_tensor(before, cnt[:, 1].unsqueeze(1).to_broadcast([P, 8, 8]), tri8, ALU.mult)
            dve.drain()
            dve.tensor_reduce(cnt[:, 2], before, AX.X, ALU.add)
            dve.drain()
            dve.tensor_tensor(cnt[:, 3], cnt[:, 2], cnt[:, 1], ALU.add)
            dve.tensor_scalar(cnt[:, 0], cnt[:, 2], float(P), float(SHARED_TILES * P), ALU.mult, ALU.add)
            dve.drain()
            ended = cmpt.rearrange("p (n e) -> p n e", e=8)
            dve.tensor_tensor(ended, cnt[:, 3].unsqueeze(1).to_broadcast([P, ROUTED_TILES, 8]), numbers.unsqueeze(2).to_broadcast([P, ROUTED_TILES, 8]), ALU.is_le)
            dve.drain()
            dve.tensor_reduce(eidf, ended, AX.X, ALU.add)
            dve.drain()
            dve.tensor_scalar(tile_expert[:, SHARED_TILES:], eidf[0:1], float(EXPERTS - 1), 1.0, ALU.min, ALU.add)
            dve.tensor_tensor(gr[0], places[:, 0:TILES, :], cnt[:, 0].unsqueeze(1).to_broadcast([P, TILES, 8]), ALU.add)
            dve.drain()
            for k in range(TOPK):
                dve.tensor_tensor(gr[3], gr[1 + k], gr[0], ALU.mult)
                dve.drain()
                dve.tensor_reduce(slotf[:, k], gr[3], AX.X, ALU.add)
                dve.drain()
            dve.tensor_copy(gather_at, slotf)
            dve.tensor_tensor(scatter_at, slotf, spare, ALU.add).then_inc(routed, 1)
            with dve.Fori(0, MTILES // 2) as it:
                for par in range(2):
                    k = 2 * it + par
                    for g in range(2):
                        dve.wait_ge(M["up_mm"], 2 * k + g + 1)
                        dve.tensor_scalar(upc[g], banks[:, 3 + g, 0:3 * P], LIMIT * XSCALE * WSCALE, -LIMIT * XSCALE * WSCALE, ALU.min, ALU.max).then_inc(M["clip"], 1)
                        dve.wait_ge(M["clip"], 2 * k + g + 1)
                        dve.wait_ge(M["silu"], 2 * k + g + 1)
                        dve.scalar_tensor_tensor(h32[g], sil[g], SILU_LIMIT, upc[g], ALU.min, ALU.mult).then_inc(M["h"], 1)
                    for g in range(2):
                        dve.wait_ge(M["hi"], 2 * k + g + 1)
                        dve.tensor_tensor(eh[par][:, 1, 3 * g:3 * g + 3, :].rearrange("p f n -> p (f n)"), h32[g],
                                          eh[par][:, 0, 3 * g:3 * g + 3, :].rearrange("p f n -> p (f n)"), ALU.subtract).then_inc(M["lo"], 1)
            dve.wait_ge(sy_in, 32)
            dve.tensor_tensor(h, h, shared_y, ALU.add).then_inc(h_shared, 1)
            for half in range(2):
                dve.wait_ge(gathered[half], 16 * TILES)
                for t in range(8 * half, 8 * half + 8):
                    for k in range(TOPK):
                        dve.drain()
                        dve.scalar_tensor_tensor(h[:, t], got[:, k, t], wk[:, k, t:t + 1], h[:, t], ALU.mult, ALU.add)
            dve.drain()
            dve.wait_ge(consts2_set, 1)

            def attention(a, n, masked):
                for j in range(2):
                    dve.wait_ge(a["v_mm"], n[j])
                    for im in range(2):
                        ins = dve.tensor_tensor(vx[j][:, 2 * im:2 * im + 2, :].rearrange("p t (g e) -> p (t g) e", g=4),
                                      bank(j, 3 - 3 * im)[0:111, 0:408].rearrange("p (g e) -> p g e", e=51),
                                      m_v.unsqueeze(1).to_broadcast([111, 8, 51]), ALU.mult)
                    ins.then_inc(a["vx"], 1)
                for j in range(2):
                    dve.wait_ge(a["s_mm"], n[j])
                    s2 = banks[:, 4 * j + 1:4 * j + 3, 0:444].rearrange("p t (h n) -> p t h n", h=12)
                    if masked:
                        for t in range(2):
                            dve.tensor_tensor(sc[j][:, t], s2[:, t], m_causal.unsqueeze(1).to_broadcast([P, 12, NTOK]), ALU.add)
                        dve.drain()
                        s2 = sc[j]
                    dve.tensor_reduce(mx[j], s2, AX.X, ALU.max).then_inc(a["mx"], 1)
                    dve.wait_ge(a["mx"], n[j])
                    for t in range(2):
                        ins = dve.tensor_tensor(sc[j][:, t], s2[:, t], mx[j][:, t].unsqueeze(2).to_broadcast([P, 12, NTOK]), ALU.subtract)
                    ins.then_inc(a["sub"], 1)
                for j in range(2):
                    dve.wait_ge(a["o_mm"], n[j])
                    o4 = bank(j, 1)[:, 0:408].rearrange("p (t h e) -> p t h e", t=2, h=NH)
                    dve.reciprocal(den[j], o4[:, :, :, 16]).then_inc(a["rden"], 1)
                    dve.wait_ge(a["rden"], n[j])
                    for t in range(2):
                        ins = dve.tensor_tensor(ao[j][:, t, 0:D].rearrange("p (h e) -> p h e", h=NH), o4[:, t, :, 0:16],
                                      den[j][:, t].unsqueeze(2).to_broadcast([P, NH, HD]), ALU.mult)
                    ins.then_inc(a["ao"], 1)

            with dve.Fori(0, DUOS // 2) as it:
                n = [2 * it + 1, 2 * it + 2]
                ht, h1 = h_tiles(it)
                normalised(A1, h1, n)
                attention(A1, n, True)
                for j in range(2):
                    dve.wait_ge(A1["pr_mm"], n[j])
                    dve.tensor_tensor(ht[j], ht[j], bank(j, 3)[:, 0:2 * D].rearrange("p (t d) -> p t d", t=2), ALU.add).then_inc(A1["h"], 1)

            dve.wait_ge(bw_mm, 1)
            for n0 in range(3):
                f = slice(452 * n0, 452 * n0 + 452)
                dve.tensor_tensor(w_f1[64:68, 1, f], w_f1[64:68, 1, f], banks[64:68, 1 + n0, 0:452], ALU.add)
            dve.tensor_scalar(w_f1[:, 0, :], w_f1[:, 0, :], gb[:, 0, 0:1], None, ALU.mult)
            dve.tensor_scalar(w_f1[0:64, 1, :], w_f1[0:64, 1, :], gb[0:64, 1, 0:1], None, ALU.mult).then_inc(bw_set, 1)
            dve.drain()
            with dve.Fori(0, DUOS // 2) as it:
                n = [2 * it + 1, 2 * it + 2]
                ht, h1 = h_tiles(it)
                normalised(A2, h1, n)
                for j in range(2):
                    dve.wait_ge(A2["xn"], n[j])
                    for t in range(2):
                        dve.bn_stats(st[j][:, t, :], xn[j][:, t, 0:D])
                    dve.drain()
                    for t in range(2):
                        dve.bn_aggr(mv[j][:, t, :], st[j][:, t, :])
                    dve.drain()
                    dve.tensor_scalar_add(ve[j], mv[j][:, :, 1], EPS2).then_inc(A2["ve2"], 1)
                    dve.tensor_tensor(ht[j], ht[j], xn[j][:, :, 0:D], ALU.add).then_inc(A2["hx"], 1)
                for j in range(2):
                    dve.wait_ge(A2["lg_mm"], n[j])
                    l2 = bank(j, 1)[:, 0:8].rearrange("p (t e) -> p t e", t=2)
                    dve.tensor_reduce(l1s[j], l2, AX.X, ALU.max).then_inc(A2["lgmx"], 1)
                    dve.wait_ge(A2["lgmx"], n[j])
                    dve.tensor_tensor(lg[j], l2, l1s[j].unsqueeze(2).to_broadcast([P, 2, 4]), ALU.subtract).then_inc(A2["lgsub"], 1)
                for j in range(2):
                    dve.wait_ge(A2["lgexp"], n[j])
                    dve.tensor_reduce(l1s[j], pr[j], AX.X, ALU.add).then_inc(A2["lgsum"], 1)
                    dve.wait_ge(A2["lgsum"], n[j])
                    dve.reciprocal(l1s[j], l1s[j]).then_inc(A2["lgrec"], 1)
                    dve.wait_ge(A2["lgrec"], n[j])
                    dve.tensor_tensor(pr[j], pr[j], l1s[j].unsqueeze(2).to_broadcast([P, 2, 4]), ALU.mult).then_inc(A2["p"], 1)
                    dve.wait_ge(A2["p"], n[j])
                    dve.tensor_tensor(dg[j].rearrange("p t e n -> p (t e) n"), eye37.unsqueeze(1).to_broadcast([P, 8, NTOK]),
                                      pr[j].rearrange("p t e -> p (t e)").unsqueeze(2).to_broadcast([P, 8, NTOK]), ALU.mult).then_inc(A2["dg"], 1)
                for j in range(2):
                    dve.wait_ge(A2["bc_mm"], n[j])
                    others = bank(j, 2)[:, 0:296].rearrange("p (e n) -> p e n", n=NTOK)
                    own = pr[j].rearrange("p t e -> p (t e)").unsqueeze(2).to_broadcast([P, 8, NTOK])
                    g3 = gt[j].rearrange("p t e n -> p (t e) n")
                    e3 = eq[j].rearrange("p t e n -> p (t e) n")
                    dve.tensor_tensor(g3, others, own, ALU.is_gt)
                    dve.tensor_tensor(e3, others, own, ALU.is_equal).then_inc(A2["cmp"], 1)
                    dve.wait_ge(A2["cmp"], n[j])
                    dve.tensor_tensor(e3, e3, tri.unsqueeze(1).to_broadcast([P, 8, NTOK]), ALU.mult)
                    dve.drain()
                    dve.tensor_tensor(g3, g3, e3, ALU.add).then_inc(A2["cmp2"], 1)
                    dve.wait_ge(A2["cmp2"], n[j])
                    dve.tensor_reduce(rank[j].rearrange("p t e -> p (t e)"), g3, AX.X, ALU.add).then_inc(A2["rank"], 1)
                    dve.wait_ge(A2["rank"], n[j])
                    dve.tensor_scalar(sg[j][:, 0], rank[j], CAP - 0.5, None, ALU.is_lt)
                    dve.drain()
                    dve.tensor_tensor(sg[j][:, 1], sg[j][:, 0], pr[j], ALU.mult)
                    dve.drain()
                    for e in (2, 1, 0):
                        dve.tensor_tensor(sg[j][:, :, :, e], sg[j][:, :, :, e], sg[j][:, :, :, e + 1], ALU.add)
                        dve.drain()
                    dve.wait_ge(A2["rs2"], n[j])
                    dve.tensor_tensor(rsr[j], sg[j][:, 0], rs[j].unsqueeze(2).to_broadcast([P, 2, 4]), ALU.mult).then_inc(A2["rsr"], 1)
                    dve.wait_ge(A2["rsr"], n[j])
                    for t in range(2):
                        for r, (a0, a1) in enumerate(RNG):
                            dve.tensor_scalar(yn[j][:, t, a0:a1], xn[j][:, t, a0:a1], mv[j][:, t, 0:1], rsr[j][:, t, r:r + 1], ALU.subtract, ALU.mult)
                    dve.tensor_copy(yn[j][:, :, 192:196], sg[j][:, 0]).then_inc(A2["yn"], 1)
                attention(A2, n, False)
                for j in range(2):
                    dve.wait_ge(A2["fc_mm"], n[j])
                    for r, (a0, a1) in enumerate(RNG):
                        dve.tensor_tensor(zz[j][:, :, a0:a1], bank(j, 3)[:, 0:2 * D].rearrange("p (t d) -> p t d", t=2)[:, :, a0:a1],
                                          sg[j][:, 1, :, r:r + 1].to_broadcast([P, 2, a1 - a0]), ALU.mult)
                    dve.drain()
                    dve.tensor_tensor(ht[j], ht[j], zz[j], ALU.add).then_inc(A2["h"], 1)


def two_chunks(w):
    a = np.zeros((256, w.shape[1]), w.dtype)
    a[:w.shape[0]] = w
    return np.ascontiguousarray(a.reshape(2, 128, -1).transpose(1, 0, 2))


def qkv17(w, rows, ones_row):
    a = two_chunks(w.T)
    for r, v in rows.items():
        a[r, 1] = v
    v17 = np.zeros((P, 2, NH, 17), w.dtype)
    v17[..., :16] = a[:, :, 2 * D:].reshape(P, 2, NH, HD)
    v17[ones_row, 1, :, 16] = 1
    return np.concatenate([a[:, :, :2 * D], v17.reshape(P, 2, -1)], 2)


def kernel(**inputs):
    import concourse.bacc as _bacc
    from concourse.bass_utils import run_bass_kernel_spmd as _run
    x = np.asarray(inputs["x"])
    g = {k: np.asarray(v) for k, v in inputs.items()}
    pt = x.reshape(NIMG, 6, 16, 6, 16, 3).transpose(0, 1, 3, 2, 4, 5).reshape(NIMG, 36, 6, 128)
    xp = np.zeros((NIMG, SLOT, 6, 128), x.dtype)
    xp[:, 1:37] = pt
    xp = np.ascontiguousarray(xp.reshape(TILES, P, 6, 128).transpose(0, 3, 2, 1))
    pos = np.zeros((2, SLOT, D), x.dtype)
    pos[:, :NTOK] = g["L0_tok_pos_embedding"]
    oh = np.zeros((2, 2, SLOT), np.float32)
    oh[0, :, 0] = 1
    oh[1, :, 1:NTOK] = 1
    addrows = np.stack([g["L0_tok_cls_token"].reshape(D), g["L0_tok_b_proj"]])
    m17 = np.zeros((P, NH, 17), np.float32)
    for e in range(P):
        m17[e, :8][np.arange(8) == e // 16] = 1
        if e >= 64:
            m17[e, 8:][np.arange(8, 12) == (e + 64) // 16] = 1
    def experts(name):
        return np.concatenate([g[f"L0_ffn_{name}s"][None], g[f"L0_ffn_{name}"]])

    def halves(name):
        w = experts(name)
        return np.stack([w[:, :P], np.concatenate([w[:, P:], w[:, P:]], 1)], 1)

    valid = (np.arange(P) % SLOT < NTOK)
    row = np.arange(TILES)[None] * P + np.arange(P)[:, None]
    spare = np.stack([SPARE_ROWS + k * TILES * P + row for k in range(TOPK)], 1) * ~valid[:, None, None]
    route = np.concatenate([valid[:, None], spare.reshape(P, -1), np.tile(np.arange(10) * P, (P, 1)), np.tile(np.arange(ROUTED_TILES), (P, 1))], 1).astype(np.float32)

    i, jj = np.arange(NTOK)[:, None], np.arange(NTOK)[None, :]
    mask = np.where(((jj % 8 == 0) & (jj <= i)) | (jj == i) | (jj == i - 1), 0, -1e30).astype(np.float32)
    pad = np.zeros((SLOT - NTOK, NTOK), np.float32)
    kmask = m17[:, :, 0]
    vmask = np.zeros((3, NTOK, 3, 17), np.float32)
    for k in range(3):
        vmask[k, :, k] = 1
    rng = np.zeros((D, 4), np.float32)
    for k, (a0, a1) in enumerate(RNG):
        rng[a0:a1, k] = 1
    same = np.zeros((2, SLOT, 2, SLOT), np.float32)
    for k in range(2):
        same[k, :, k] = 1
    same = same.reshape(P, P)
    ffn_w1 = np.concatenate([two_chunks(g["L1_ffn_w1"][:MLP].T), qkv17(g["L1_ffn_w1"][MLP:], {64: g["L1_ffn_b1"][MLP:]}, 68)], 2)
    ffn_w1[64, 1, :MLP] = g["L1_ffn_b1"][:MLP]
    w2 = np.zeros((1024, 2 * D), np.float32)
    w2[:960] = g["L1_ffn_w2"].T
    w2[960] = g["L1_ffn_b2"]
    arrays = {
        "x_patches": xp, "tok_w": g["L0_tok_W_proj"].reshape(6, 128, D).transpose(1, 0, 2), "tok_pos": pos.reshape(P, D),
        "tok_onehot": oh.reshape(2, P), "tok_addrows": addrows, "l0_qkv": two_chunks(g["L0_attn_qkv_w"].T),
        "l0_proj": two_chunks(np.concatenate([g["L0_attn_proj_w"].T, g["L0_attn_proj_b"][None]])),
        "l1_w": qkv17(g["L1_attn_qkv_w"], {64: g["L1_attn_qkv_b"]}, 64),
        "l1_out": two_chunks(np.concatenate([g["L1_attn_out_w"].T, g["L1_attn_out_b"][None]])),
        "l1_mask": np.concatenate([mask, pad] * 2), "kmask": kmask, "vmask": vmask.reshape(3 * NTOK, 51),
        "ffn_w1": ffn_w1, "ffn_w2": w2.reshape(8, P, 2, D).transpose(1, 0, 2, 3), "ffn_router": two_chunks(g["L1_ffn_w_router"].T),
        "ffn_gb": two_chunks(np.stack([g["L1_ffn_gamma1"], g["L1_ffn_beta1"]], 1)), "ffn_ranges": two_chunks(rng),
        "slot_eye": np.concatenate([np.eye(NTOK, dtype=np.float32), pad] * 2), "same_image": same,
        "earlier": np.concatenate([np.tril(np.ones((NTOK, NTOK), np.float32), -1), pad] * 2),
        "moe_13": np.stack([halves("w1"), halves("w3")], 1).reshape(9, 4, P, FFN), "gate_w": two_chunks(g["L0_ffn_gate_w"]),
        "moe_2": experts("w2").reshape(9, 2, 3, P, D).transpose(0, 1, 3, 2, 4).reshape(9, 2, P, 3 * D),
        "route_c": route, "lt_in": np.triu(np.ones((P, P), np.float32), 1), "ones_in": np.ones((P, P), np.float32),
        "gate_bias": np.tile(g["L0_ffn_gate_bias"], (P, 1)), "before8": np.tile(np.tril(np.ones((8, 8), np.float32), -1), (P, 1, 1)),
        "ident_in": np.eye(P, dtype=np.float32), "hmask17": m17.reshape(P, 204),
    }
    arrays = {k: np.ascontiguousarray(v) for k, v in arrays.items()}
    nc = _bacc.Bacc("TRN2", target_bir_lowering=False, num_devices=1)
    args = {k: nc.dram_tensor(k + "_dram", v.shape, mybir.dt.from_np(v.dtype), kind="ExternalInput").ap() for k, v in arrays.items()}
    out = nc.dram_tensor("out_dram", (NIMG, NTOK, D), F32, kind="ExternalOutput").ap()
    vit(nc, out=out, **args)
    r = _run(nc, [{k + "_dram": v for k, v in arrays.items()}], core_ids=[0])
    return r.results[0]["out_dram"]
```

```python
import numpy as np
import concourse.bass as bass
from concourse import mybir
from contextlib import ExitStack

F32 = mybir.dt.float32
F16 = mybir.dt.float16
I32 = mybir.dt.int32
ALU = mybir.AluOpType
ACT = mybir.ActivationFunctionType
AX = mybir.AxisListType

P = 128
SLOT = 64
NIMG, NTOK, D, NH, HD = 32, 37, 192, 12, 16
TILES = NIMG // 2
DUOS = TILES // 2
LN_EPS = 1e-5
EPS2 = 1e-6
V_COLS, V_COLS0, V_COLS3 = NH * (HD + 1), 8 * (HD + 1), 3 * (HD + 1)
QKV17 = 2 * D + V_COLS
KEY_COLS, KEY_COLS0, TOKENS3, TOKENS4 = NH * NTOK, 8 * NTOK, 3 * NTOK, 4 * NTOK
MLP = 768
FFN = 768
LIMIT = 10.0
SILU_LIMIT = LIMIT / (1 + float(np.exp(-LIMIT)))
CAP = NTOK // 2
EXPERTS, TOPK = 8, 2
SHARED_TILES = -(-NIMG * NTOK // P)
ROUTED_TILES = (NIMG * NTOK * TOPK - EXPERTS) // P + EXPERTS
MTILES = SHARED_TILES + ROUTED_TILES
ZERO_TILES = -(-ROUTED_TILES // 4)
GROUP = 4
WORDS = ROUTED_TILES // GROUP + 1
ZERO_STORES = 4
ALL = EXPERTS + 1
WORD_MAX = ALL ** (GROUP + 1) - 1
SPARE_ROWS = MTILES * P
XSCALE, WSCALE = 16.0, 16.0
UNITS = 6
RNG = ((0, 24), (24, 48), (48, 96), (96, 192))


class Place:

    def __init__(self, nc, start):
        self.nc, self.at = nc, start

    def take(self, name, shape, dt=F32):
        size = {F32: 4, I32: 4, F16: 2}[dt]
        for n in shape[1:]:
            size *= n
        t = self.nc.alloc_sbuf_tensor_at(name, shape, dt, offset=self.at)[tuple(slice(None) for _ in shape)]
        self.at += -(-size // 32) * 32
        return t


def vit(nc, x_patches, tok_w, tok_pos, tok_onehot, tok_addrows, l0_qkv, l0_proj, ident_in, hmask17,
        moe_13, moe_2, gate_w, gate_bias, before8, route_c, lt_in, ones_in,
        l1_w, l1_out, l1_mask, kmask, vmask, ffn_w1, ffn_w2, ffn_router, ffn_gb, ffn_ranges, slot_eye, same_image, earlier, out):
    xs = nc.dram_tensor("moe_rows_in", [SPARE_ROWS + TOPK * TILES * P, 2 * D], F16).ap()
    ys = nc.dram_tensor("moe_rows_out", [MTILES * P, D], F32).ap()
    with ExitStack() as ctx:
        def sem(name):
            return ctx.enter_context(nc.semaphore(name))

        banks = ctx.enter_context(nc.psum_tensor("banks", [P, 8, 512], F32))[:, :, :]
        keep = Place(nc, -(-nc.sbuf_base // 32) * 32)
        ident = keep.take("ident", [P, P])
        ident16 = keep.take("ident16", [P, P], F16)
        pos_bias = keep.take("pos_bias", [P, D])
        mask17 = keep.take("mask17", [P, V_COLS])
        neghalf = keep.take("neghalf", [P, 2])
        w_g = keep.take("w_g", [P, 2, 8])
        h = keep.take("h", [P, TILES, D])
        rows16 = keep.take("rows16", [P, TILES, 2 * D], F16)
        shared_y = rows16.bitcast(F32)
        xn = [keep.take(f"xn{j}", [P, 2, 256]) for j in range(2)]
        xc = [keep.take(f"xc{j}", [P, 2, 4 * SLOT]) for j in range(2)]
        ao = [keep.take(f"ao{j}", [P, 2, 256]) for j in range(2)]
        den = [keep.take(f"den{j}", [P, 2, NH]) for j in range(2)]
        st = [keep.take(f"st{j}", [P, 2, 6]) for j in range(2)]
        st2 = [keep.take(f"st2{j}", [P, 2, 6]) for j in range(2)]
        mv2 = [keep.take(f"mv2{j}", [P, 2, 2]) for j in range(2)]
        ve2 = [keep.take(f"ve2{j}", [P, 2]) for j in range(2)]
        rs2 = [keep.take(f"rs2{j}", [P, 2]) for j in range(2)]
        mv = [keep.take(f"mv{j}", [P, 2, 2]) for j in range(2)]
        ve = [keep.take(f"ve{j}", [P, 2]) for j in range(2)]
        rs = [keep.take(f"rs{j}", [P, 2]) for j in range(2)]
        gbias = keep.take("gbias", [P, 8])
        route = keep.take("route", [P, 1 + TOPK * TILES + SHARED_TILES + ROUTED_TILES])
        glog = keep.take("glog", [P, TILES, EXPERTS])
        root_score = keep.take("root_score", [P, TILES, EXPERTS])
        choice = [keep.take(f"choice{k}", [P, TILES, EXPERTS]) for k in range(TOPK)]
        sel = keep.take("sel", [P, TILES + 1, EXPERTS])
        tile_e = keep.take("tile_e", [1, SHARED_TILES - 2 + GROUP * (WORDS + 1)])
        wk = keep.take("wk", [P, TOPK, TILES])
        gather_at = keep.take("gather_at", [P, TOPK, TILES], I32)
        scatter_at = keep.take("scatter_at", [P, TOPK, TILES], I32)
        tile_experts = keep.take("tile_experts", [1, WORDS], I32)

        ex = Place(nc, keep.at)
        w13 = [ex.take(f"w13_{part}", [P, ALL, 2, FFN], F16) for part in range(3)]
        w2r = [ex.take(f"w2r_{part}", [P, ALL, 6, D], F16) for part in range(2)]
        la = Place(nc, keep.at)
        got = la.take("got", [P, TOPK, TILES, D])
        w_f1 = la.take("w_f1", [P, 2, MLP + QKV17])
        w_f2 = la.take("w_f2", [P, 8, 2, D])
        w_f2s = la.take("w_f2s", [P, 8, D])
        w_r = la.take("w_r", [P, 2, 4])
        gb = la.take("gb", [P, 2, 2])
        ranges = la.take("ranges", [P, 2, 4])
        beta4 = la.take("beta4", [P, 2, 4])
        eye37 = la.take("eye37", [P, NTOK])
        samei = la.take("samei", [P, P])
        tri = la.take("tri", [P, NTOK])
        xr = [la.take(f"xr{j}", [P, 2, 4, 3 * NTOK]) for j in range(2)]
        aot = [la.take(f"aot{j}", [P, 2, 2 * P]) for j in range(2)]
        kc = [la.take(f"kc{j}", [P, 2, 4, NTOK]) for j in range(2)]
        kx = [la.take(f"kx{j}", [P, 4, 12 * NTOK]) for j in range(2)]
        sc = [la.take(f"sc{j}", [P, 2, 12, NTOK]) for j in range(2)]
        vx = [la.take(f"vx{j}", [3 * NTOK, 4, V_COLS]) for j in range(2)]
        mx = [la.take(f"mx{j}", [P, 2, 12]) for j in range(2)]
        lg = [la.take(f"lg{j}", [P, 2, 4]) for j in range(2)]
        pr = [la.take(f"pr{j}", [P, 2, 4]) for j in range(2)]
        l1s = [la.take(f"l1s{j}", [P, 2]) for j in range(2)]
        rank = [la.take(f"rank{j}", [P, 2, 4]) for j in range(2)]
        sg = [la.take(f"sg{j}", [P, 2, 2, 4]) for j in range(2)]
        rsr = [la.take(f"rsr{j}", [P, 2, 4]) for j in range(2)]
        dg = [la.take(f"dg{j}", [P, 2, 4, NTOK]) for j in range(2)]
        gt = [la.take(f"gt{j}", [P, 2, 4, NTOK]) for j in range(2)]
        eq = [la.take(f"eq{j}", [P, 2, 4, NTOK]) for j in range(2)]
        zz = [la.take(f"zz{j}", [P, 2, D]) for j in range(2)]
        qp = [la.take(f"qp{j}", [P, 2, 4, SLOT]) for j in range(2)]
        assert la.at <= ex.at

        sp1 = Place(nc, ex.at)
        stage = [sp1.take(f"stage{r}", [P, FFN]) for r in range(3)]
        sp2 = Place(nc, ex.at)
        w_l1 = sp2.take("w_l1", [P, 2, QKV17])
        w_l1o = sp2.take("w_l1o", [P, 2, D])
        m_causal = sp2.take("m_causal", [P, NTOK])
        m_k = sp2.take("m_k", [P, 12])
        m_v = sp2.take("m_v", [3 * NTOK, V_COLS3])
        assert sp2.at <= sp1.at

        p1 = Place(nc, sp1.at)
        w_tok = p1.take("w_tok", [P, 6, D])
        w_qkv0 = p1.take("w_qkv0", [P, 2, 3 * D])
        w_proj0 = p1.take("w_proj0", [P, 2, D])
        patches = [p1.take(f"patches{t}", [P, 6, P]) for t in range(2)]
        kpos = [p1.take(f"kpos{j}", [P, 2, D]) for j in range(2)]
        v17 = [p1.take(f"v17{j}", [P, 2, NH, 17]) for j in range(2)]
        qt = [p1.take(f"qt{j}", [P, 2, 2 * P]) for j in range(2)]
        p0 = Place(nc, p1.at)
        onehot = p0.take("onehot", [2, P])
        addrows = p0.take("addrows", [2, D])
        kvm = [p1.take(f"kvm{j}", [P, 4, V_COLS]) for j in range(2)]
        p2 = Place(nc, sp1.at)
        positive = p2.take("positive", [P, TILES, 8])
        log_exp = [p2.take(f"log_exp{k}", [P, TILES, 8]) for k in range(3)]
        softplus = p2.take("softplus", [P, TILES, 8])
        score = p2.take("score", [P, TILES, 8])
        ahead = p2.take("ahead", [P, TILES, 8, 8])
        place_of = p2.take("place_of", [P, TILES, 8])
        tri8 = p2.take("tri8", [P, 8, 8])
        lt = p2.take("lt", [P, P])
        ones = p2.take("ones", [P, P])
        product = p2.take("product", [P, TILES, 8])
        rows_of = p2.take("rows_of", [P, TILES, 8])
        gsum = p2.take("gsum", [P, TILES])
        cnt = p2.take("cnt", [P, 4, 8])
        slotf = p2.take("slotf", [P, TOPK, TILES])
        cmpt = p2.take("cmpt", [P, ROUTED_TILES * 8])
        eidf = p2.take("eidf", [P, ROUTED_TILES])
        xg = [p2.take(f"xg{k}", [P, 2 * D], F16) for k in range(2)]
        xt16 = [p2.take(f"xt16{k}", [P, 4, P], F16) for k in range(2)]
        sil = [p2.take(f"sil{g}", [P, 3 * P]) for g in range(2)]
        upc = [p2.take(f"upc{g}", [P, 3 * P]) for g in range(2)]
        h32 = [p2.take(f"h32{g}", [P, 3 * P]) for g in range(2)]
        eh = [p2.take(f"eh{k}", [P, 2, 6, P], F16) for k in range(2)]
        ysb = [p2.take(f"ysb{k}", [P, D]) for k in range(2)]
        p3 = Place(nc, sp1.at)
        pt = [p3.take(f"pt{j}", [3 * NTOK, 2, 4, P]) for j in range(2)]
        hid = [p3.take(f"hid{j}", [P, 6, 4, SLOT]) for j in range(2)]
        yn = [p3.take(f"yn{j}", [P, 2, 256]) for j in range(2)]
        assert max(p1.at, p2.at, p3.at) <= nc.sbuf_usable_end, (p1.at, p2.at, p3.at, nc.sbuf_usable_end)

        tok_in = sem("tok_in"); w_in = sem("w_in"); c1_in = sem("c1_in"); c2_in = sem("c2_in"); r_in = sem("r_in")
        patches_in = [sem("patches_in0"), sem("patches_in1")]
        consts_set = sem("consts_set"); qp_set = sem("qp_set"); consts2_set = sem("consts2_set"); zeros_set = sem("zeros_set"); zeroed = sem("zeroed")
        posb_mm = sem("posb_mm"); posb_set = sem("posb_set"); tok_mm = sem("tok_mm")
        ve1 = sem("ve1"); rs1 = sem("rs1"); xn1 = sem("xn1")
        xt1_mm = sem("xt1_mm"); xt1 = sem("xt1")
        kv_mm = sem("kv_mm"); kset = sem("kset"); vset = sem("vset")
        q_mm = sem("q_mm"); qset = sem("qset")
        kvi_mm = sem("kvi_mm"); kvm_set = sem("kvm_set")
        o_mm = sem("o_mm"); den_e = sem("den_e"); den_set = sem("den_set"); ao_set = sem("ao_set")
        at_mm = sem("at_mm"); at_set = sem("at_set")
        pr_mm = sem("pr_mm")
        stage_in = [sem(f"stage_in{r}") for r in range(3)]
        high_set = sem("high_set"); stage_free = sem("stage_free")
        rows_hi = sem("rows_hi"); rows_set = sem("rows_set"); rows_out = sem("rows_out")
        A0 = {n: sem("g_" + n) for n in "ve rs xn xt_mm xt lg_mm lg abs exp ln sp sq".split()}
        sel_set = sem("sel_set"); count_mm = sem("count_mm"); routed = sem("routed"); scattered = sem("scattered")
        M = {n: sem("m_" + n) for n in "xt_mm xt gate_mm up_mm silu clip h hi lo y_mm y".split()}
        xg_in = [sem("xg_in0"), sem("xg_in1")]
        y_out = [sem("y_out0"), sem("y_out1")]
        shared_zeroed = sem("shared_zeroed"); shared_in = sem("shared_in")
        gathered = [sem("gathered0"), sem("gathered1")]
        NAMES = "xr ve rs xn xt_mm xt k_mm q k kx v_mm vx s_mm mx sub e pt_mm pt o_mm rden ao at_mm at h".split()
        A1 = {n: sem("l1_" + n) for n in NAMES + ["pr_mm"]}
        A2 = {n: sem("f_" + n) for n in NAMES + "kx2 lg_mm lgmx lgsub lgexp lgsum lgrec p dg bc_mm cmp cmp2 rank ve2 rs2 rsr yn yt_mm yt mlp_mm gelu fc_mm".split()}
        beta4_set = sem("beta4_set"); bw_mm = sem("bw_mm"); bw_added = sem("bw_added"); bw_set = sem("bw_set"); w2_set = sem("w2_set")
        out_done = sem("out_done")

        block = ctx.enter_context(nc.Block())
        embedding = ((onehot, tok_onehot), (addrows, tok_addrows), (pos_bias, tok_pos), (w_tok, tok_w), (ident, ident_in))
        first = ((w_qkv0, l0_qkv), (mask17, hmask17), (w_proj0, l0_proj), (w_g, gate_w), (gbias, gate_bias),
                 (route, route_c))
        second = ((tri8, before8), (lt, lt_in), (ones, ones_in))
        third = ((w_l1, l1_w), (w_l1o, l1_out), (m_causal, l1_mask), (m_k, kmask), (m_v, vmask))
        fourth = ((w_f1, ffn_w1), (gb, ffn_gb), (ranges, ffn_ranges), (w_f2, ffn_w2), (w_r, ffn_router), (eye37, slot_eye), (samei, same_image), (tri, earlier))

        def bank(j, n):
            return banks[:, 4 * j + n]

        third_cols = (MLP + QKV17) // 3

        def routed_rows(k):
            return xs[bass.ds(P * k, P), :]

        @block.sync
        def _(sp):
            for dst, src in embedding:
                sp.dma_start(dst, src).then_inc(tok_in, 16)
            for dst, src in first:
                sp.dma_start(dst, src).then_inc(w_in, 16)
            def load_stage(e, u):
                if u < 4:
                    src, dst = moe_13.rearrange("e u p f -> (e u) p f")[bass.ds(4 * e + u, 1)].rearrange("o p f -> (o p) f"), stage[u % 3]
                else:
                    src, dst = moe_2.rearrange("e u p f -> (e u) p f")[bass.ds(2 * e + u - 4, 1)].rearrange("o p f -> (o p) f"), stage[u % 3][:, 0:3 * D]
                sp.dma_start(dst, src).then_inc(stage_in[u % 3], 16)

            for u in range(3):
                load_stage(0, u)
            sp.wait_ge(zeros_set, 1)
            zeros = rows16[:, TILES - 1, :]
            sp.dma_start(xs[NIMG * NTOK:SHARED_TILES * P], zeros[0:SHARED_TILES * P - NIMG * NTOK]).then_inc(zeroed, 16)
            with sp.Fori(0, ZERO_STORES) as it:
                for q in range(12):
                    sp.wait_ge(stage_free, 12 * it + q + 1)
                    load_stage(2 * it + (q + 3) // UNITS, (q + 3) % UNITS)
                    if q == UNITS:
                        sp.dma_start(xs[bass.ds(SHARED_TILES * P + ZERO_TILES * P * it, ZERO_TILES * P)].rearrange("(n p) f -> p n f", p=P),
                                     zeros.unsqueeze(1).to_broadcast([P, ZERO_TILES, 2 * D])).then_inc(zeroed, 16)
            sp.wait_ge(pr_mm, DUOS)
            for dst, src in second:
                sp.dma_start(dst, src).then_inc(r_in, 16)
            def load_rows(k, par):
                sp.dma_start(xg[par], routed_rows(k)).then_inc(xg_in[par], 16)

            def store_rows(k, par):
                sp.wait_ge(M["y"], k + 1)
                sp.dma_start(ys[bass.ds(P * k, P), :], ysb[par]).then_inc(y_out[par], 16)

            sp.wait_ge(rows_out, 32 * (DUOS - 1))
            load_rows(0, 0)
            load_rows(1, 1)
            sp.wait_ge(rows_out, 32 * DUOS)
            sp.wait_ge(zeroed, 16 * (ZERO_STORES + 1))
            sp.wait_ge(M["xt_mm"], 1)
            load_rows(2, 0)
            sp.wait_ge(M["xt_mm"], 2)
            load_rows(3, 1)
            store_rows(0, 0)
            sp.wait_ge(M["xt_mm"], 3)
            load_rows(4, 0)
            for u in range(3, UNITS):
                sp.wait_ge(stage_free, UNITS * EXPERTS + u - 2)
                load_stage(EXPERTS, u)
            store_rows(1, 1)
            sp.wait_ge(M["xt_mm"], 4)
            load_rows(5, 1)
            store_rows(2, 0)
            with sp.Fori(1, SHARED_TILES // 2 - 2) as it:
                for par in range(2):
                    sp.wait_ge(M["xt_mm"], 2 * it + par + 3)
                    load_rows(2 * it + par + 4, par)
                    store_rows(2 * it + par + 1, 1 - par)
            sp.wait_ge(stage_free, UNITS * ALL)
            for dst, src in third:
                sp.dma_start(dst, src).then_inc(c1_in, 16)
            sp.wait_ge(scattered, 16 * TOPK * TILES)
            with sp.Fori(0, (MTILES - SHARED_TILES) // 2) as it:
                for par in range(2):
                    sp.wait_ge(M["xt_mm"], 2 * it + par + SHARED_TILES - 1)
                    load_rows(2 * it + par + SHARED_TILES, par)
                    store_rows(2 * it + par + SHARED_TILES - 3, 1 - par)
            store_rows(MTILES - 3, 1)
            store_rows(MTILES - 2, 0)
            store_rows(MTILES - 1, 1)
            sp.wait_ge(M["y_mm"], MTILES)
            for dst, src in fourth:
                sp.dma_start(dst, src).then_inc(c2_in, 16)
            sp.wait_ge(A2["h"], DUOS)
            for im in range(2):
                o = out.rearrange("(t i) n d -> i n t d", i=2)[im]
                sp.dma_start(o, h[SLOT * im:SLOT * im + NTOK, :, :]).then_inc(out_done, 16)
            sp.wait_ge(out_done, 32)

        @block.gpsimd
        def _(pool):
            pool.memset(rows16[:, TILES - 1, :], 0.0).then_inc(zeros_set, 1)
            pool.memset(neghalf, -0.5)
            pool.memset(tile_e, 0.0)
            for j in range(2):
                pool.memset(xn[j][:, :, 192:193], 1.0)
                pool.memset(xn[j][:, :, 193:256], 0.0)
                pool.memset(ao[j][:, :, 192:193], 1.0)
                pool.memset(ao[j][:, :, 193:256], 0.0)
                ins = pool.memset(v17[j][:, :, :, 16:17], 1.0)
            ins.then_inc(consts_set, 1)

            def load_patches(tile, t):
                pool.dma_start(patches[t], x_patches[bass.ds(tile, 1)].rearrange("o p c n -> (o p) c n")).then_inc(patches_in[t], 16)

            load_patches(0, 0)
            load_patches(1, 1)

            def root0(d, ready, done, place):
                pool.wait_ge(ready, d + 1)
                pool.tensor_tensor(place[1], place[0], neghalf, ALU.pow).then_inc(done, 1)

            def next_patches(d):
                for t in range(2):
                    pool.wait_ge(tok_mm, 2 * d + t - 1)
                    load_patches(2 * d + t, t)

            def rows_to_dram(d):
                pool.wait_ge(rows_set, d + 1)
                for im in range(2):
                    pool.dma_start(xs[0:NIMG * NTOK].rearrange("(t i n) f -> i n t f", i=2, n=NTOK)[im][:, bass.ds(2 * d, 2), :],
                                   rows16[SLOT * im:SLOT * im + NTOK, bass.ds(2 * d, 2), :]).then_inc(rows_out, 16)

            def embed_step(d, j, first, last, most):
                if not first:
                    root0(d - 1, A0["ve"], A0["rs"], (ve2[1 - j], rs2[1 - j]))
                if not last:
                    if most:
                        next_patches(d + 2)
                    root0(d + 1, ve1, rs1, (ve[1 - j], rs[1 - j]))
                if not first:
                    rows_to_dram(d - 1)

            root0(0, ve1, rs1, (ve[0], rs[0]))
            next_patches(1)
            embed_step(0, 0, True, False, True)
            with pool.Fori(0, DUOS // 2 - 2) as it:
                for i in range(2):
                    embed_step(2 * it + 1 + i, 1 - i, False, False, True)
            embed_step(DUOS - 3, 1, False, False, True)
            embed_step(DUOS - 2, 0, False, False, False)
            embed_step(DUOS - 1, 1, False, True, False)
            root0(DUOS - 1, A0["ve"], A0["rs"], (ve2[1], rs2[1]))
            pool.wait_ge(rows_out, 32 * (DUOS - 1))
            rows_to_dram(DUOS - 1)
            pool.wait_ge(routed, 1)
            pool.wait_ge(zeroed, 16 * (ZERO_STORES + 1))
            for k in range(TOPK):
                for t in range(TILES):
                    pool.indirect_dma_start(out=xs, out_offset=bass.IndirectOffsetOnAxis(ap=scatter_at[:, k, t:t + 1], axis=0),
                                            in_=rows16[:, t, :], in_offset=None).then_inc(scattered, 16)
            pool.wait_ge(scattered, 16 * TOPK * TILES)
            pool.wait_ge(rows_out, 32 * DUOS)
            pool.memset(shared_y, 0.0).then_inc(shared_zeroed, 1)
            pool.wait_ge(shared_zeroed, 1)
            for par in range(2):
                pool.wait_ge(y_out[par], 16 * SHARED_TILES // 2)
            for im in range(2):
                pool.dma_start(shared_y[SLOT * im:SLOT * im + NTOK, :, :],
                               ys[0:NIMG * NTOK].rearrange("(t i n) d -> i n t d", i=2, n=NTOK)[im]).then_inc(shared_in, 16)
            for par in range(2):
                pool.wait_ge(y_out[par], 16 * MTILES // 2)
            pool.wait_ge(M["y_mm"], MTILES)

            def gather(d, j):
                for i in range(2):
                    for k in range(TOPK):
                        pool.indirect_dma_start(out=got[:, k, 2 * d + i, :], out_offset=None, in_=ys,
                                                in_offset=bass.IndirectOffsetOnAxis(ap=gather_at[:, k, 2 * d + i:2 * d + i + 1], axis=0)).then_inc(gathered[j], 16)

            def root(a, d, j, ready="ve", done="rs"):
                pool.wait_ge(a[ready], d + 1)
                pool.tensor_tensor(rs[j], ve[j], neghalf, ALU.pow).then_inc(a[done], 1)

            def head_keys(a, d, j, images):
                pool.wait_ge(a["k"], d + 1)
                for h0, nh, c in ((0, 8, 0), (8, 4, 1)):
                    for im in images:
                        ins = pool.tensor_tensor(kx[j][:, im, NTOK * h0:NTOK * (h0 + nh)].rearrange("p (h n) -> p h n", h=nh),
                                                 kc[j][:, c, im].unsqueeze(1).to_broadcast([P, nh, NTOK]),
                                                 m_k[:, h0:h0 + nh].unsqueeze(2).to_broadcast([P, nh, NTOK]), ALU.mult)
                ins.then_inc(a["kx"], 1)

            gather(0, 0)
            gather(1, 1)
            root(A1, 0, 0)
            gather(2, 0)
            root(A1, 1, 1)
            for j in range(2):
                ins = pool.memset(qp[j], 0.0)
            ins.then_inc(qp_set, 1)
            pool.wait_ge(c2_in, 16 * len(fourth))
            for c in range(2):
                ins = pool.tensor_tensor(beta4[:, c], ranges[:, c], gb[:, c, 1:2].to_broadcast([P, 4]), ALU.mult)
            ins.then_inc(beta4_set, 1)
            pool.wait_ge(c1_in, 16 * len(third))
            head_keys(A1, 0, 0, range(4))

            def attention_step(d, j, more):
                head_keys(A1, d + 1, 1 - j, range(4))
                if more:
                    root(A1, d + 2, j)
                if d + 3 < DUOS:
                    gather(d + 3, 1 - j)
                if d == DUOS - 3:
                    for j2 in range(2):
                        pool.memset(hid[j2], 0.0)
                        pool.memset(yn[j2][:, :, 196:197], 1.0)
                        ins = pool.memset(yn[j2][:, :, 197:256], 0.0)
                    ins.then_inc(consts2_set, 1)
                    pool.tensor_tensor(w_f2s, w_f2[:, :, 0, :], w_f2[:, :, 1, :], ALU.add).then_inc(w2_set, 1)

            for d in range(DUOS - 1):
                attention_step(d, d % 2, d < DUOS - 2)
            def ffn_roots(d, j):
                root(A2, d, j)
                root(A2, d, j, "ve2", "rs2")

            ffn_roots(0, 0)
            ffn_roots(1, 1)
            with pool.Fori(0, DUOS // 2 - 1) as it:
                for j in range(2):
                    head_keys(A2, 2 * it + j, j, range(2))
                    ffn_roots(2 * it + j + 2, j)
            head_keys(A2, DUOS - 2, 0, range(2))
            head_keys(A2, DUOS - 1, 1, range(2))

        @block.tensor
        def _(pe):
            def turned_duo(src, b, d, j, ready, done):
                pe.wait_ge(ready, d + 1)
                for c in range(2):
                    for t in range(2):
                        mm = pe.transpose(bank(j, b)[:, (2 * c + t) * P:(2 * c + t + 1) * P], src[j][:, t, c * P:(c + 1) * P], ident)
                mm.then_inc(done, 1)

            def tokens(d, j):
                for t in range(2):
                    pe.wait_ge(patches_in[t], 16 * d + 16)
                    for c in range(6):
                        mm = pe.matmul(bank(j, 0)[:, t * D:(t + 1) * D], patches[t][:, c, :], w_tok[:, c, :], start=(c == 0), stop=(c == 5))
                    mm.then_inc(tok_mm, 1)

            def rows_by_weights(o, cols, j, k1, t, w, f):
                pe.matmul(o, cols[j][:, 0, P * t:P * t + P], w[:, 0, f], start=True, stop=False)
                return pe.matmul(o, cols[j][0:k1, 1, P * t:P * t + P], w[0:k1, 1, f], start=False, stop=True)

            def keys_values(d, j):
                pe.wait_ge(xt1, d + 1)
                for b, f in ((2, slice(D, 2 * D)), (3, slice(2 * D, 3 * D))):
                    for t in range(2):
                        mm = rows_by_weights(bank(j, b)[:, t * D:(t + 1) * D], xc, j, 64, t, w_qkv0, f)
                mm.then_inc(kv_mm, 1)

            def queries(d, j):
                for c in range(2):
                    f = slice(64 * c, 64 * c + P)
                    o = bank(j, 0)[:, 256 * c:256 * c + 256]
                    pe.matmul(o, w_qkv0[:, 0, f], xc[j][:, 0, :], start=True, stop=False)
                    mm = pe.matmul(o, w_qkv0[0:64, 1, f], xc[j][0:64, 1, :], start=False, stop=True)
                mm.then_inc(q_mm, 1)

            def keys_by_values(d, j):
                pe.wait_ge(kset, d + 1)
                pe.wait_ge(vset, d + 1)
                for t in range(2):
                    for im in range(2):
                        r = slice(SLOT * im, SLOT * im + NTOK)
                        o = bank(j, 2 + im)[:, V_COLS * t:V_COLS * t + V_COLS]
                        vr = v17[j][r, t].rearrange("p h e -> p (h e)")
                        pe.matmul(o[:, 0:V_COLS0], kpos[j][r, t, 0:P], vr[:, 0:V_COLS0], start=True, stop=True)
                        mm = pe.matmul(o[:, V_COLS0:V_COLS], kpos[j][r, t, 64:192], vr[:, V_COLS0:V_COLS], start=True, stop=True)
                mm.then_inc(kvi_mm, 1)

            def queries_by_sums(d, j):
                pe.wait_ge(qset, d + 1)
                pe.wait_ge(kvm_set, d + 1)
                for t in range(2):
                    for im in range(2):
                        o = bank(j, 1)[SLOT * im:SLOT * im + SLOT, V_COLS * t:V_COLS * t + V_COLS]
                        q0 = P * t + SLOT * im
                        pe.matmul(o[:, 0:V_COLS0], qt[j][:, 0, q0:q0 + SLOT], kvm[j][:, 2 * im + t, 0:V_COLS0], start=True, stop=True)
                        mm = pe.matmul(o[:, V_COLS0:V_COLS], qt[j][:, 1, q0:q0 + SLOT], kvm[j][:, 2 * im + t, V_COLS0:V_COLS], start=True, stop=True)
                mm.then_inc(o_mm, 1)

            def projection(d, j):
                pe.wait_ge(at_set, d + 1)
                for t in range(2):
                    mm = rows_by_weights(bank(j, 2)[:, t * D:(t + 1) * D], xc, j, 65, t, w_proj0, slice(0, D))
                mm.then_inc(pr_mm, 1)

            def gate_logits(d, j):
                pe.wait_ge(A0["xt"], d + 1)
                for t in range(2):
                    mm = rows_by_weights(bank(j, 2)[:, 8 * t:8 * t + 8], xc, j, 64, t, w_g, slice(0, 8))
                mm.then_inc(A0["lg_mm"], 1)

            def embed_step(d, j, first, last):
                if not last:
                    tokens(d + 1, 1 - j)
                keys_by_values(d, j)
                if not first:
                    turned_duo(xn, 3, d - 1, 1 - j, A0["xn"], A0["xt_mm"])
                    gate_logits(d - 1, 1 - j)
                queries_by_sums(d, j)
                if not last:
                    turned_duo(xn, 1, d + 1, 1 - j, xn1, xt1_mm)
                    if not first:
                        pe.wait_ge(A0["lg"], d)
                    keys_values(d + 1, 1 - j)
                turned_duo(ao, 0, d, j, ao_set, at_mm)
                if not last:
                    queries(d + 1, 1 - j)
                projection(d, j)

            pe.wait_ge(tok_in, 16 * len(embedding))
            pe.matmul(bank(1, 0)[:, 0:D], onehot, addrows, start=True, stop=True).then_inc(posb_mm, 1)
            tokens(0, 0)
            pe.wait_ge(posb_set, 1)
            turned_duo(xn, 1, 0, 0, xn1, xt1_mm)
            pe.wait_ge(w_in, 16 * len(first))
            keys_values(0, 0)
            queries(0, 0)
            embed_step(0, 0, True, False)
            with pe.Fori(0, DUOS // 2 - 1) as it:
                for i in range(2):
                    embed_step(2 * it + 1 + i, 1 - i, False, False)
            embed_step(DUOS - 1, 1, False, True)
            turned_duo(xn, 3, DUOS - 1, 1, A0["xn"], A0["xt_mm"])
            gate_logits(DUOS - 1, 1)

            def turn_rows(k, par):
                pe.wait_ge(xg_in[par], 8 * (k - par) + 16)
                o = banks[:, 0].bitcast(F16)
                pe.transpose(o[:, 0:P], xg[par][:, 0:P], ident16)
                for i, c0 in ((1, P), (3, D + P)):
                    for half in range(2):
                        mm = pe.transpose(o[64 * half:64 * half + 64, P * i:P * i + P], xg[par][:, c0:c0 + 64], ident16)
                pe.transpose(o[:, 2 * P:3 * P], xg[par][:, D:D + P], ident16).then_inc(M["xt_mm"], 1)

            def gate_up(k, par, e, first=False):
                pe.wait_ge(M["xt"], k + 1)
                for g in range(2):
                    for m, b, free, done in ((0, 1, "silu", "gate_mm"), (1, 3, "clip", "up_mm")):
                        if not first:
                            pe.wait_ge(M[free], 2 * k + g - 1)
                        for f in range(3):
                            o = banks[:, b + g, P * f:P * f + P]
                            c0 = P * (3 * g + f)
                            for i, (part, x) in enumerate(((0, 0), (0, 2), (1, 0), (2, 1), (2, 3))):
                                w = w13[part][:, bass.ds(e, 1), m, c0:c0 + P].rearrange("p o f -> p (o f)")
                                mm = pe.matmul(o, w, xt16[par][:, x, :], start=(i == 0), stop=(i == 4))
                        mm.then_inc(M[done], 1)

            def down(k, par, e):
                pe.wait_ge(M["lo"], 2 * k + 2)
                o = banks[:, 5 + par, 0:D]
                for f in range(6):
                    for i, (hx, wx) in enumerate(((0, 0), (1, 0), (0, 1))):
                        w = w2r[wx][:, bass.ds(e, 1), f, :].rearrange("p o d -> p (o d)")
                        mm = pe.matmul(o, eh[par][:, hx, f, :], w, start=(f == 0 and i == 0), stop=(f == 5 and i == 2))
                mm.then_inc(M["y_mm"], 1)

            pe.wait_ge(stage_free, UNITS * EXPERTS)
            turn_rows(0, 0)
            pe.wait_ge(M["xt"], 1)
            turn_rows(1, 1)
            gate_up(0, 0, 0, first=True)

            pe.wait_ge(r_in, 16 * len(second))
            pe.wait_ge(sel_set, 1)
            places = banks[:, 7][:, 0:8 * (TILES + 1)]
            pe.matmul(places, lt, sel.rearrange("p t e -> p (t e)"), start=True, stop=False)
            for t in range(TILES):
                mm = pe.matmul(places.rearrange("p (t e) -> p t e", e=8)[:, t + 1:, :], ones,
                               sel[:, t:t + 1, :].to_broadcast([P, TILES - t, 8]), start=False, stop=(t == TILES - 1))
            mm.then_inc(count_mm, 1)

            with pe.Fori(0, SHARED_TILES // 2 - 1) as it:
                for par in range(2):
                    k = 2 * it + 1 + par
                    pe.wait_ge(M["xt"], k + 1)
                    turn_rows(k + 1, par)
                    gate_up(k, 1 - par, 0)
                    down(k - 1, par, 0)
            pe.wait_ge(stage_free, UNITS * ALL)
            pe.wait_ge(routed, 1)
            def expert(word, n):
                return (word // ALL ** n) % ALL

            def word_of(n):
                return pe.value_load(tile_experts[0:1, bass.ds(n, 1)], min_val=0, max_val=WORD_MAX)

            def routed_tile(k, par, word, n):
                pe.wait_ge(M["xt"], k + 1)
                turn_rows(k + 1, par)
                gate_up(k, 1 - par, expert(word, n + 1))
                down(k - 1, par, expert(word, n))

            assert ROUTED_TILES % GROUP == 2
            with pe.Fori(0, WORDS - 1) as it:
                word = word_of(it)
                for n in range(GROUP):
                    routed_tile(GROUP * it + SHARED_TILES - 1 + n, n % 2, word, n)
            word = word_of(WORDS - 1)
            for n in range(2):
                routed_tile(MTILES - 3 + n, n, word, n)
            gate_up(MTILES - 1, 1, expert(word, 3))
            down(MTILES - 2, 0, expert(word, 2))
            down(MTILES - 1, 1, expert(word, 3))

            def toks(buf, j, k, c):
                return buf[j][0:k, c].rearrange("p (i s) -> p i s", s=SLOT)[:, :, 0:NTOK]

            def queries_keys(a, w, f0, k1, d, j, x_set):
                pe.wait_ge(x_set, d + 1)
                for b, g in ((1, f0), (2, f0 + D)):
                    for c in range(2):
                        f = slice(g + 64 * c, g + 64 * c + P)
                        o = bank(j, b)[:, TOKENS4 * c:TOKENS4 * c + TOKENS4].rearrange("p (i n) -> p i n", n=NTOK)
                        pe.matmul(o, w[:, 0, f], toks(xc, j, P, 0), start=True, stop=False)
                        mm = pe.matmul(o, w[0:k1, 1, f], toks(xc, j, k1, 1), start=False, stop=True)
                mm.then_inc(a["k_mm"], 1)

            def values(a, w, f0, k1, d, j, images=(0, 1)):
                pe.wait_ge(a["xr"], d + 1)
                for im in images:
                    for t in range(2):
                        f = slice(f0 + 2 * D, f0 + QKV17)
                        o = bank(j, 3 - 3 * im)[0:3 * NTOK, V_COLS * t:V_COLS * t + V_COLS]
                        pe.matmul(o, xr[j][:, 0, 2 * t + im], w[:, 0, f], start=True, stop=False)
                        mm = pe.matmul(o, xr[j][0:k1, 1, 2 * t + im], w[0:k1, 1, f], start=False, stop=True)
                if 1 in images:
                    mm.then_inc(a["v_mm"], 1)

            def scores(a, d, j):
                pe.wait_ge(a["q"], d + 1)
                pe.wait_ge(a["kx"], d + 1)
                if a is A2:
                    pe.wait_ge(a["kx2"], d + 1)
                for t in range(2):
                    for im in range(2):
                        o = bank(j, 1 + t)[SLOT * im:SLOT * im + SLOT, 0:KEY_COLS]
                        i = 2 * t + im
                        pe.matmul(o[:, 0:KEY_COLS0], qp[j][:, 0, i, :], kx[j][:, i, 0:KEY_COLS0], start=True, stop=True)
                        mm = pe.matmul(o[:, KEY_COLS0:KEY_COLS], qp[j][:, 1, i, :], kx[j][:, i, KEY_COLS0:KEY_COLS], start=True, stop=True)
                mm.then_inc(a["s_mm"], 1)

            def turned_probs(a, d, j):
                pe.wait_ge(a["e"], d + 1)
                for t in range(2):
                    for g in range(4):
                        mm = pe.transpose(bank(j, 1 + t)[0:TOKENS3, P * g:P * g + P],
                                          sc[j][:, t, 3 * g:3 * g + 3, :].rearrange("p h n -> p (h n)"), ident)
                mm.then_inc(a["pt_mm"], 1)

            def weighted_values(a, d, j):
                pe.wait_ge(a["pt"], d + 1)
                pe.wait_ge(a["vx"], d + 1)
                for t in range(2):
                    for im in range(2):
                        for g in range(4):
                            o = bank(j, 1)[SLOT * im:SLOT * im + SLOT, V_COLS * t + V_COLS3 * g:V_COLS * t + V_COLS3 * g + V_COLS3]
                            mm = pe.matmul(o, pt[j][:, t, g, SLOT * im:SLOT * im + SLOT], vx[j][:, 2 * im + t, V_COLS3 * g:V_COLS3 * g + V_COLS3], start=True, stop=True)
                mm.then_inc(a["o_mm"], 1)

            def router(d, j):
                pe.wait_ge(A2["xt"], d + 1)
                for t in range(2):
                    o = bank(j, 1)[:, 4 * t:4 * t + 4]
                    pe.matmul(o, xc[j][:, 0, P * t:P * t + P], w_r[:, 0, :], start=True, stop=False)
                    mm = pe.matmul(o, xc[j][0:64, 1, P * t:P * t + P], w_r[0:64, 1, :], start=False, stop=True)
                mm.then_inc(A2["lg_mm"], 1)

            def spread_probs(d, j):
                pe.wait_ge(A2["dg"], d + 1)
                pe.matmul(bank(j, 2)[:, 0:KEY_COLS0], samei, dg[j].rearrange("p t e n -> p (t e n)"), start=True, stop=True).then_inc(A2["bc_mm"], 1)

            def attention_step(d, j, more, most):
                if more:
                    queries_keys(A1, w_l1, 0, 65, d + 1, 1 - j, A1["xt"])
                    pe.wait_ge(A1["mx"], d + 1)
                    values(A1, w_l1, 0, 65, d + 1, 1 - j, (0,))
                turned_probs(A1, d, j)
                if more:
                    values(A1, w_l1, 0, 65, d + 1, 1 - j, (1,))
                else:
                    spread_probs(0, 0)
                weighted_values(A1, d, j)
                if more:
                    scores(A1, d + 1, 1 - j)
                turned_duo(ao, 2, d, j, A1["ao"], A1["at_mm"])
                if most:
                    turned_duo(xn, 0, d + 2, j, A1["xn"], A1["xt_mm"])
                pe.wait_ge(A1["at"], d + 1)
                for t in range(2):
                    mm = rows_by_weights(bank(j, 3)[:, t * D:(t + 1) * D], aot, j, 65, t, w_l1o, slice(0, D))
                mm.then_inc(A1["pr_mm"], 1)

            pe.wait_ge(c1_in, 16 * len(third))
            turned_duo(xn, 0, 0, 0, A1["xn"], A1["xt_mm"])
            queries_keys(A1, w_l1, 0, 65, 0, 0, A1["xt"])
            values(A1, w_l1, 0, 65, 0, 0)
            turned_duo(xn, 0, 1, 1, A1["xn"], A1["xt_mm"])
            pe.wait_ge(beta4_set, 1)
            for n0 in range(3):
                f = slice(third_cols * n0, third_cols * n0 + third_cols)
                o = banks[64:68, 5 + n0, 0:third_cols]
                pe.matmul(o, beta4[:, 0, :], w_f1[:, 0, f], start=True, stop=False)
                mm = pe.matmul(o, beta4[0:64, 1, :], w_f1[0:64, 1, f], start=False, stop=True)
            mm.then_inc(bw_mm, 1)
            pe.wait_ge(qp_set, 1)
            scores(A1, 0, 0)
            pe.wait_ge(bw_added, 1)
            with pe.Fori(0, DUOS // 2 - 1) as it:
                for j in range(2):
                    attention_step(2 * it + j, j, True, True)
            attention_step(DUOS - 2, 0, True, False)
            turned_duo(xn, 0, 0, 0, A2["xn"], A2["xt_mm"])
            router(0, 0)
            attention_step(DUOS - 1, 1, False, False)

            def mlp_in(d, j, b):
                for i in range(3):
                    f = slice(P * (3 * b + i), P * (3 * b + i + 1))
                    o = bank(j, 3 * b)[:, TOKENS4 * i:TOKENS4 * i + TOKENS4].rearrange("p (i n) -> p i n", n=NTOK)
                    pe.matmul(o, w_f1[:, 0, f], toks(xc, j, P, 0), start=True, stop=False)
                    mm = pe.matmul(o, w_f1[0:69, 1, f], toks(xc, j, 69, 1), start=False, stop=True)
                mm.then_inc(A2["mlp_mm"], 1)

            def ffn_step(d, j, first, last):
                queries_keys(A2, w_f1, MLP, 69, d, j, A2["yt"])
                values(A2, w_f1, MLP, 69, d, j)
                scores(A2, d, j)
                if not last:
                    if not first:
                        pe.wait_ge(A2["h"], d)
                    turned_duo(xn, 0, d + 1, 1 - j, A2["xn"], A2["xt_mm"])
                pe.wait_ge(A2["vx"], d + 1)
                mlp_in(d, j, 0)
                mlp_in(d, j, 1)
                turned_probs(A2, d, j)
                if not last:
                    router(d + 1, 1 - j)
                weighted_values(A2, d, j)
                if not last:
                    spread_probs(d + 1, 1 - j)
                pe.wait_ge(A2["gelu"], d + 1)
                for t in range(2):
                    for c in range(6):
                        pe.matmul(bank(j, 3 * t)[:, 0:D], hid[j][:, c, 2 * t:2 * t + 2, :].rearrange("p i s -> p (i s)"), w_f2s[:, c, :], start=(c == 0), stop=False)
                turned_duo(ao, 2, d, j, A2["ao"], A2["at_mm"])
                if not last:
                    turned_duo(yn, 0, d + 1, 1 - j, A2["yn"], A2["yt_mm"])
                pe.wait_ge(A2["at"], d + 1)
                for t in range(2):
                    o = bank(j, 3 * t)[:, 0:D]
                    pe.matmul(o, xc[j][:, 0, P * t:P * t + P], w_f2s[:, 6, :], start=False, stop=False)
                    mm = pe.matmul(o, xc[j][0:65, 1, P * t:P * t + P], w_f2s[0:65, 7, :], start=False, stop=True)
                mm.then_inc(A2["fc_mm"], 1)

            pe.wait_ge(bw_set, 1)
            pe.wait_ge(w2_set, 1)
            pe.wait_ge(consts2_set, 1)
            turned_duo(yn, 0, 0, 0, A2["yn"], A2["yt_mm"])
            ffn_step(0, 0, True, False)
            with pe.Fori(0, DUOS // 2 - 1) as it:
                for i in range(2):
                    ffn_step(2 * it + 1 + i, 1 - i, False, False)
            ffn_step(DUOS - 1, 1, False, True)

        @block.scalar
        def _(act):
            def high(e, u, wait):
                act.wait_ge(stage_in[u % 3], wait)
                if u < 4:
                    dst = w13[2 * (u % 2)][:, bass.ds(e, 1), u // 2, :].rearrange("p o f -> p (o f)")
                    src = stage[u % 3]
                else:
                    dst = w2r[0][:, bass.ds(e, 1), 3 * (u - 4):3 * (u - 4) + 3, :].rearrange("p o c d -> p (o c) d")
                    src = stage[u % 3][:, 0:3 * D].rearrange("p (c d) -> p c d", c=3)
                act.activation(dst, src, ACT.Copy, scale=WSCALE).then_inc(high_set, 1)

            act.wait_ge(tok_in, 16 * len(embedding))
            act.copy(ident16, ident)

            def columns_duo(b, d, j, ready, done, cols):
                act.wait_ge(ready, d + 1)
                act.copy(cols[j].rearrange("p c n -> p (c n)"), bank(j, b)).then_inc(done, 1)

            def units(e, a, b):
                for u in range(a, b):
                    high(e, u, 32 * e + 16 * (u // 3) + 16)

            def rows_high(d, j):
                act.wait_ge(A0["xn"], d + 1)
                act.activation(rows16[:, bass.ds(2 * d, 2), 0:D], xn[j][:, :, 0:D], ACT.Copy, scale=XSCALE).then_inc(rows_hi, 1)

            def values17(d, j):
                act.wait_ge(kv_mm, d + 1)
                act.copy(v17[j][:, :, :, 0:16], bank(j, 3)[:, 0:2 * D].rearrange("p (t h e) -> p t h e", t=2, h=NH)).then_inc(vset, 1)

            def embed_step(d, j, last):
                units(d, 0, 1)
                rows_high(d - 1, 1 - j)
                units(d, 1, 2)
                columns_duo(3, d - 1, 1 - j, A0["xt_mm"], A0["xt"], xc)
                units(d, 2, 3)
                if not last:
                    columns_duo(1, d + 1, 1 - j, xt1_mm, xt1, xc)
                units(d, 3, 4 if last else 6)
                if not last:
                    values17(d + 1, 1 - j)
                columns_duo(0, d, j, at_mm, at_set, xc)
                if last:
                    units(d, 4, 6)

            act.wait_ge(consts_set, 1)
            columns_duo(1, 0, 0, xt1_mm, xt1, xc)
            values17(0, 0)
            units(0, 0, 2)
            columns_duo(1, 1, 1, xt1_mm, xt1, xc)
            units(0, 2, 4)
            values17(1, 1)
            columns_duo(0, 0, 0, at_mm, at_set, xc)
            units(0, 4, 6)
            with act.Fori(0, DUOS // 2 - 1) as it:
                for i in range(2):
                    embed_step(2 * it + 1 + i, 1 - i, False)
            embed_step(DUOS - 1, 1, True)
            act.wait_ge(zeroed, 16 * (ZERO_STORES + 1))
            rows_high(DUOS - 1, 1)
            columns_duo(3, DUOS - 1, 1, A0["xt_mm"], A0["xt"], xc)

            def turned(k, par):
                act.wait_ge(M["xt_mm"], k + 1)
                act.copy(xt16[par].rearrange("p c n -> p (c n)"), banks[:, 0].bitcast(F16)[:, 0:4 * P]).then_inc(M["xt"], 1)

            def hidden(k, par, first=False):
                for g in range(2):
                    act.wait_ge(M["gate_mm"], 2 * k + g + 1)
                    if not first:
                        act.wait_ge(M["h"], 2 * k + g - 1)
                    act.activation(sil[g], banks[:, 1 + g, 0:3 * P], ACT.Silu, scale=1 / (XSCALE * WSCALE)).then_inc(M["silu"], 1)
                for g in range(2):
                    act.wait_ge(M["h"], 2 * k + g + 1)
                    act.copy(eh[par][:, 0, 3 * g:3 * g + 3, :].rearrange("p f n -> p (f n)"), h32[g]).then_inc(M["hi"], 1)

            def result(k, par, first=False):
                act.wait_ge(M["y_mm"], k + 1)
                if not first:
                    act.wait_ge(y_out[par], 8 * (k - par))
                act.activation(ysb[par], banks[:, 5 + par, 0:D], ACT.Copy, scale=1 / (XSCALE * WSCALE * WSCALE)).then_inc(M["y"], 1)

            act.wait_ge(A0["lg"], DUOS)
            act.activation(log_exp[0], glog, ACT.Abs).then_inc(A0["abs"], 1)
            act.wait_ge(A0["abs"], 1)
            act.activation(log_exp[1], log_exp[0], ACT.Exp, scale=-1.0).then_inc(A0["exp"], 1)
            act.wait_ge(A0["exp"], 1)
            act.activation(log_exp[2], log_exp[1], ACT.Ln, bias=1.0).then_inc(A0["ln"], 1)
            turned(0, 0)
            act.wait_ge(A0["sp"], 1)
            act.activation(root_score, softplus, ACT.Sqrt).then_inc(A0["sq"], 1)
            turned(1, 1)
            hidden(0, 0, first=True)
            turned(2, 0)
            hidden(1, 1)
            result(0, 0, first=True)
            units(EXPERTS, 0, 3)
            turned(3, 1)
            hidden(2, 0)
            result(1, 1, first=True)
            units(EXPERTS, 3, 6)
            with act.Fori(0, MTILES // 2 - 2) as it:
                for par in range(2):
                    k = 2 * it + 3 + par
                    turned(k + 1, par)
                    hidden(k, 1 - par)
                    result(k - 1, par)
            hidden(MTILES - 1, 1)
            result(MTILES - 2, 0)
            result(MTILES - 1, 1)

            def three_copies(a, d, j, x_set):
                act.wait_ge(x_set, d + 1)
                for c in range(2):
                    ins = act.copy(xr[j][:, c].rearrange("p i (r n) -> p i r n", r=3),
                                   xc[j][:, c].rearrange("p (i s) -> p i s", s=SLOT)[:, :, 0:NTOK].unsqueeze(2).to_broadcast([P, 4, 3, NTOK]))
                ins.then_inc(a["xr"], 1)

            def queries_keys(a, d, j):
                act.wait_ge(a["k_mm"], d + 1)
                act.copy(kc[j].rearrange("p c i n -> p (c i n)"), bank(j, 2)[:, 0:KEY_COLS0]).then_inc(a["k"], 1)
                act.copy(qp[j][:, :, :, 0:NTOK], bank(j, 1)[:, 0:KEY_COLS0].rearrange("p (c i n) -> p c i n", c=2, n=NTOK)).then_inc(a["q"], 1)

            def probs(a, d, j):
                act.wait_ge(a["sub"], d + 1)
                act.activation(sc[j], sc[j], ACT.Exp, scale=HD ** -0.5).then_inc(a["e"], 1)

            def turned_probs(a, d, j):
                act.wait_ge(a["pt_mm"], d + 1)
                for t in range(2):
                    ins = act.copy(pt[j][:, t].rearrange("p g n -> p (g n)"), bank(j, 1 + t)[0:TOKENS3, :])
                ins.then_inc(a["pt"], 1)

            def attention_front(d, j):
                three_copies(A1, d, j, A1["xt"])
                queries_keys(A1, d, j)

            def router_exp(d, j):
                act.wait_ge(A2["lgsub"], d + 1)
                act.activation(pr[j], lg[j], ACT.Exp).then_inc(A2["lgexp"], 1)

            def attention_step(d, j, more, most):
                if more:
                    attention_front(d + 1, 1 - j)
                probs(A1, d, j)
                if not more:
                    router_exp(0, 0)
                turned_probs(A1, d, j)
                columns_duo(2, d, j, A1["at_mm"], A1["at"], aot)
                if most:
                    columns_duo(0, d + 2, j, A1["xt_mm"], A1["xt"], xc)

            columns_duo(0, 0, 0, A1["xt_mm"], A1["xt"], xc)
            act.wait_ge(qp_set, 1)
            attention_front(0, 0)
            columns_duo(0, 1, 1, A1["xt_mm"], A1["xt"], xc)
            with act.Fori(0, DUOS // 2 - 1) as it:
                for j in range(2):
                    attention_step(2 * it + j, j, True, True)
            attention_step(DUOS - 2, 0, True, False)
            columns_duo(0, 0, 0, A2["xt_mm"], A2["xt"], xc)
            attention_step(DUOS - 1, 1, False, False)

            def ffn_columns(d, j):
                columns_duo(0, d, j, A2["yt_mm"], A2["yt"], xc)
                three_copies(A2, d, j, A2["yt"])

            def ffn_step(d, j, more):
                queries_keys(A2, d, j)
                if more:
                    columns_duo(0, d + 1, 1 - j, A2["xt_mm"], A2["xt"], xc)
                probs(A2, d, j)
                turned_probs(A2, d, j)
                if more:
                    router_exp(d + 1, 1 - j)
                act.wait_ge(A2["mlp_mm"], 2 * d + 2)
                for b in range(2):
                    for i in range(3):
                        ins = act.activation(hid[j][:, 3 * b + i, :, 0:NTOK],
                                             bank(j, 3 * b)[:, TOKENS4 * i:TOKENS4 * i + TOKENS4].rearrange("p (i n) -> p i n", n=NTOK), ACT.Gelu)
                ins.then_inc(A2["gelu"], 1)
                columns_duo(2, d, j, A2["at_mm"], A2["at"], xc)
                if more:
                    ffn_columns(d + 1, 1 - j)

            ffn_columns(0, 0)
            with act.Fori(0, DUOS // 2 - 1) as it:
                for j in range(2):
                    ffn_step(2 * it + j, j, True)
            ffn_step(DUOS - 2, 0, True)
            ffn_step(DUOS - 1, 1, False)

        @block.vector
        def _(dve):
            def duo_tiles(d):
                return (h[:, bass.ds(2 * d, 2), :],
                        [h[:, bass.ds(2 * d + t, 1), :].rearrange("p o d -> p (o d)") for t in range(2)])

            def variances(src, eps, done, s6, s2, v):
                for t in range(2):
                    dve.bn_stats(s6[:, t, :], src[t])
                dve.drain()
                for t in range(2):
                    dve.bn_aggr(s2[:, t, :], s6[:, t, :])
                dve.drain()
                dve.tensor_scalar_add(v, s2[:, :, 1], eps).then_inc(done, 1)

            def less_mean_over_deviation(dst, src, mean, root, done):
                for t in range(2):
                    ins = dve.tensor_scalar(dst[:, t, 0:D], src[t], mean[:, t, 0:1], root[:, t:t + 1], ALU.subtract, ALU.mult)
                ins.then_inc(done, 1)

            def low(e, u, n):
                dve.wait_ge(high_set, n)
                if u < 4:
                    rows = slice(64 * (u % 2), P)
                    hi = w13[2 * (u % 2)][rows, bass.ds(e, 1), u // 2, :].rearrange("p o f -> p (o f)")
                    lo = w13[1 + u % 2][rows, bass.ds(e, 1), u // 2, :].rearrange("p o f -> p (o f)")
                    src = stage[u % 3][rows]
                else:
                    rows = slice(3 * (u - 4), 3 * (u - 4) + 3)
                    hi = w2r[0][:, bass.ds(e, 1), rows, :].rearrange("p o c d -> p (o c) d")
                    lo = w2r[1][:, bass.ds(e, 1), rows, :].rearrange("p o c d -> p (o c) d")
                    src = stage[u % 3][:, 0:3 * D].rearrange("p (c d) -> p c d", c=3)
                dve.scalar_tensor_tensor(lo, src, WSCALE, hi, ALU.mult, ALU.subtract).then_inc(stage_free, 1)

            def units(e, a, b):
                for u in range(a, b):
                    low(e, u, 6 * e + u + 1)

            def tokens(d, j):
                dve.wait_ge(tok_mm, 2 * d + 2)
                ht, h1 = duo_tiles(d)
                dve.tensor_tensor(ht, bank(j, 0)[:, 0:2 * D].rearrange("p (t d) -> p t d", t=2),
                                  pos_bias.unsqueeze(1).to_broadcast([P, 2, D]), ALU.add)
                dve.drain()
                variances(h1, LN_EPS, ve1, st[j], mv[j], ve[j])

            def token_rows(d, j, behind):
                if behind:
                    dve.drain()
                    dve.wait_ge(A0["xt_mm"], d - 1)
                dve.wait_ge(rs1, d + 1)
                less_mean_over_deviation(xn[j], duo_tiles(d)[1], mv[j], rs[j], xn1)

            def keys_queries(d, j):
                dve.wait_ge(kv_mm, d + 1)
                dve.tensor_scalar(kpos[j].rearrange("p t d -> p (t d)"), bank(j, 2)[:, 0:2 * D], 0.0, HD ** -0.5, ALU.max, ALU.add).then_inc(kset, 1)
                dve.wait_ge(q_mm, d + 1)
                dve.tensor_scalar(qt[j].rearrange("p c n -> p (c n)"), bank(j, 0), 0.0, HD ** -0.5, ALU.max, ALU.add).then_inc(qset, 1)

            def masked_sums(d, j):
                dve.wait_ge(kvi_mm, d + 1)
                for im in range(2):
                    ins = dve.tensor_tensor(kvm[j][:, 2 * im:2 * im + 2, :], bank(j, 2 + im)[:, 0:2 * V_COLS].rearrange("p (i n) -> p i n", i=2),
                                            mask17.unsqueeze(1).to_broadcast([P, 2, V_COLS]), ALU.mult)
                ins.then_inc(kvm_set, 1)

            def over_keys(d, j):
                dve.wait_ge(o_mm, d + 1)
                o4 = bank(j, 1)[:, 0:2 * V_COLS].rearrange("p (t h e) -> p t h e", t=2, h=NH)
                dve.tensor_scalar_add(den[j], o4[:, :, :, 16], 1e-6).then_inc(den_e, 1)
                dve.wait_ge(den_e, d + 1)
                dve.reciprocal(den[j], den[j]).then_inc(den_set, 1)
                dve.wait_ge(den_set, d + 1)
                for t in range(2):
                    ins = dve.tensor_tensor(ao[j][:, t, 0:D].rearrange("p (h e) -> p h e", h=NH), o4[:, t, :, 0:16],
                                            den[j][:, t].unsqueeze(2).to_broadcast([P, NH, HD]), ALU.mult)
                ins.then_inc(ao_set, 1)

            def add_attention(d, j):
                dve.wait_ge(pr_mm, d + 1)
                ht, h1 = duo_tiles(d)
                dve.tensor_tensor(ht, ht, bank(j, 2)[:, 0:2 * D].rearrange("p (t d) -> p t d", t=2), ALU.add)
                dve.drain()
                variances(h1, LN_EPS, A0["ve"], st2[j], mv2[j], ve2[j])

            def gate_rows(d, j):
                dve.wait_ge(A0["rs"], d + 1)
                less_mean_over_deviation(xn[j], duo_tiles(d)[1], mv2[j], rs2[j], A0["xn"])

            def rows_low(d, j):
                dve.wait_ge(rows_hi, d + 1)
                dve.scalar_tensor_tensor(rows16[:, bass.ds(2 * d, 2), D:2 * D], xn[j][:, :, 0:D], XSCALE,
                                         rows16[:, bass.ds(2 * d, 2), 0:D], ALU.mult, ALU.subtract).then_inc(rows_set, 1)

            def logits(d, j):
                dve.wait_ge(A0["lg_mm"], d + 1)
                dve.tensor_copy(glog[:, bass.ds(2 * d, 2), :], bank(j, 2)[:, 0:16].rearrange("p (t e) -> p t e", t=2)).then_inc(A0["lg"], 1)

            def embed_step(d, j, last):
                add_attention(d - 1, 1 - j)
                gate_rows(d - 1, 1 - j)
                units(d, 0, 1)
                if not last:
                    tokens(d + 1, 1 - j)
                masked_sums(d, j)
                rows_low(d - 1, 1 - j)
                if not last:
                    token_rows(d + 1, 1 - j, True)
                logits(d - 1, 1 - j)
                over_keys(d, j)
                units(d, 1, 4 if last else 6)
                if not last:
                    keys_queries(d + 1, 1 - j)

            dve.wait_ge(tok_in, 16 * len(embedding))
            dve.wait_ge(posb_mm, 1)
            dve.tensor_tensor(pos_bias, pos_bias, bank(1, 0)[:, 0:D], ALU.add).then_inc(posb_set, 1)
            dve.memset(sel[:, TILES, :], 0.0)
            dve.wait_ge(posb_set, 1)
            dve.wait_ge(consts_set, 1)
            tokens(0, 0)
            token_rows(0, 0, False)
            dve.wait_ge(w_in, 16 * len(first))
            keys_queries(0, 0)
            units(0, 0, 2)
            tokens(1, 1)
            masked_sums(0, 0)
            token_rows(1, 1, False)
            over_keys(0, 0)
            units(0, 2, 4)
            keys_queries(1, 1)
            units(0, 4, 6)
            with dve.Fori(0, DUOS // 2 - 1) as it:
                for i in range(2):
                    embed_step(2 * it + 1 + i, 1 - i, False)
            embed_step(DUOS - 1, 1, True)
            add_attention(DUOS - 1, 1)
            units(DUOS - 1, 4, 6)
            gate_rows(DUOS - 1, 1)
            rows_low(DUOS - 1, 1)
            logits(DUOS - 1, 1)

            dve.drain()
            dve.tensor_scalar(positive, glog, 0.0, None, ALU.max)
            dve.drain()
            dve.wait_ge(A0["ln"], 1)
            dve.tensor_tensor(softplus, positive, log_exp[2], ALU.add).then_inc(A0["sp"], 1)
            for e in range(EXPERTS):
                ins = dve.memset(ahead[:, :, e, e:e + 1], 0.0)
            dve.wait_ge(A0["sq"], 1)
            dve.tensor_tensor(score, root_score, gbias.unsqueeze(1).to_broadcast([P, TILES, 8]), ALU.add)
            dve.drain()
            for e in range(EXPERTS):
                if e > 0:
                    dve.tensor_tensor(ahead[:, :, e, 0:e], score[:, :, 0:e], score[:, :, e:e + 1].to_broadcast([P, TILES, e]), ALU.is_ge)
                if e < EXPERTS - 1:
                    dve.tensor_tensor(ahead[:, :, e, e + 1:], score[:, :, e + 1:], score[:, :, e:e + 1].to_broadcast([P, TILES, EXPERTS - 1 - e]), ALU.is_gt)
            dve.drain()
            dve.tensor_reduce(place_of, ahead, AX.X, ALU.add)
            dve.drain()
            for k in range(TOPK):
                dve.tensor_scalar(choice[k], place_of, float(k), route[:, 0:1], ALU.is_equal, ALU.mult)
            dve.drain()
            dve.tensor_tensor(sel[:, 0:TILES, :], choice[0], choice[1], ALU.add).then_inc(sel_set, 1)

            lists = 1 + TOPK * TILES
            spare = route[:, 1:lists].rearrange("p (k t) -> p k t", k=TOPK)
            whole = route[:, lists:lists + SHARED_TILES]
            numbers = route[:, lists + SHARED_TILES:]

            def hidden(k, par):
                for g in range(2):
                    dve.wait_ge(M["up_mm"], 2 * k + g + 1)
                    dve.tensor_scalar(upc[g], banks[:, 3 + g, 0:3 * P], LIMIT * XSCALE * WSCALE, -LIMIT * XSCALE * WSCALE, ALU.min, ALU.max).then_inc(M["clip"], 1)
                    dve.wait_ge(M["clip"], 2 * k + g + 1)
                    dve.wait_ge(M["silu"], 2 * k + g + 1)
                    dve.scalar_tensor_tensor(h32[g], sil[g], SILU_LIMIT, upc[g], ALU.min, ALU.mult).then_inc(M["h"], 1)
                for g in range(2):
                    dve.wait_ge(M["hi"], 2 * k + g + 1)
                    dve.tensor_tensor(eh[par][:, 1, 3 * g:3 * g + 3, :].rearrange("p f n -> p (f n)"), h32[g],
                                      eh[par][:, 0, 3 * g:3 * g + 3, :].rearrange("p f n -> p (f n)"), ALU.subtract).then_inc(M["lo"], 1)

            hidden(0, 0)
            dve.wait_ge(r_in, 16 * len(second))
            dve.wait_ge(count_mm, 1)
            places = banks[:, 7][:, 0:8 * (TILES + 1)].rearrange("p (t e) -> p t e", e=8)
            dve.tensor_copy(cnt[:, 0], places[:, TILES, :])
            dve.drain()
            full = cmpt[:, 0:EXPERTS * SHARED_TILES].rearrange("p (e q) -> p e q", e=8)
            dve.tensor_tensor(full, cnt[:, 0].unsqueeze(2).to_broadcast([P, 8, SHARED_TILES]), whole.unsqueeze(1).to_broadcast([P, 8, SHARED_TILES]), ALU.is_gt)
            dve.drain()
            dve.tensor_reduce(cnt[:, 1], full, AX.X, ALU.add)
            dve.drain()
            before = cmpt[:, 0:EXPERTS ** 2].rearrange("p (a b) -> p a b", a=8)
            dve.tensor_tensor(before, cnt[:, 1].unsqueeze(1).to_broadcast([P, 8, 8]), tri8, ALU.mult)
            dve.drain()
            dve.tensor_reduce(cnt[:, 2], before, AX.X, ALU.add)
            dve.drain()
            dve.tensor_tensor(cnt[:, 3], cnt[:, 2], cnt[:, 1], ALU.add)
            dve.tensor_scalar(cnt[:, 0], cnt[:, 2], float(P), float(SHARED_TILES * P), ALU.mult, ALU.add)
            dve.drain()
            ended = cmpt.rearrange("p (n e) -> p n e", e=8)
            dve.tensor_tensor(ended, cnt[:, 3].unsqueeze(1).to_broadcast([P, ROUTED_TILES, 8]), numbers.unsqueeze(2).to_broadcast([P, ROUTED_TILES, 8]), ALU.is_le)
            dve.drain()
            dve.tensor_reduce(eidf, ended, AX.X, ALU.add)
            dve.drain()
            dve.tensor_scalar(tile_e[:, SHARED_TILES:MTILES], eidf[0:1], float(EXPERTS - 1), 1.0, ALU.min, ALU.add)
            dve.drain()
            digits = tile_e[:, SHARED_TILES - 2:].rearrange("p (n g) -> p n g", g=GROUP)
            words = cmpt[0:1, 0:WORDS]
            dve.scalar_tensor_tensor(words, digits[:, 1:WORDS + 1, 0], float(ALL), digits[:, 0:WORDS, GROUP - 1], ALU.mult, ALU.add)
            dve.drain()
            for n in range(GROUP - 2, -1, -1):
                place = words if n else tile_experts
                dve.scalar_tensor_tensor(place, words, float(ALL), digits[:, 0:WORDS, n], ALU.mult, ALU.add)
                dve.drain()
            dve.tensor_tensor(rows_of, places[:, 0:TILES, :], cnt[:, 0].unsqueeze(1).to_broadcast([P, TILES, 8]), ALU.add)
            dve.drain()
            for k in range(TOPK):
                dve.tensor_tensor(product, choice[k], rows_of, ALU.mult)
                dve.drain()
                dve.tensor_reduce(slotf[:, k], product, AX.X, ALU.add)
                dve.drain()
            dve.tensor_copy(gather_at, slotf)
            dve.tensor_tensor(scatter_at, slotf, spare, ALU.add).then_inc(routed, 1)
            hidden(1, 1)
            units(EXPERTS, 0, 3)
            hidden(2, 0)
            units(EXPERTS, 3, 6)
            hidden(3, 1)
            for k in range(TOPK):
                dve.tensor_tensor(product, choice[k], root_score, ALU.mult)
                dve.drain()
                dve.tensor_reduce(wk[:, k], product, AX.X, ALU.add)
                dve.drain()
            dve.tensor_tensor(gsum, wk[:, 0], wk[:, 1], ALU.add)
            dve.drain()
            dve.tensor_scalar(gsum, gsum, 1e-6, None, ALU.max)
            dve.drain()
            dve.reciprocal(gsum, gsum)
            dve.drain()
            dve.tensor_tensor(wk, wk, gsum.unsqueeze(1).to_broadcast([P, TOPK, TILES]), ALU.mult)
            with dve.Fori(2, MTILES // 2) as it:
                for par in range(2):
                    hidden(2 * it + par, par)
            dve.wait_ge(shared_in, 32)
            dve.tensor_tensor(h, h, shared_y, ALU.add)
            dve.drain()

            def add_experts(d, j):
                dve.wait_ge(gathered[j], 32 * (d - j) + 64)
                for k in range(TOPK):
                    for i in range(2):
                        row = h[:, bass.ds(2 * d + i, 1), :].rearrange("p o d -> p (o d)")
                        dve.scalar_tensor_tensor(row, got[:, k, bass.ds(2 * d + i, 1), :].rearrange("p o d -> p (o d)"),
                                                 wk[:, k, bass.ds(2 * d + i, 1)], row, ALU.mult, ALU.add)
                    dve.drain()

            def normalised_duo(a, d, j):
                variances(duo_tiles(d)[1], LN_EPS, a["ve"], st[j], mv[j], ve[j])
                over_deviation(a, d, j)

            def over_deviation(a, d, j):
                dve.wait_ge(a["rs"], d + 1)
                less_mean_over_deviation(xn[j], duo_tiles(d)[1], mv[j], rs[j], a["xn"])

            def masked_values(a, d, j):
                dve.wait_ge(a["v_mm"], d + 1)
                for im in range(2):
                    ins = dve.tensor_tensor(vx[j][:, 2 * im:2 * im + 2, :].rearrange("p t (g e) -> p (t g) e", g=4),
                                            bank(j, 3 - 3 * im)[0:TOKENS3, 0:2 * V_COLS].rearrange("p (g e) -> p g e", e=V_COLS3),
                                            m_v.unsqueeze(1).to_broadcast([TOKENS3, 8, V_COLS3]), ALU.mult)
                ins.then_inc(a["vx"], 1)

            def less_maximum(a, d, j, masked):
                dve.wait_ge(a["s_mm"], d + 1)
                s2 = banks[:, 4 * j + 1:4 * j + 3, 0:KEY_COLS].rearrange("p t (h n) -> p t h n", h=12)
                if masked:
                    for t in range(2):
                        dve.tensor_tensor(sc[j][:, t], s2[:, t], m_causal.unsqueeze(1).to_broadcast([P, 12, NTOK]), ALU.add)
                    dve.drain()
                    s2 = sc[j]
                dve.tensor_reduce(mx[j], s2, AX.X, ALU.max).then_inc(a["mx"], 1)
                dve.wait_ge(a["mx"], d + 1)
                for t in range(2):
                    ins = dve.tensor_tensor(sc[j][:, t], s2[:, t], mx[j][:, t].unsqueeze(2).to_broadcast([P, 12, NTOK]), ALU.subtract)
                ins.then_inc(a["sub"], 1)

            def over_sum(a, d, j):
                dve.wait_ge(a["o_mm"], d + 1)
                o4 = bank(j, 1)[:, 0:2 * V_COLS].rearrange("p (t h e) -> p t h e", t=2, h=NH)
                dve.reciprocal(den[j], o4[:, :, :, 16]).then_inc(a["rden"], 1)
                dve.wait_ge(a["rden"], d + 1)
                for t in range(2):
                    ins = dve.tensor_tensor(ao[j][:, t, 0:D].rearrange("p (h e) -> p h e", h=NH), o4[:, t, :, 0:16],
                                            den[j][:, t].unsqueeze(2).to_broadcast([P, NH, HD]), ALU.mult)
                ins.then_inc(a["ao"], 1)

            def inner_variances(d, j):
                dve.wait_ge(A2["xn"], d + 1)
                variances([xn[j][:, t, 0:D] for t in range(2)], EPS2, A2["ve2"], st[j], mv[j], ve[j])
                ht = duo_tiles(d)[0]
                dve.tensor_tensor(ht, ht, xn[j][:, :, 0:D], ALU.add)

            def router_max(d, j):
                dve.wait_ge(A2["lg_mm"], d + 1)
                l2 = bank(j, 1)[:, 0:8].rearrange("p (t e) -> p t e", t=2)
                dve.tensor_reduce(l1s[j], l2, AX.X, ALU.max).then_inc(A2["lgmx"], 1)
                dve.wait_ge(A2["lgmx"], d + 1)
                dve.tensor_tensor(lg[j], l2, l1s[j].unsqueeze(2).to_broadcast([P, 2, 4]), ALU.subtract).then_inc(A2["lgsub"], 1)

            def router_probs(d, j):
                dve.wait_ge(A2["lgexp"], d + 1)
                dve.tensor_reduce(l1s[j], pr[j], AX.X, ALU.add).then_inc(A2["lgsum"], 1)
                dve.wait_ge(A2["lgsum"], d + 1)
                dve.reciprocal(l1s[j], l1s[j]).then_inc(A2["lgrec"], 1)
                dve.wait_ge(A2["lgrec"], d + 1)
                dve.tensor_tensor(pr[j], pr[j], l1s[j].unsqueeze(2).to_broadcast([P, 2, 4]), ALU.mult).then_inc(A2["p"], 1)
                dve.wait_ge(A2["p"], d + 1)
                dve.tensor_tensor(dg[j].rearrange("p t e n -> p (t e) n"), eye37.unsqueeze(1).to_broadcast([P, 8, NTOK]),
                                  pr[j].rearrange("p t e -> p (t e)").unsqueeze(2).to_broadcast([P, 8, NTOK]), ALU.mult).then_inc(A2["dg"], 1)

            def ranks(d, j):
                dve.wait_ge(A2["bc_mm"], d + 1)
                others = bank(j, 2)[:, 0:KEY_COLS0].rearrange("p (e n) -> p e n", n=NTOK)
                own = pr[j].rearrange("p t e -> p (t e)").unsqueeze(2).to_broadcast([P, 8, NTOK])
                g3 = gt[j].rearrange("p t e n -> p (t e) n")
                e3 = eq[j].rearrange("p t e n -> p (t e) n")
                dve.tensor_tensor(g3, others, own, ALU.is_gt)
                dve.tensor_tensor(e3, others, own, ALU.is_equal).then_inc(A2["cmp"], 1)
                dve.wait_ge(A2["cmp"], d + 1)
                dve.tensor_tensor(e3, e3, tri.unsqueeze(1).to_broadcast([P, 8, NTOK]), ALU.mult)
                dve.drain()
                dve.tensor_tensor(g3, g3, e3, ALU.add).then_inc(A2["cmp2"], 1)
                dve.wait_ge(A2["cmp2"], d + 1)
                dve.tensor_reduce(rank[j].rearrange("p t e -> p (t e)"), g3, AX.X, ALU.add).then_inc(A2["rank"], 1)

            def scaled_rows(d, j):
                dve.wait_ge(A2["rank"], d + 1)
                dve.tensor_scalar(sg[j][:, 0], rank[j], CAP - 0.5, None, ALU.is_lt)
                dve.drain()
                dve.tensor_tensor(sg[j][:, 1], sg[j][:, 0], pr[j], ALU.mult)
                dve.drain()
                for e in (2, 1, 0):
                    dve.tensor_tensor(sg[j][:, :, :, e], sg[j][:, :, :, e], sg[j][:, :, :, e + 1], ALU.add)
                    dve.drain()
                dve.wait_ge(A2["rs2"], d + 1)
                dve.tensor_tensor(rsr[j], sg[j][:, 0], rs[j].unsqueeze(2).to_broadcast([P, 2, 4]), ALU.mult).then_inc(A2["rsr"], 1)
                dve.wait_ge(A2["rsr"], d + 1)
                for t in range(2):
                    for r, (a0, a1) in enumerate(RNG):
                        dve.tensor_scalar(yn[j][:, t, a0:a1], xn[j][:, t, a0:a1], mv[j][:, t, 0:1], rsr[j][:, t, r:r + 1], ALU.subtract, ALU.mult)
                dve.tensor_copy(yn[j][:, :, 192:196], sg[j][:, 0]).then_inc(A2["yn"], 1)

            def add_output(d, j):
                dve.wait_ge(A1["pr_mm"], d + 1)
                ht = duo_tiles(d)[0]
                dve.tensor_tensor(ht, ht, bank(j, 3)[:, 0:2 * D].rearrange("p (t d) -> p t d", t=2), ALU.add).then_inc(A1["h"], 1)

            def attention_step(d, j):
                less_maximum(A1, d, j, True)
                add_experts(d + 2, j)
                normalised_duo(A1, d + 2, j)
                masked_values(A1, d + 1, 1 - j)
                over_sum(A1, d, j)
                add_output(d, j)

            dve.wait_ge(c1_in, 16 * len(third))
            add_experts(0, 0)
            normalised_duo(A1, 0, 0)
            add_experts(1, 1)
            normalised_duo(A1, 1, 1)
            masked_values(A1, 0, 0)
            dve.wait_ge(bw_mm, 1)
            for n0 in range(3):
                f = slice(third_cols * n0, third_cols * n0 + third_cols)
                ins = dve.tensor_tensor(w_f1[64:68, 1, f], w_f1[64:68, 1, f], banks[64:68, 5 + n0, 0:third_cols], ALU.add)
            ins.then_inc(bw_added, 1)
            with dve.Fori(0, DUOS // 2 - 1) as it:
                for j in range(2):
                    attention_step(2 * it + j, j)
            less_maximum(A1, DUOS - 2, 0, True)
            normalised_duo(A2, 0, 0)
            dve.tensor_scalar(w_f1[:, 0, :], w_f1[:, 0, :], gb[:, 0, 0:1], None, ALU.mult)
            masked_values(A1, DUOS - 1, 1)
            over_sum(A1, DUOS - 2, 0)
            add_output(DUOS - 2, 0)
            less_maximum(A1, DUOS - 1, 1, True)
            inner_variances(0, 0)
            router_max(0, 0)
            router_probs(0, 0)
            dve.tensor_scalar(w_f1[0:64, 1, :], w_f1[0:64, 1, :], gb[0:64, 1, 0:1], None, ALU.mult).then_inc(bw_set, 1)
            ranks(0, 0)
            over_sum(A1, DUOS - 1, 1)
            scaled_rows(0, 0)
            add_output(DUOS - 1, 1)
            dve.drain()

            def head_keys(d, j):
                dve.wait_ge(A2["k"], d + 1)
                for h0, nh, c in ((0, 8, 0), (8, 4, 1)):
                    for im in (2, 3):
                        ins = dve.tensor_tensor(kx[j][:, im, NTOK * h0:NTOK * (h0 + nh)].rearrange("p (h n) -> p h n", h=nh),
                                                kc[j][:, c, im].unsqueeze(1).to_broadcast([P, nh, NTOK]),
                                                m_k[:, h0:h0 + nh].unsqueeze(2).to_broadcast([P, nh, NTOK]), ALU.mult)
                ins.then_inc(A2["kx2"], 1)

            def ffn_step(d, j, more, most):
                head_keys(d, j)
                masked_values(A2, d, j)
                less_maximum(A2, d, j, False)
                if more:
                    router_max(d + 1, 1 - j)
                    router_probs(d + 1, 1 - j)
                over_sum(A2, d, j)
                if more:
                    ranks(d + 1, 1 - j)
                    scaled_rows(d + 1, 1 - j)
                if most:
                    normalised_duo(A2, d + 2, j)
                    inner_variances(d + 2, j)
                dve.wait_ge(A2["fc_mm"], d + 1)
                for r, (a0, a1) in enumerate(RNG):
                    dve.tensor_tensor(zz[j][:, :, a0:a1], banks[:, 4 * j:4 * j + 4:3, a0:a1],
                                      sg[j][:, 1, :, r:r + 1].to_broadcast([P, 2, a1 - a0]), ALU.mult)
                dve.drain()
                ht = duo_tiles(d)[0]
                dve.tensor_tensor(ht, ht, zz[j], ALU.add).then_inc(A2["h"], 1)

            normalised_duo(A2, 1, 1)
            inner_variances(1, 1)
            with dve.Fori(0, DUOS // 2 - 1) as it:
                for j in range(2):
                    ffn_step(2 * it + j, j, True, True)
            ffn_step(DUOS - 2, 0, True, False)
            ffn_step(DUOS - 1, 1, False, False)


def two_chunks(w):
    a = np.zeros((256, w.shape[1]), w.dtype)
    a[:w.shape[0]] = w
    return np.ascontiguousarray(a.reshape(2, 128, -1).transpose(1, 0, 2))


def qkv17(w, rows, ones_row):
    a = two_chunks(w.T)
    for r, v in rows.items():
        a[r, 1] = v
    v17 = np.zeros((P, 2, NH, 17), w.dtype)
    v17[..., :16] = a[:, :, 2 * D:].reshape(P, 2, NH, HD)
    v17[ones_row, 1, :, 16] = 1
    return np.concatenate([a[:, :, :2 * D], v17.reshape(P, 2, -1)], 2)


def kernel(**inputs):
    import concourse.bacc as _bacc
    from concourse.bass_utils import run_bass_kernel_spmd as _run
    x = np.asarray(inputs["x"])
    g = {k: np.asarray(v) for k, v in inputs.items()}
    pt = x.reshape(NIMG, 6, 16, 6, 16, 3).transpose(0, 1, 3, 2, 4, 5).reshape(NIMG, 36, 6, 128)
    xp = np.zeros((NIMG, SLOT, 6, 128), x.dtype)
    xp[:, 1:37] = pt
    xp = np.ascontiguousarray(xp.reshape(TILES, P, 6, 128).transpose(0, 3, 2, 1))
    pos = np.zeros((2, SLOT, D), x.dtype)
    pos[:, :NTOK] = g["L0_tok_pos_embedding"]
    oh = np.zeros((2, 2, SLOT), np.float32)
    oh[0, :, 0] = 1
    oh[1, :, 1:NTOK] = 1
    addrows = np.stack([g["L0_tok_cls_token"].reshape(D), g["L0_tok_b_proj"]])
    m17 = np.zeros((P, NH, 17), np.float32)
    for e in range(P):
        m17[e, :8][np.arange(8) == e // 16] = 1
        if e >= 64:
            m17[e, 8:][np.arange(8, 12) == (e + 64) // 16] = 1
    def experts(name):
        return np.concatenate([g[f"L0_ffn_{name}s"][None], g[f"L0_ffn_{name}"]])

    def halves(name):
        w = experts(name)
        return np.stack([w[:, :P], np.concatenate([w[:, P:], w[:, P:]], 1)], 1)

    valid = (np.arange(P) % SLOT < NTOK)
    row = np.arange(TILES)[None] * P + np.arange(P)[:, None]
    spare = np.stack([SPARE_ROWS + k * TILES * P + row for k in range(TOPK)], 1) * ~valid[:, None, None]
    route = np.concatenate([valid[:, None], spare.reshape(P, -1), np.tile(np.arange(SHARED_TILES) * P, (P, 1)), np.tile(np.arange(ROUTED_TILES), (P, 1))], 1).astype(np.float32)

    i, jj = np.arange(NTOK)[:, None], np.arange(NTOK)[None, :]
    mask = np.where(((jj % 8 == 0) & (jj <= i)) | (jj == i) | (jj == i - 1), 0, -1e30).astype(np.float32)
    pad = np.zeros((SLOT - NTOK, NTOK), np.float32)
    kmask = m17[:, :, 0]
    vmask = np.zeros((3, NTOK, 3, 17), np.float32)
    for k in range(3):
        vmask[k, :, k] = 1
    rng = np.zeros((D, 4), np.float32)
    for k, (a0, a1) in enumerate(RNG):
        rng[a0:a1, k] = 1
    same = np.zeros((2, SLOT, 2, SLOT), np.float32)
    for k in range(2):
        same[k, :, k] = 1
    same = same.reshape(P, P)
    ffn_w1 = np.concatenate([two_chunks(g["L1_ffn_w1"][:MLP].T), qkv17(g["L1_ffn_w1"][MLP:], {64: g["L1_ffn_b1"][MLP:]}, 68)], 2)
    ffn_w1[64, 1, :MLP] = g["L1_ffn_b1"][:MLP]
    w2 = np.zeros((1024, 2 * D), np.float32)
    w2[:960] = g["L1_ffn_w2"].T
    w2[960] = g["L1_ffn_b2"]
    arrays = {
        "x_patches": xp, "tok_w": g["L0_tok_W_proj"].reshape(6, 128, D).transpose(1, 0, 2), "tok_pos": pos.reshape(P, D),
        "tok_onehot": oh.reshape(2, P), "tok_addrows": addrows, "l0_qkv": two_chunks(g["L0_attn_qkv_w"].T),
        "l0_proj": two_chunks(np.concatenate([g["L0_attn_proj_w"].T, g["L0_attn_proj_b"][None]])),
        "l1_w": qkv17(g["L1_attn_qkv_w"], {64: g["L1_attn_qkv_b"]}, 64),
        "l1_out": two_chunks(np.concatenate([g["L1_attn_out_w"].T, g["L1_attn_out_b"][None]])),
        "l1_mask": np.concatenate([mask, pad] * 2), "kmask": kmask, "vmask": vmask.reshape(3 * NTOK, V_COLS3),
        "ffn_w1": ffn_w1, "ffn_w2": w2.reshape(8, P, 2, D).transpose(1, 0, 2, 3), "ffn_router": two_chunks(g["L1_ffn_w_router"].T),
        "ffn_gb": two_chunks(np.stack([g["L1_ffn_gamma1"], g["L1_ffn_beta1"]], 1)), "ffn_ranges": two_chunks(rng),
        "slot_eye": np.concatenate([np.eye(NTOK, dtype=np.float32), pad] * 2), "same_image": same,
        "earlier": np.concatenate([np.tril(np.ones((NTOK, NTOK), np.float32), -1), pad] * 2),
        "moe_13": np.stack([halves("w1"), halves("w3")], 1).reshape(ALL, 4, P, FFN), "gate_w": two_chunks(g["L0_ffn_gate_w"]),
        "moe_2": experts("w2").reshape(ALL, 2, 3, P, D).transpose(0, 1, 3, 2, 4).reshape(ALL, 2, P, 3 * D),
        "route_c": route, "lt_in": np.triu(np.ones((P, P), np.float32), 1), "ones_in": np.ones((P, P), np.float32),
        "gate_bias": np.tile(g["L0_ffn_gate_bias"], (P, 1)), "before8": np.tile(np.tril(np.ones((8, 8), np.float32), -1), (P, 1, 1)),
        "ident_in": np.eye(P, dtype=np.float32), "hmask17": m17.reshape(P, V_COLS),
    }
    arrays = {k: np.ascontiguousarray(v) for k, v in arrays.items()}
    nc = _bacc.Bacc("TRN2", target_bir_lowering=False, num_devices=1)
    args = {k: nc.dram_tensor(k + "_dram", v.shape, mybir.dt.from_np(v.dtype), kind="ExternalInput").ap() for k, v in arrays.items()}
    out = nc.dram_tensor("out_dram", (NIMG, NTOK, D), F32, kind="ExternalOutput").ap()
    vit(nc, out=out, **args)
    r = _run(nc, [{k + "_dram": v for k, v in arrays.items()}], core_ids=[0])
    return r.results[0]["out_dram"]
```
